# Optimizing a Trainium2 kernel written in Bass

```python
import numpy as np
import jax
import jax.numpy as jnp

def _softmax(x, axis=-1):
    return jax.nn.softmax(x, axis=axis)

def _gelu(x):
    return jax.nn.gelu(x, approximate=True)

def _silu(x):
    return jax.nn.silu(x)

def _sigmoid(x):
    return jax.nn.sigmoid(x)

def _layernorm(x, axis=-1, eps=1e-05):
    m = jnp.mean(x, axis=axis, keepdims=True)
    v = jnp.var(x, axis=axis, keepdims=True)
    return (x - m) / jnp.sqrt(v + eps)

def _scatter_add(tgt, idx, src, axis=0):
    return tgt.at[idx].add(src)

def _segment_sum(src, seg, n):
    return jax.ops.segment_sum(src, seg, n)
kernel_name = 'mk_decoder_preln_d2_seqx_r8_bf4083'

def setup_inputs(seed: int=0):
    np.random.seed(seed)
    _w = jnp.asarray

    def _rec_inputs():
        import jax
        import jax.numpy as jnp
        _rk = jax.random.key(seed)
        x = 0.5 + 0.2887 * jax.random.normal(jax.random.fold_in(_rk, 1), (4, 256, 256), jnp.float32)
        _lenS = 256 - jax.random.randint(jax.random.fold_in(_rk, 7), (4,), 0, max(1, 256 // 4) + 1, jnp.int32)
        _lenS2 = 256 - jax.random.randint(jax.random.fold_in(_rk, 8), (4,), 0, max(1, 256 // 4) + 1, jnp.int32)
        _ctx_512P = jax.random.normal(jax.random.fold_in(_rk, 11), (4, 16, 64), jnp.float32)
        _ctx_512c = jax.random.dirichlet(jax.random.fold_in(_rk, 511), 0.3 * jnp.ones((16,), jnp.float32), (4, 256))
        _ctx_512t = jnp.einsum('bsk,bkd->bsd', _ctx_512c, _ctx_512P)
        _ctx_512t = _ctx_512t * jax.lax.rsqrt(jnp.mean(jnp.square(_ctx_512t)) + 1e-12) * 0.953939
        ctx_512 = -0.000392918 + 0.999932 * (_ctx_512t + 0.3 * jax.random.normal(jax.random.fold_in(_rk, 611), (4, 256, 64), jnp.float32))
        return (x, ctx_512)
    x, ctx_512 = _rec_inputs()

    def _L0_attn_setup():
        import jax, jax.numpy as jnp
        import numpy as np
        import math
        E = 256
        H = 16
        D = E // H

        def _alibi_slopes(n):

            def pow2_slopes(n):
                start = 2 ** (-2 ** (-(math.log2(n) - 3)))
                return [start * start ** i for i in range(n)]
            if math.log2(n).is_integer():
                return pow2_slopes(n)
            c = 2 ** math.floor(math.log2(n))
            return pow2_slopes(c) + _alibi_slopes(2 * c)[::2][:n - c]

        def _alibi_bias(seq_len):
            slopes = jnp.asarray(_alibi_slopes(H), dtype=jnp.float32)
            pos = jnp.arange(seq_len)
            rel = jnp.abs(pos[None, :] - pos[:, None]).astype(jnp.float32)
            return -slopes[:, None, None] * rel[None, :, :]
        key = jax.random.key(seed)
        ks = jax.random.split(key, 5)
        B, S = (2, 256)
        scale = 1.0 / math.sqrt(E)
        x = jax.random.normal(ks[0], (B, S, E), dtype=jnp.float32)
        Wq = jax.random.normal(ks[1], (E, E), dtype=jnp.float32) * scale
        Wk = jax.random.normal(ks[2], (E, E), dtype=jnp.float32) * scale
        Wv = jax.random.normal(ks[3], (E, E), dtype=jnp.float32) * scale
        Wo = jax.random.normal(ks[4], (E, E), dtype=jnp.float32) * scale
        z = jnp.zeros((E,), dtype=jnp.float32)
        return {'x': x, 'Wq': Wq, 'bq': z, 'Wk': Wk, 'bk': z, 'Wv': Wv, 'bv': z, 'Wo': Wo, 'bo': z}
    _L0_attn_all = _L0_attn_setup()
    _L0_attn_in = {k: v for k, v in _L0_attn_all.items() if k in ('Wq', 'bq', 'Wk', 'bk', 'Wv', 'bv', 'Wo', 'bo')}
    del _L0_attn_all

    def _L0_xattn_setup():
        import jax, jax.numpy as jnp
        import numpy as np
        B, N, D = (16, 256, 64)
        H = 4
        TOP_K_RATIO = 0.3
        key = jax.random.key(seed)
        k1, k2, k3, k4 = jax.random.split(key, 4)
        h = jax.random.normal(k1, (B, N, D), dtype=jnp.float32)
        adj_raw = jax.random.uniform(k2, (B, N, N), dtype=jnp.float32)
        lim = 1.0 / np.sqrt(D)
        Wq = jax.random.uniform(k3, (D, D), minval=-lim, maxval=lim, dtype=jnp.float32)
        Wk = jax.random.uniform(k4, (D, D), minval=-lim, maxval=lim, dtype=jnp.float32)
        gamma_raw = jnp.float32(-0.85)
        return {'h': h, 'adj_raw': adj_raw, 'Wq': Wq, 'Wk': Wk, 'gamma_raw': gamma_raw}
    _L0_xattn_all = _L0_xattn_setup()
    _L0_xattn_in = {k: v for k, v in _L0_xattn_all.items() if k in ('Wq', 'Wk', 'gamma_raw')}
    del _L0_xattn_all

    def _L0_ffn_setup():
        import jax, jax.numpy as jnp
        import numpy as np
        E, H, I = (8, 256, 512)
        TOP_K = 1
        B, S = (1, 256)
        key = jax.random.key(seed)
        ks = jax.random.split(key, 7)
        std = 0.02
        return {'hidden_states': jax.random.normal(ks[0], (B, S, H), dtype=jnp.float32), 'router_w': jax.random.normal(ks[1], (E, H), dtype=jnp.float32) * std, 'gate_up_proj': jax.random.normal(ks[2], (E, H, 2 * I), dtype=jnp.float32) * std, 'down_proj': jax.random.normal(ks[3], (E, I, H), dtype=jnp.float32) * std, 'shared_gate_w': jax.random.normal(ks[4], (H, I), dtype=jnp.float32) * std, 'shared_up_w': jax.random.normal(ks[5], (H, I), dtype=jnp.float32) * std, 'shared_down_w': jax.random.normal(ks[6], (I, H), dtype=jnp.float32) * std}
    _L0_ffn_all = _L0_ffn_setup()
    _L0_ffn_in = {k: v for k, v in _L0_ffn_all.items() if k in ('router_w', 'gate_up_proj', 'down_proj', 'shared_gate_w', 'shared_up_w', 'shared_down_w')}
    del _L0_ffn_all

    def _L1_attn_setup():
        import jax, jax.numpy as jnp
        import numpy as np
        B, N, H = (2, 512, 256)
        NH, HD = (16, 128)
        BLK = 32
        EPS = 1e-06

        def _lightning_attn(x, slope_rate, w_qkv, w_gate, w_out, norm_w):
            b, n, _ = x.shape
            h, d = (NH, HD)
            nb = n // BLK
            qkv = jax.nn.silu(jnp.einsum('bnf,of->bno', x, w_qkv))
            qkv = qkv.reshape(b, n, h, 3 * d)
            q, k, v = jnp.split(qkv, 3, axis=-1)
            q = q.transpose(0, 2, 1, 3)
            k = k.transpose(0, 2, 1, 3)
            v = v.transpose(0, 2, 1, 3)
            s = slope_rate.astype(jnp.float32)
            arr = jnp.arange(1, BLK + 1, dtype=jnp.float32)
            q_decay = jnp.exp(-s * arr[:, None])
            k_decay = jnp.exp(-s * (BLK - arr)[:, None])
            idx = arr[:, None] - arr[None, :]
            diag_decay = jnp.where(idx >= 0, jnp.exp(-s * idx), 0.0)
            block_decay = jnp.exp(-s * BLK)
            qb = q.reshape(b, h, nb, BLK, d).transpose(2, 0, 1, 3, 4)
            kb = k.reshape(b, h, nb, BLK, d).transpose(2, 0, 1, 3, 4)
            vb = v.reshape(b, h, nb, BLK, d).transpose(2, 0, 1, 3, 4)

            def step(kv, blk):
                qi, ki, vi = blk
                o_inter = jnp.einsum('bhmd,bhde->bhme', qi * q_decay, kv)
                qk = jnp.einsum('bhmd,bhnd->bhmn', qi, ki) * diag_decay
                o_intra = jnp.einsum('bhmn,bhne->bhme', qk, vi)
                kv_new = block_decay * kv + jnp.einsum('bhmd,bhme->bhde', ki * k_decay, vi)
                return (kv_new, o_inter + o_intra)
            kv0 = jnp.zeros((b, h, d, d), dtype=jnp.float32)
            _, out = jax.lax.scan(step, kv0, (qb, kb, vb))
            out = out.transpose(1, 2, 0, 3, 4).reshape(b, h, n, d)
            out = out.transpose(0, 2, 1, 3).reshape(b, n, h * d)
            var = jnp.mean(out * out, axis=-1, keepdims=True)
            out = norm_w * (out * jax.lax.rsqrt(var + EPS))
            gate = jax.nn.sigmoid(jnp.einsum('bnf,of->bno', x, w_gate))
            return jnp.einsum('bno,fo->bnf', gate * out, w_out)
        key = jax.random.key(seed)
        ks = jax.random.split(key, 5)
        scale = 0.02
        x = jax.random.normal(ks[0], (B, N, H), dtype=jnp.float32)
        slopes = (1.0 / 2.0 ** (8.0 * np.arange(1, NH + 1) / NH)).astype(np.float32)
        slope_rate = jnp.asarray(slopes).reshape(NH, 1, 1)
        w_qkv = jax.random.normal(ks[1], (3 * NH * HD, H), dtype=jnp.float32) * scale
        w_gate = jax.random.normal(ks[2], (NH * HD, H), dtype=jnp.float32) * scale
        w_out = jax.random.normal(ks[3], (H, NH * HD), dtype=jnp.float32) * scale
        norm_w = jnp.ones((NH * HD,), dtype=jnp.float32)
        return {'hidden_states': x, 'slope_rate': slope_rate, 'w_qkv': w_qkv, 'w_gate': w_gate, 'w_out': w_out, 'norm_w': norm_w}
    _L1_attn_all = _L1_attn_setup()
    _L1_attn_in = {k: v for k, v in _L1_attn_all.items() if k in ('slope_rate', 'w_qkv', 'w_gate', 'w_out', 'norm_w')}
    del _L1_attn_all

    def _L1_xattn_setup():
        import jax, jax.numpy as jnp
        import numpy as np
        P_ASEM = 0.6
        key = jax.random.key(seed)
        k1, k2, k3 = jax.random.split(key, 3)
        B, N, D = (8, 256, 64)
        x = jax.random.normal(k1, (B, N, D), dtype=jnp.float32)
        adj = jax.random.uniform(k2, (B, N, N), dtype=jnp.float32)
        bound = 1.0 / np.sqrt(2 * D)
        W = jax.random.uniform(k3, (1, 2 * D), dtype=jnp.float32, minval=-bound, maxval=bound)
        b = jnp.zeros((1,), dtype=jnp.float32)
        return {'x': x, 'adj': adj, 'W': W, 'b': b}
    _L1_xattn_all = _L1_xattn_setup()
    _L1_xattn_in = {k: v for k, v in _L1_xattn_all.items() if k in ('W', 'b')}
    del _L1_xattn_all

    def _L1_ffn_setup():
        import jax, jax.numpy as jnp
        import numpy as np
        H = 256
        key = jax.random.key(seed)
        ks = jax.random.split(key, 10)
        s = 1.0 / np.sqrt(H)
        x = jax.random.normal(ks[0], (4, 256, H), dtype=jnp.float32)
        Wg = jax.random.uniform(ks[1], (2, H), jnp.float32, -s, s)
        W0a = jax.random.uniform(ks[2], (2 * H, H), jnp.float32, -s, s)
        b0a = jax.random.uniform(ks[3], (2 * H,), jnp.float32, -s, s)
        W0b = jax.random.uniform(ks[4], (H, 2 * H), jnp.float32, -s, s)
        b0b = jax.random.uniform(ks[5], (H,), jnp.float32, -s, s)
        W1a = jax.random.uniform(ks[6], (2 * H, H), jnp.float32, -s, s)
        b1a = jax.random.uniform(ks[7], (2 * H,), jnp.float32, -s, s)
        W1b = jax.random.uniform(ks[8], (H, 2 * H), jnp.float32, -s, s)
        b1b = jax.random.uniform(ks[9], (H,), jnp.float32, -s, s)
        return {'x': x, 'Wg': Wg, 'W0a': W0a, 'b0a': b0a, 'W0b': W0b, 'b0b': b0b, 'W1a': W1a, 'b1a': b1a, 'W1b': W1b, 'b1b': b1b}
    _L1_ffn_all = _L1_ffn_setup()
    _L1_ffn_in = {k: v for k, v in _L1_ffn_all.items() if k in ('Wg', 'W0a', 'b0a', 'W0b', 'b0b', 'W1a', 'b1a', 'W1b', 'b1b')}
    del _L1_ffn_all
    return {'x': x, 'ctx_512': ctx_512, 'L0_attn_Wq': _L0_attn_in['Wq'], 'L0_attn_bq': _L0_attn_in['bq'], 'L0_attn_Wk': _L0_attn_in['Wk'], 'L0_attn_bk': _L0_attn_in['bk'], 'L0_attn_Wv': _L0_attn_in['Wv'], 'L0_attn_bv': _L0_attn_in['bv'], 'L0_attn_Wo': _L0_attn_in['Wo'], 'L0_attn_bo': _L0_attn_in['bo'], 'L0_xattn_Wq': _L0_xattn_in['Wq'], 'L0_xattn_Wk': _L0_xattn_in['Wk'], 'L0_xattn_gamma_raw': _L0_xattn_in['gamma_raw'], 'L0_ffn_router_w': _L0_ffn_in['router_w'], 'L0_ffn_gate_up_proj': _L0_ffn_in['gate_up_proj'], 'L0_ffn_down_proj': _L0_ffn_in['down_proj'], 'L0_ffn_shared_gate_w': _L0_ffn_in['shared_gate_w'], 'L0_ffn_shared_up_w': _L0_ffn_in['shared_up_w'], 'L0_ffn_shared_down_w': _L0_ffn_in['shared_down_w'], 'L1_attn_slope_rate': _L1_attn_in['slope_rate'], 'L1_attn_w_qkv': _L1_attn_in['w_qkv'], 'L1_attn_w_gate': _L1_attn_in['w_gate'], 'L1_attn_w_out': _L1_attn_in['w_out'], 'L1_attn_norm_w': _L1_attn_in['norm_w'], 'L1_xattn_W': _L1_xattn_in['W'], 'L1_xattn_b': _L1_xattn_in['b'], 'L1_ffn_Wg': _L1_ffn_in['Wg'], 'L1_ffn_W0a': _L1_ffn_in['W0a'], 'L1_ffn_b0a': _L1_ffn_in['b0a'], 'L1_ffn_W0b': _L1_ffn_in['W0b'], 'L1_ffn_b0b': _L1_ffn_in['b0b'], 'L1_ffn_W1a': _L1_ffn_in['W1a'], 'L1_ffn_b1a': _L1_ffn_in['b1a'], 'L1_ffn_W1b': _L1_ffn_in['W1b'], 'L1_ffn_b1b': _L1_ffn_in['b1b']}

def reference(x, ctx_512, L0_attn_Wq, L0_attn_bq, L0_attn_Wk, L0_attn_bk, L0_attn_Wv, L0_attn_bv, L0_attn_Wo, L0_attn_bo, L0_xattn_Wq, L0_xattn_Wk, L0_xattn_gamma_raw, L0_ffn_router_w, L0_ffn_gate_up_proj, L0_ffn_down_proj, L0_ffn_shared_gate_w, L0_ffn_shared_up_w, L0_ffn_shared_down_w, L1_attn_slope_rate, L1_attn_w_qkv, L1_attn_w_gate, L1_attn_w_out, L1_attn_norm_w, L1_xattn_W, L1_xattn_b, L1_ffn_Wg, L1_ffn_W0a, L1_ffn_b0a, L1_ffn_W0b, L1_ffn_b0b, L1_ffn_W1a, L1_ffn_b1a, L1_ffn_W1b, L1_ffn_b1b):
    import jax
    import jax.numpy as jnp

    def _L0_attn_ref(x, Wq, bq, Wk, bk, Wv, bv, Wo, bo):
        import jax, jax.numpy as jnp
        import numpy as np
        import math
        E = 256
        H = 16
        D = E // H

        def _alibi_slopes(n):

            def pow2_slopes(n):
                start = 2 ** (-2 ** (-(math.log2(n) - 3)))
                return [start * start ** i for i in range(n)]
            if math.log2(n).is_integer():
                return pow2_slopes(n)
            c = 2 ** math.floor(math.log2(n))
            return pow2_slopes(c) + _alibi_slopes(2 * c)[::2][:n - c]

        def _alibi_bias(seq_len):
            slopes = jnp.asarray(_alibi_slopes(H), dtype=jnp.float32)
            pos = jnp.arange(seq_len)
            rel = jnp.abs(pos[None, :] - pos[:, None]).astype(jnp.float32)
            return -slopes[:, None, None] * rel[None, :, :]
        B, S, _ = x.shape

        def proj(W, b):
            return (x @ W.T + b).reshape(B, S, H, D).transpose(0, 2, 1, 3)
        q = proj(Wq, bq)
        k = proj(Wk, bk)
        v = proj(Wv, bv)
        scores = jnp.einsum('bhqd,bhkd->bhqk', q, k) / math.sqrt(D)
        causal = jnp.triu(jnp.ones((S, S), dtype=bool), k=1)
        scores = jnp.where(causal[None, None], -jnp.inf, scores)
        scores = scores + _alibi_bias(S)[None]
        probs = jax.nn.softmax(scores, axis=-1)
        out = jnp.einsum('bhqk,bhkd->bhqd', probs, v)
        out = out.transpose(0, 2, 1, 3).reshape(B, S, E)
        return out @ Wo.T + bo

    def _L0_xattn_ref(h, adj_raw, Wq, Wk, gamma_raw):
        import jax, jax.numpy as jnp
        import numpy as np
        B, N, D = (16, 256, 64)
        H = 4
        TOP_K_RATIO = 0.3
        b, n, dm = h.shape
        d = dm // H
        Q = (h @ Wq.T).reshape(b, n, H, d).transpose(0, 2, 1, 3)
        K = (h @ Wk.T).reshape(b, n, H, d).transpose(0, 2, 1, 3)
        sim = jnp.einsum('bhnd,bhmd->bnm', Q, K) / (jnp.sqrt(jnp.float32(d)) * H)
        k = max(1, int(n * TOP_K_RATIO))
        topk_vals = jax.lax.top_k(sim, k)[0]
        threshold = topk_vals[:, :, -1:]
        sparse_mask = (sim >= threshold).astype(sim.dtype)
        A_learned = jax.nn.sigmoid(sim) * sparse_mask
        A_learned = (A_learned + jnp.swapaxes(A_learned, -1, -2)) * 0.5
        gamma = jax.nn.sigmoid(gamma_raw)
        return (1.0 - gamma) * adj_raw + gamma * A_learned

    def _L0_ffn_ref(hidden_states, router_w, gate_up_proj, down_proj, shared_gate_w, shared_up_w, shared_down_w):
        import jax, jax.numpy as jnp
        import numpy as np
        E, H, I = (8, 256, 512)
        TOP_K = 1
        B, S = (1, 256)
        orig_shape = hidden_states.shape
        x = hidden_states.reshape(-1, H)
        T = x.shape[0]
        logits = x @ router_w.T
        top_vals, top_idx = jax.lax.top_k(logits, TOP_K)
        scores = jnp.full_like(logits, -jnp.inf)
        scores = scores.at[jnp.arange(T)[:, None], top_idx].set(top_vals)
        scores = jax.nn.sigmoid(scores.astype(jnp.float32)).astype(logits.dtype)
        xr = x[None, :, :] * scores.T[:, :, None]
        gate_up = jnp.einsum('eth,ehf->etf', xr, gate_up_proj)
        gate, up = jnp.split(gate_up, 2, axis=-1)
        routed = jnp.einsum('etf,efh->eth', up * jax.nn.silu(gate), down_proj)
        routed_sum = routed.sum(axis=0)
        shared = jax.nn.silu(x @ shared_gate_w) * (x @ shared_up_w) @ shared_down_w
        return (shared + routed_sum).reshape(orig_shape)

    def _L1_attn_ref(hidden_states, slope_rate, w_qkv, w_gate, w_out, norm_w):
        import jax, jax.numpy as jnp
        import numpy as np
        B, N, H = (2, 512, 256)
        NH, HD = (16, 128)
        BLK = 32
        EPS = 1e-06

        def _lightning_attn(x, slope_rate, w_qkv, w_gate, w_out, norm_w):
            b, n, _ = x.shape
            h, d = (NH, HD)
            nb = n // BLK
            qkv = jax.nn.silu(jnp.einsum('bnf,of->bno', x, w_qkv))
            qkv = qkv.reshape(b, n, h, 3 * d)
            q, k, v = jnp.split(qkv, 3, axis=-1)
            q = q.transpose(0, 2, 1, 3)
            k = k.transpose(0, 2, 1, 3)
            v = v.transpose(0, 2, 1, 3)
            s = slope_rate.astype(jnp.float32)
            arr = jnp.arange(1, BLK + 1, dtype=jnp.float32)
            q_decay = jnp.exp(-s * arr[:, None])
            k_decay = jnp.exp(-s * (BLK - arr)[:, None])
            idx = arr[:, None] - arr[None, :]
            diag_decay = jnp.where(idx >= 0, jnp.exp(-s * idx), 0.0)
            block_decay = jnp.exp(-s * BLK)
            qb = q.reshape(b, h, nb, BLK, d).transpose(2, 0, 1, 3, 4)
            kb = k.reshape(b, h, nb, BLK, d).transpose(2, 0, 1, 3, 4)
            vb = v.reshape(b, h, nb, BLK, d).transpose(2, 0, 1, 3, 4)

            def step(kv, blk):
                qi, ki, vi = blk
                o_inter = jnp.einsum('bhmd,bhde->bhme', qi * q_decay, kv)
                qk = jnp.einsum('bhmd,bhnd->bhmn', qi, ki) * diag_decay
                o_intra = jnp.einsum('bhmn,bhne->bhme', qk, vi)
                kv_new = block_decay * kv + jnp.einsum('bhmd,bhme->bhde', ki * k_decay, vi)
                return (kv_new, o_inter + o_intra)
            kv0 = jnp.zeros((b, h, d, d), dtype=jnp.float32)
            _, out = jax.lax.scan(step, kv0, (qb, kb, vb))
            out = out.transpose(1, 2, 0, 3, 4).reshape(b, h, n, d)
            out = out.transpose(0, 2, 1, 3).reshape(b, n, h * d)
            var = jnp.mean(out * out, axis=-1, keepdims=True)
            out = norm_w * (out * jax.lax.rsqrt(var + EPS))
            gate = jax.nn.sigmoid(jnp.einsum('bnf,of->bno', x, w_gate))
            return jnp.einsum('bno,fo->bnf', gate * out, w_out)
        return _lightning_attn(hidden_states, slope_rate, w_qkv, w_gate, w_out, norm_w)

    def _L1_xattn_ref(x, adj, W, b):
        import jax, jax.numpy as jnp
        import numpy as np
        P_ASEM = 0.6
        D = x.shape[-1]
        Wi = W[:, :D]
        Wj = W[:, D:]
        si = jnp.einsum('bnd,d->bn', x, Wi[0])
        sj = jnp.einsum('bnd,d->bn', x, Wj[0])
        xij = jax.nn.sigmoid(si[:, :, None] + sj[:, None, :] + b[0])
        return P_ASEM * xij + (1.0 - P_ASEM) * adj

    def _L1_ffn_ref(x, Wg, W0a, b0a, W0b, b0b, W1a, b1a, W1b, b1b):
        import jax, jax.numpy as jnp
        import numpy as np
        H = 256
        scores = jax.nn.softmax(jnp.einsum('bsh,eh->bse', x, Wg), axis=-1)
        top_expert = jnp.argmax(scores, axis=-1)
        h0 = jax.nn.gelu(jnp.einsum('bsh,fh->bsf', x, W0a) + b0a, approximate=False)
        out0 = jnp.einsum('bsf,hf->bsh', h0, W0b) + b0b
        h1 = jax.nn.relu(jnp.einsum('bsh,fh->bsf', x, W1a) + b1a)
        out1 = jnp.einsum('bsf,hf->bsh', h1, W1b) + b1b
        mask0 = (top_expert == 0).astype(x.dtype)[..., None]
        return out0 * mask0 + out1 * (1.0 - mask0)
    x = x + _L0_attn_ref(_layernorm(x, axis=-1), L0_attn_Wq, L0_attn_bq, L0_attn_Wk, L0_attn_bk, L0_attn_Wv, L0_attn_bv, L0_attn_Wo, L0_attn_bo)
    x = x + _L0_xattn_ref(ctx_512, _layernorm(x, axis=-1), L0_xattn_Wq, L0_xattn_Wk, L0_xattn_gamma_raw)
    x = x + _L0_ffn_ref(_layernorm(x, axis=-1), L0_ffn_router_w, L0_ffn_gate_up_proj, L0_ffn_down_proj, L0_ffn_shared_gate_w, L0_ffn_shared_up_w, L0_ffn_shared_down_w)
    x = x + _L1_attn_ref(_layernorm(x, axis=-1), L1_attn_slope_rate, L1_attn_w_qkv, L1_attn_w_gate, L1_attn_w_out, L1_attn_norm_w)
    x = x + _L1_xattn_ref(ctx_512, _layernorm(x, axis=-1), L1_xattn_W, L1_xattn_b)
    x = x + _L1_ffn_ref(_layernorm(x, axis=-1), L1_ffn_Wg, L1_ffn_W0a, L1_ffn_b0a, L1_ffn_W0b, L1_ffn_b0b, L1_ffn_W1a, L1_ffn_b1a, L1_ffn_W1b, L1_ffn_b1b)
    return x

_drawn_inputs = setup_inputs


def setup_inputs(seed=0):
    import zlib

    import numpy as np

    out = dict(_drawn_inputs(seed))
    spreads = {'L0_attn_bq': (0.0, 0.1),
     'L0_attn_bk': (0.0, 2.0),
     'L0_attn_bv': (0.0, 0.1),
     'L0_attn_bo': (0.0, 0.1),
     'L1_attn_norm_w': (1.0, 0.2)}
    factors = {'L0_ffn_router_w': 5.232,
     'L0_ffn_gate_up_proj': 3.825,
     'L0_ffn_down_proj': 4.283,
     'L1_ffn_b0a': 8.0,
     'L1_ffn_b0b': 4.073,
     'L1_ffn_b1a': 7.597,
     'L1_ffn_b1b': 4.164,
     'L0_ffn_shared_gate_w': 3.221,
     'L0_ffn_shared_up_w': 3.973,
     'L0_ffn_shared_down_w': 3.464}
    for name, (base, spread) in spreads.items():
        noise = np.random.default_rng([zlib.crc32(name.encode()), seed]).standard_normal(out[name].shape)
        drawn = base * np.exp(spread * noise) if base else spread * noise
        out[name] = jnp.asarray(drawn.astype(out[name].dtype))
    for name, factor in factors.items():
        out[name] = (out[name] * factor).astype(out[name].dtype)
    return out
```

```python
from contextlib import ExitStack

import concourse.bass as bass
from concourse import mybir
from concourse.alu_op_type import AluOpType as ALU

ACT = mybir.ActivationFunctionType
F32 = mybir.dt.float32
F32R = mybir.dt.float32r
U32 = mybir.dt.uint32
I32 = mybir.dt.int32
X = mybir.AxisListType.X

P = 128
B, S, E = 4, 256, 256
T = B * S // P
TB = S // P
K = E // P
H0, D0 = 16, 16
HB = P // D0
C = 64
TOPK = int(S * 0.3)
NEXP, FI = 8, 512
FB = FI // P
NSLOT = T + NEXP - 1
HALF = B * S // 2
H1, D1 = 16, 128
BIG = 1e30
EPS = 1e-5
ds = bass.ds


class Chain:

    def __init__(self, eng, sem, base=0):
        self.eng, self.sem, self.base, self.n = eng, sem, base, 0

    def __call__(self, ins):
        ins.then_inc(self.sem, 1)
        self.n += 1
        self.eng.wait_ge(self.sem, self.base + self.n)


def wait_past(eng, sem, value):
    if not isinstance(value, int) or value > 0:
        eng.wait_ge(sem, value)


def decoder(nc, a, sorted_in, sorted_out, out):
    ctx = ExitStack()
    with ctx:
        base = -(-nc.sbuf_base // 64) * 64
        cursor = [base]

        def sb(name, shape, dt=F32):
            n = 4
            for s in shape[1:]:
                n *= s
            at = cursor[0]
            cursor[0] = at + -(-n // 64) * 64
            assert cursor[0] <= nc.sbuf_usable_end, (name, cursor[0] - nc.sbuf_usable_end)
            return nc.alloc_sbuf_tensor_at(name, shape, dt, offset=at)

        def sem(name):
            return ctx.enter_context(nc.semaphore(name))

        banks = ctx.enter_context(nc.psum_tensor("banks", [P, 8, 512], F32))
        ps = [banks[:, i, :] for i in range(8)]

        x = sb("x", [P, T, E])
        at_xn = cursor[0]
        xn = sb("xn", [P, T, E])
        at_xh = cursor[0]
        xh = sb("xh", [P, K, B * S], F32R)
        at_xl = cursor[0]
        xl = sb("xl", [P, K, B * S], F32R)
        ident = sb("ident", [P, P])
        before = sb("before", [P, P])
        ones = sb("ones", [P, P])
        headmask = sb("headmask", [P, HB])
        mhalf = sb("mhalf", [P, TB])
        stats = sb("stats", [P, 2, TB, 6])
        mv = sb("mv", [P, 2, TB, 2])
        ve = sb("ve", [P, 2, TB])
        rstd = sb("rstd", [P, 2, TB])
        bcol = sb("bcol", [P, 4])
        gam = sb("gam", [P, 4])
        zero_row = sb("zero_row", [P, E])
        top8 = sb("top8", [P, TB, 8])
        nmax = sb("nmax", [P, 4, 2])
        psums = sb("psums", [P, TB, H0])
        prec = sb("prec", [P, TB, H0])
        small_end = cursor[0] + 4096
        cursor[0] = small_end

        at_g = cursor[0]
        gu = sb("gu", [P, NEXP, K, 2 * FI])
        at_gu_tail = cursor[0] - 2 * K * 2 * FI * 4
        at_r = cursor[0]

        at_s = cursor[0]
        sgh, sgl, suh, sul = (sb(n, [P, K, FI], F32R) for n in ("sgh", "sgl", "suh", "sul"))
        at_c = cursor[0]
        qT = sb("qT", [P, K, B * S])
        kT = sb("kT", [P, K, B * S])
        v = sb("v", [P, T, E])
        awh = sb("awh", [P, 4, K, E], F32R)
        awl = sb("awl", [P, 4, K, E], F32R)
        alibi = sb("alibi", [P, H0, S])
        at_raw = cursor[0]
        aw = sb("aw", [P, 4, K, E])
        cursor[0] = at_raw
        on = sb("on", [P, TB, E])
        oh = sb("oh", [P, K, S], F32R)
        ol = sb("ol", [P, K, S], F32R)
        adj = sb("adj", [P, TB, S])
        qm = sb("qm", [P, 2, S])
        pr = sb("pr", [P, 4, 3 * P])
        prT = sb("prT", [P, 2, 3 * P])
        work = sb("work", [P, TB, S])
        tanh_sim = sb("tanh_sim", [P, TB, S])
        mask = sb("mask", [P, TB, S])
        adj_sum = sb("adj_sum", [P, TB, S])
        brow = sb("brow", [P, 2, E])
        cursor[0] = at_gu_tail
        ctxT = sb("ctxT", [C, B * S])
        xw = sb("xw", [C, 2, C])
        cQ = sb("cQ", [C, B * S])
        cK = sb("cK", [C, B * S])
        cursor[0] = at_xh
        sim = sb("sim", [P, T, S])
        shared_raw = sb("shared_raw", [P, 2, K, FI])


        cursor[0] = at_c
        head_raw = sb("head_raw", [P, 2, K, 4 * D1])
        dn = sb("dn", [P, NEXP, FB, E])
        sd = sb("sd", [P, FB, E])
        hT = sb("hT", [P, FB, HALF])
        gate = sb("gate", [P, 2, HALF])
        xg = sb("xg", [P, 3, E])
        xgT = sb("xgT", [P, 2, K, P])
        rgate = sb("rgate", [P, FI])
        rh = sb("rh", [P, FI])
        rhT = sb("rhT", [P, FB, P])
        yb = sb("yb", [P, 2, E])
        yg = sb("yg", [P, T, E])
        rw = sb("rw", [P, K, NEXP])
        rwh = sb("rwh", [P, K, NEXP], F32R)
        rwl = sb("rwl", [P, K, NEXP], F32R)
        lg = sb("lg", [P, T, NEXP])
        hit = sb("hit", [P, T, NEXP])
        toplg = sb("toplg", [P, T])
        score = sb("score", [P, T])
        which = sb("which", [P, T])
        onehot = sb("onehot", [P, NEXP, T])
        upto = sb("upto", [P, NEXP, T])
        place = sb("place", [P, NEXP, T])
        ntiles = sb("ntiles", [P, NEXP])
        ends = sb("ends", [P, NEXP])
        starts = sb("starts", [P, NEXP])
        slotf = sb("slotf", [P, T])
        slot = sb("slot", [P, T], U32)
        cmp = sb("cmp", [P, NEXP, T])
        cmp2 = sb("cmp2", [1, NSLOT + 1, NEXP])
        tilef = sb("tilef", [1, NSLOT + 1])
        tile_expert = sb("tile_expert", [1, NSLOT + 1], I32)
        end_c = cursor[0]

        cursor[0] = at_s
        wh = sb("wh", [P, 2, K, 4 * D1], F32R)
        wl = sb("wl", [P, 2, K, 4 * D1], F32R)
        cursor[0] = at_g
        heads = sb("heads", [P, H1, B * S])
        cursor[0] = at_c + 2 * K * 4 * D1 * 4
        decay = sb("decay", [P, H1, S + P])
        masked = sb("masked", [P, 2, TB, S + P])
        at_q = cursor[0]
        qd = sb("qd", [P, 2, B * S])
        kd = sb("kd", [P, 2, B * S])
        vd = sb("vd", [P, 2, T, D1])
        gd = sb("gd", [P, 2, B * S])
        wo = sb("wo", [P, H1, E])
        distance = sb("distance", [P, S + P])
        cursor[0] = at_xn
        squares = sb("squares", [P, 2, HALF])
        square_sum = sb("square_sum", [P, 2, HALF])
        cursor[0] = at_q
        fa = sb("fa", [P, 2, K, FI])
        fah = sb("fah", [P, 2, K, FI], F32R)
        fal = sb("fal", [P, 2, K, FI], F32R)
        fbrow = sb("fbrow", [P, 2, E])
        fg = sb("fg", [P, K, 2])
        fgh = sb("fgh", [P, K, 2], F32R)
        fgl = sb("fgl", [P, K, 2], F32R)
        facol = sb("facol", [P, 2 * FB])
        assert cursor[0] <= at_q + 8 * B * S * 4
        cursor[0] = at_c + 2 * K * 4 * D1 * 4
        fb = sb("fb", [P, 2, FB, E])
        pair = sb("pair", [P, T, S])
        ctx2 = sb("ctx2", [C, B * S])
        ex = sb("ex", [C, 2])
        wj = sb("wj", [C, P])
        eb = sb("eb", [P, 1])
        si = sb("si", [P, T])
        assert cursor[0] <= at_q
        cursor[0] = at_g
        f0 = sb("f0", [P, 2, FB, S])
        f1 = sb("f1", [P, 2, FB, S])
        y0 = sb("y0", [P, TB, E])
        y1 = sb("y1", [P, TB, E])
        choice = sb("choice", [P, TB, 2])
        lg2 = sb("lg2", [P, TB, 2])
        cursor[0] = small_end - 2048
        rev = sb("rev", [P, NEXP])
        steps128 = sb("steps128", [P, T])
        notfirst = sb("notfirst", [P, NEXP, T])
        tile_no = sb("tile_no", [1, NSLOT + 1])
        slopes = sb("slopes", [P, H1])
        nw = sb("nw", [P, H1])
        ms = sb("ms", [P, T])
        rms = sb("rms", [P, T])
        rhalf = sb("rhalf", [P, T])

        x_in = [sem(f"x_in{b}") for b in range(B)]
        aw_in = [sem(f"aw_in{w}") for w in range(4)]
        ctx_in, small_in, shared_in = sem("ctx_in"), sem("small_in"), sem("shared_in")
        gu_in = sem("gu_in")
        consts, const_step = sem("consts"), sem("const_step")
        gam_step = sem("gam_step")
        alibi_ready, aw_split, shared_split, bo_added = sem("alibi_ready"), sem("aw_split"), sem("shared_split"), sem("bo_added")
        ln_step = sem("ln_step")
        var_ready, rstd_ready, xn_ready = sem("var_ready"), sem("rstd_ready"), sem("xn_ready")
        xT_ready, xh_ready, xl_ready = sem("xT_ready"), sem("xh_ready"), sem("xl_ready")
        ctx_qk, ctx_qk_out, sim_ready, sim_out = sem("ctx_qk"), sem("ctx_qk_out"), sem("sim_ready"), sem("sim_out")
        q_ready, k_ready, v_ready = sem("q_ready"), sem("k_ready"), sem("v_ready")
        q_out, k_out, v_out = sem("q_out"), sem("k_out"), sem("v_out")
        qm_ready, s_ready, max_ready, p_ready = sem("qm_ready"), sem("s_ready"), sem("max_ready"), sem("p_ready")
        pT_ready, pT_out, pv_ready = sem("pT_ready"), sem("pT_out"), sem("pv_ready")
        prec_ready, o_out, oT_ready, oh_ready, ol_ready, wo_ready = (sem(n) for n in ("prec_ready", "o_out", "oT_ready", "oh_ready", "ol_ready", "wo_ready"))
        x_added, epi_step, topk_step, work_ready, tanh_ready, adj_ready, adjT_ready, adj_summed, mask_step = (
            sem(n) for n in ("x_added", "epi_step", "topk_step", "work_ready", "tanh_ready", "adj_ready", "adjT_ready", "adj_summed", "mask_step"))
        ln3_step = sem("ln3_step")
        rw_in, sd_in, dn_in, zeroed = sem("rw_in"), sem("sd_in"), sem("dn_in"), sem("zeroed")
        rw_split, logits_ready, route_step, top_ready, score_ready = (sem(n) for n in ("rw_split", "logits_ready", "route_step", "top_ready", "score_ready"))
        xs_ready, onehot_ready, counts_ready, slot_ready, tile_ready = (sem(n) for n in ("xs_ready", "onehot_ready", "counts_ready", "slot_ready", "tile_ready"))
        sgu_ready, sgate_ready, sh_ready, sdown_ready, sdown_added = (sem(n) for n in ("sgu_ready", "sgate_ready", "sh_ready", "sdown_ready", "sdown_added"))
        scattered = sem("scattered")
        xg_in = [sem(f"xg_in{i}") for i in range(3)]
        y_stored = [sem(f"y_stored{i}") for i in range(2)]
        yg_in = [sem(f"yg_in{t}") for t in range(T)]
        xg_turned, xgT_out, gu_done, rgate_ready, rh_ready, rh_turned, rhT_out, y_ready, y_out = (
            sem(n) for n in ("xg_turned", "xgT_out", "gu_done", "rgate_ready", "rh_ready", "rh_turned", "rhT_out", "y_ready", "y_out"))
        yg_added = sem("yg_added")
        head_in = [sem(f"head_in{i}") for i in range(2)]
        slopes_in, nw_in, wo_in, late_in, fb_in = sem("slopes_in"), sem("nw_in"), sem("wo_in"), sem("late_in"), sem("fb_in")
        whi_ready = sem("whi_ready")
        w_split, distance_ready, slopes_negated, powers_ready, decay_ready = (
            sem(n) for n in ("w_split", "distance_ready", "slopes_negated", "powers_ready", "decay_ready"))
        qd_ready, kd_ready, vd_ready, gd_ready = sem("qd_ready"), sem("kd_ready"), sem("vd_ready"), sem("gd_ready")
        qd_out, kd_out, vd_out, gd_out = sem("qd_out"), sem("kd_out"), sem("vd_out"), sem("gd_out")
        scores_ready, masked_ready, head_ready, head_out, squared, square_added = (
            sem(n) for n in ("scores_ready", "masked_ready", "head_ready", "head_out", "squared", "square_added"))
        squares_cleared, wo_scaled, ms_ready, rms_step, rms_ready, y1_ready, y1_added = (
            sem(n) for n in ("squares_cleared", "wo_scaled", "ms_ready", "rms_step", "rms_ready", "y1_ready", "y1_added"))
        ex_ready, pair_ready, si_out, pair_out, fa_split, fg_split = (
            sem(n) for n in ("ex_ready", "pair_ready", "si_out", "pair_out", "fa_split", "fg_split"))
        fa_in = [sem(f"fa_in{i}") for i in range(2)]
        fg_in, facol_in = sem("fg_in"), sem("facol_in")
        ln45_step = sem("ln45_step")
        up_ready, f0_out, f1_out, f_ready, f_step, choice_step, x_final = (
            sem(n) for n in ("up_ready", "f0_out", "f1_out", "f_ready", "f_step", "choice_step", "x_final"))
        done, out_done = sem("done"), sem("out_done")

        ROUNDS = -(-TOPK // 8)
        TOPK_LINKS = 2 * ROUNDS - 1
        EPI_LINKS = 9

        SLOPES = [2.0 ** (-0.5 * (i + 1)) for i in range(H0)]

        block = ctx.enter_context(nc.Block())

        def flat(ap):
            return ap.rearrange("p a b -> p (a b)")

        @block.sync
        def _(sp):
            xv = a["x"].rearrange("b (t p) e -> b p t e", p=P)
            for b in range(B):
                sp.dma_start(x[:, TB * b:TB * b + TB, :], xv[b]).then_inc(x_in[b], 16)
            sp.dma_start(ctxT[:], a["ctxT"]).then_inc(ctx_in, 16)
            sp.dma_start(xw[:], a["xw"]).then_inc(ctx_in, 16)
            for w in range(4):
                sp.dma_start(aw[:, w, :, :], a["aw"][w].rearrange("(k p) n -> p k n", p=P)).then_inc(aw_in[w], 16)
            sp.dma_start(bcol[:], a["abcol"]).then_inc(small_in, 16)
            sp.dma_start(brow[:], a["abrow"].rearrange("(o r) n -> o r n", o=1).broadcast_to([P, 2, E])).then_inc(small_in, 16)
            sp.dma_start(gam[:, 0:1], a["gamma"].broadcast_to([P, 1])).then_inc(small_in, 16)
            for e in range(NEXP - 2):
                sp.dma_start(gu[:, e], a["gu"][e].rearrange("(k p) n -> p k n", p=P)).then_inc(gu_in, 16)
            sp.wait_ge(sim_ready, B)
            for e in range(NEXP - 2, NEXP):
                sp.dma_start(gu[:, e], a["gu"][e].rearrange("(k p) n -> p k n", p=P)).then_inc(gu_in, 16)
            sp.wait_ge(v_ready, B)
            sp.dma_start(shared_raw[:, 0], a["sg"].rearrange("(k p) n -> p k n", p=P)).then_inc(shared_in, 16)
            sp.dma_start(shared_raw[:, 1], a["su"].rearrange("(k p) n -> p k n", p=P)).then_inc(shared_in, 16)
            sp.wait_ge(consts, 1)
            for j in range(NSLOT):
                sp.dma_start(sorted_in[j * P:(j + 1) * P, :], zero_row[:]).then_inc(zeroed, 16)
            sp.wait_ge(wo_ready, B)
            sp.wait_ge(adj_summed, B)
            sp.dma_start(rw[:], a["rw"]).then_inc(rw_in, 16)
            sp.dma_start(sd[:], a["sd"].rearrange("(f p) n -> p f n", p=P)).then_inc(sd_in, 16)
            for e in range(NEXP):
                sp.dma_start(dn[:, e], a["dn"][e].rearrange("(f p) n -> p f n", p=P)).then_inc(dn_in, 16)

            def load_tile(j):
                wait_past(sp, xg_turned, j - 2)
                sp.dma_start(xg[:, j % 3, :], sorted_in[j * P:(j + 1) * P, :]).then_inc(xg_in[j % 3], 16)

            sp.wait_ge(scattered, 16 * T)
            for j in range(3):
                load_tile(j)
            for j in range(NSLOT):
                sp.wait_ge(y_out, j + 1)
                sp.dma_start(sorted_out[j * P:(j + 1) * P, :], yb[:, j % 2, :]).then_inc(y_stored[j % 2], 16)
                if j + 3 < NSLOT:
                    load_tile(j + 3)
            sp.dma_start(slopes[:], a["slopes"].broadcast_to([P, H1])).then_inc(slopes_in, 16)
            sp.dma_start(nw[:], a["nw"]).then_inc(nw_in, 16)

            def load_head(h, i):
                if not isinstance(h, int) or h >= 2:
                    sp.wait_ge(w_split, h - 1)
                sp.dma_start(head_raw[:, i], a["heads"][ds(h, 1)].rearrange("o p k n -> p (o k) n")).then_inc(head_in[i], 16)

            load_head(0, 0)
            load_head(1, 1)
            sp.wait_ge(yg_added, B)
            sp.wait_ge(xl_ready, 3 * B)
            sp.dma_start(wo[:], a["wo"]).then_inc(wo_in, 16)
            with sp.Fori(2, H1 - 1, 2) as h:
                load_head(h, 0)
                load_head(h + 1, 1)
            sp.wait_ge(masked_ready, 2 * H1)
            sp.dma_start(ex[:], a["ex"]).then_inc(late_in, 16)
            sp.dma_start(eb[:], a["eb"].broadcast_to([P, 1])).then_inc(late_in, 16)
            sp.dma_start(ctx2[:], a["ctxT"]).then_inc(late_in, 16)
            sp.dma_start(fb[:, 0], a["fb"][0].rearrange("(f p) n -> p f n", p=P)).then_inc(fb_in, 16)
            sp.dma_start(fb[:, 1], a["fb"][1].rearrange("(f p) n -> p f n", p=P)).then_inc(fb_in, 16)
            sp.wait_ge(head_ready, 2 * H1)
            sp.wait_ge(head_out, 2 * H1)
            for i in range(2):
                sp.dma_start(fa[:, i], a["fa"][i].rearrange("(k p) n -> p k n", p=P)).then_inc(fa_in[i], 16)
            sp.dma_start(fg[:], a["fg"]).then_inc(fg_in, 16)
            sp.dma_start(facol[:], a["facol"]).then_inc(facol_in, 16)
            sp.dma_start(fbrow[:], a["fbrow"].rearrange("(o r) n -> o r n", o=1).broadcast_to([P, 2, E])).then_inc(facol_in, 16)
            ov = out.rearrange("b (t p) e -> b p t e", p=P)
            for b in range(B):
                sp.wait_ge(x_final, b + 1)
                sp.dma_start(ov[b], x[:, TB * b:TB * b + TB, :]).then_inc(out_done, 16)
            sp.wait_ge(out_done, 16 * B)

        @block.gpsimd
        def _(pool):
            step = Chain(pool, const_step)
            step(pool.memset(ones[:], 1.0))
            pool.memset(mhalf[:], -0.5)
            pool.memset(zero_row[:], 0.0)
            pool.affine_select(ident[:], ones[:], [[-1, P]], ALU.is_equal, 0.0, base=0, channel_multiplier=1)
            step(pool.memset(headmask[:], -1.0 / D0 ** 0.5))
            step(pool.affine_select(headmask[:], headmask[:], [[-D0, HB]], ALU.is_ge, 0.0, base=0, channel_multiplier=1))
            pool.affine_select(headmask[:], headmask[:], [[D0, HB]], ALU.is_ge, 0.0, base=D0 - 1, channel_multiplier=-1)
            pool.iota(rev[:], [[-1, NEXP]], base=NEXP, channel_multiplier=0, allow_small_or_imprecise_dtypes=True)
            pool.iota(steps128[:], [[P, T]], base=0, channel_multiplier=0, allow_small_or_imprecise_dtypes=True)
            pool.iota(tile_no[:], [[1, NSLOT + 1]], base=0, channel_multiplier=0, allow_small_or_imprecise_dtypes=True)
            step(pool.memset(notfirst[:], 1.0))
            pool.memset(notfirst[:, :, 0:1], 0.0)
            pool.affine_select(before[:], ones[:], [[1, P]], ALU.is_gt, 0.0, base=0, channel_multiplier=-1)\
                .then_inc(consts, 1)

            def root(n, slot):
                pool.wait_ge(var_ready, n + 1)
                pool.tensor_tensor(rstd[:, slot], ve[:, slot], mhalf[:], ALU.pow).then_inc(rstd_ready, 1)

            root(0, 0)
            root(1, 1)
            step(pool.iota(flat(alibi[:, H0 - 1:H0, :]), [[-1, S]], base=P, channel_multiplier=1,
                           allow_small_or_imprecise_dtypes=True))
            root(2, 0)
            root(3, 1)
            for w in range(4):
                pool.wait_ge(aw_in[w], 16)
                step(pool.tensor_copy(awh[:, w], aw[:, w]))
                pool.tensor_tensor(awl[:, w], aw[:, w], awh[:, w].bitcast(F32), ALU.subtract).then_inc(aw_split, 1)
            for h in range(H0):
                last = pool.tensor_scalar(alibi[:, h, :], alibi[:, H0 - 1, :], SLOPES[h], None, ALU.mult)
            step(last)
            pool.affine_select(alibi[:], alibi[:], [[0, H0], [-1, S]], ALU.is_ge, BIG, base=P, channel_multiplier=1)\
                .then_inc(alibi_ready, 1)
            pool.wait_ge(small_in, 48)
            for b in range(B):
                pool.wait_ge(xn_ready, TB * (b + 1))
                pool.tensor_tensor(x[:, TB * b:TB * b + TB, :], x[:, TB * b:TB * b + TB, :],
                                   brow[:, 1:2, :].broadcast_to([P, TB, E]), ALU.add).then_inc(bo_added, 1)

            def attention(b, epilogue):
                pool.wait_ge(sim_out, B)
                wait_past(pool, adj_ready, b)
                pool.tensor_copy(work[:], sim[:, ds(b * TB, TB), :]).then_inc(work_ready, 1)
                pool.wait_ge(q_out, B)
                for h in range(H0):
                    wait_past(pool, s_ready, b * H0 + h - 1)
                    pool.tensor_tensor(qm[:, h % 2, :], qT[:, h // HB, ds(b * S, S)],
                                       headmask[:, h % HB:h % HB + 1].broadcast_to([P, S]), ALU.mult)\
                        .then_inc(qm_ready, 1)
                    if epilogue and h == 9:
                        roots_of(b - 1, 0)
                    if epilogue and h == 12:
                        roots_of(b - 1, 1)

            def roots_of(b, n):
                pool.wait_ge(var_ready, b * 2 + B + 1 + n)
                pool.tensor_tensor(rstd[:, 0], ve[:, 0], mhalf[:], ALU.pow).then_inc(rstd_ready, 1)

            attention(0, False)
            pool.wait_ge(shared_in, 32)
            for w, (hi, lo) in enumerate(((sgh, sgl), (suh, sul))):
                step(pool.tensor_copy(hi[:], shared_raw[:, w]))
                pool.tensor_tensor(lo[:], shared_raw[:, w], hi[:].bitcast(F32), ALU.subtract).then_inc(shared_split, 2)
            for b in range(1, B):
                attention(b, True)
            roots_of(B - 1, 0)
            roots_of(B - 1, 1)
            pool.wait_ge(rw_in, 16)
            step(pool.tensor_copy(rwh[:], rw[:]))
            pool.tensor_tensor(rwl[:], rw[:], rwh[:].bitcast(F32), ALU.subtract).then_inc(rw_split, 1)
            pool.wait_ge(zeroed, 16 * NSLOT)
            pool.wait_ge(slot_ready, 1)
            for t in range(T):
                pool.wait_ge(xs_ready, t + 1)
                pool.indirect_dma_start(out=sorted_in, out_offset=bass.IndirectOffsetOnAxis(ap=slot[:, t:t + 1], axis=0),
                                        in_=xn[:, t, :], in_offset=None).then_inc(scattered, 16)
            for i in range(2):
                pool.wait_ge(y_stored[i], 16 * ((NSLOT + 1 - i) // 2))
            for t in range(T):
                pool.indirect_dma_start(out=yg[:, t, :], out_offset=None, in_=sorted_out,
                                        in_offset=bass.IndirectOffsetOnAxis(ap=slot[:, t:t + 1], axis=0))\
                    .then_inc(yg_in[t], 16)

            pool.wait_ge(y_ready, NSLOT)
            pool.iota(distance[:, 0:S], [[1, S]], base=0, channel_multiplier=-1, allow_small_or_imprecise_dtypes=True)
            step(pool.iota(distance[:, S:S + P], [[1, P]], base=0, channel_multiplier=-1, allow_small_or_imprecise_dtypes=True))
            pool.tensor_scalar(distance[:], distance[:], 0.0, None, ALU.max).then_inc(distance_ready, 1)
            for b in range(B):
                root(3 * B + b, b % 2)

            def split_head(h, i):
                if isinstance(h, int) and h < 2:
                    pool.wait_ge(head_in[i], 16)
                    if h == 0:
                        pool.wait_ge(sdown_ready, B)
                else:
                    pool.wait_ge(head_in[i], 8 * (h - i) + 16)
                    pool.wait_ge(vd_ready, h - 1)
                    pool.wait_ge(gd_ready, h - 1)
                pool.tensor_tensor(wh[:, i].rearrange("p k n -> p (k n)"), head_raw[:, i].rearrange("p k n -> p (k n)"),
                                   ones[:, 0:1].broadcast_to([P, K * 4 * D1]), ALU.mult).then_inc(whi_ready, 1)
                pool.wait_ge(whi_ready, h + 1)
                pool.tensor_tensor(wl[:, i], head_raw[:, i], wh[:, i].bitcast(F32), ALU.subtract).then_inc(w_split, 1)

            def add_squares(h):
                for half in range(2):
                    pool.wait_ge(squared, 2 * h + half + 1)
                    pool.tensor_tensor(square_sum[:, half], square_sum[:, half], squares[:, half], ALU.add)\
                        .then_inc(square_added, 1)

            split_head(0, 0)
            split_head(1, 1)
            pool.wait_ge(powers_ready, H1)
            pool.affine_select(decay[:, :, 0:S], decay[:, :, 0:S], [[0, H1], [1, S]], ALU.is_ge, 0.0, base=0, channel_multiplier=-1)
            pool.affine_select(decay[:, :, S:S + P], decay[:, :, S:S + P], [[0, H1], [1, P]], ALU.is_ge, 0.0, base=0,
                               channel_multiplier=-1).then_inc(decay_ready, 1)
            pool.wait_ge(xl_ready, 3 * B)
            step(pool.memset(square_sum[:], 0.0))
            pool.wait_ge(wo_in, 16)
            pool.wait_ge(nw_in, 16)
            step(pool.tensor_scalar(nw[:], nw[:], 0.5, None, ALU.mult))
            pool.tensor_tensor(wo[:], wo[:], nw[:].unsqueeze(2).broadcast_to([P, H1, E]), ALU.mult).then_inc(wo_scaled, 1)
            add_squares(0)
            split_head(2, 0)
            add_squares(1)
            split_head(3, 1)
            with pool.Fori(2, H1 - 2, 2) as h:
                add_squares(h)
                split_head(h + 2, 0)
                add_squares(h + 1)
                split_head(h + 3, 1)
            add_squares(H1 - 2)
            add_squares(H1 - 1)
            pool.wait_ge(rms_step, 1)
            pool.memset(rhalf[:], -0.5).then_inc(rms_step, 1)
            pool.wait_ge(rms_step, 2)
            pool.tensor_tensor(rms[:], ms[:], rhalf[:], ALU.pow).then_inc(rms_ready, 1)
            for i in range(2):
                pool.wait_ge(fa_in[i], 16)
                step(pool.tensor_copy(fah[:, i], fa[:, i]))
                pool.tensor_tensor(fal[:, i], fa[:, i], fah[:, i].bitcast(F32), ALU.subtract).then_inc(fa_split, 1)
            for b in range(B):
                root(4 * B + 2 * b, b % 2)
                root(4 * B + 2 * b + 1, b % 2)
                if b == 0:
                    pool.wait_ge(fg_in, 16)
                    step(pool.tensor_copy(fgh[:], fg[:]))
                    pool.tensor_tensor(fgl[:], fg[:], fgh[:].bitcast(F32), ALU.subtract).then_inc(fg_split, 1)

        @block.vector
        def _(dve):
            ln = Chain(dve, ln_step)

            def norm_stats(link, src, slot, n_sem=var_ready):
                for t in range(TB):
                    last = dve.bn_stats(stats[:, slot, t, :], src[t])
                link(last)
                for t in range(TB):
                    last = dve.bn_aggr(mv[:, slot, t, :], stats[:, slot, t, :])
                link(last)
                dve.tensor_scalar(ve[:, slot, :], mv[:, slot, :, 1], EPS, None, ALU.add).then_inc(var_ready, 1)

            def normalise(dst, src, slot):
                for t in range(TB):
                    last = dve.tensor_scalar(dst[t], src[t], mv[:, slot, t, 0:1], rstd[:, slot, t:t + 1],
                                             ALU.subtract, ALU.mult)
                return last

            def tiles(buf, b):
                return [buf[:, TB * b + t, :] for t in range(TB)]

            def low_part(n, b):
                dve.wait_ge(xh_ready, n + 1)
                dve.tensor_tensor(xl[:, :, b * S:(b + 1) * S], ps[7][:].rearrange("p (k s) -> p k s", k=K),
                                  xh[:, :, b * S:(b + 1) * S].bitcast(F32), ALU.subtract).then_inc(xl_ready, 1)

            for b in range(B + 1):
                if b < B:
                    dve.wait_ge(x_in[b], 16)
                    norm_stats(ln, tiles(x, b), b % 2)
                if b >= 1:
                    dve.wait_ge(rstd_ready, b)
                    normalise(tiles(xn, b - 1), tiles(x, b - 1), (b - 1) % 2).then_inc(xn_ready, TB)
            dve.wait_ge(small_in, 48)
            low_part(0, 0)
            for b in range(B):
                if b + 1 < B:
                    low_part(b + 1, b + 1)
                dve.wait_ge(v_ready, b + 1)
                dve.tensor_tensor(v[:, TB * b:TB * b + TB, :], ps[2][:].rearrange("p (t e) -> p t e", t=TB),
                                  brow[:, 0:1, :].broadcast_to([P, TB, E]), ALU.add).then_inc(v_out, 1)
            gs = Chain(dve, gam_step, 1)
            dve.wait_ge(gam_step, 1)
            gs(dve.tensor_scalar(gam[:, 1:2], gam[:, 1:2], 1.0, None, ALU.add))
            gs(dve.reciprocal(gam[:, 2:3], gam[:, 1:2]))
            dve.tensor_scalar(gam[:, 1:2], gam[:, 2:3], -1.0, 1.0, ALU.mult, ALU.add)
            gs(dve.tensor_scalar(gam[:, 3:4], gam[:, 2:3], 0.25, None, ALU.mult))

            def topk_round(b, r):
                j, r = divmod(r, ROUNDS)
                base = b * (TB * TOPK_LINKS) + j * TOPK_LINKS + 2 * r
                if r == 0:
                    wait_past(dve, work_ready, b + 1)
                if r > 0:
                    wait_past(dve, topk_step, base)
                dve.max(top8[:, j, :], work[:, j, :]).then_inc(topk_step, 1)
                if r < ROUNDS - 1:
                    wait_past(dve, topk_step, base + 1)
                    dve.match_replace(work[:, j, :], top8[:, j, :], work[:, j, :], -3.0e38).then_inc(topk_step, 1)
                elif j == TB - 1:
                    wait_past(dve, topk_step, base + 1)

            def sparse_adjacency(b):
                at = (TOPK - 1) % 8
                for t in range(TB):
                    last = dve.tensor_scalar(mask[:, t, :], sim[:, ds(b * TB + t, 1), :], top8[:, t, at:at + 1], None,
                                             ALU.is_ge)
                last.then_inc(mask_step, 1)
                dve.wait_ge(mask_step, b + 1)
                dve.wait_ge(tanh_ready, b + 1)
                dve.scalar_tensor_tensor(flat(adj[:]), flat(tanh_sim[:]), 1.0, flat(mask[:]), ALU.add, ALU.mult)\
                    .then_inc(adj_ready, 1)

            def epilogue(b, part, link):
                xb = x[:, ds(b * TB, TB), :]
                if part == 0:
                    dve.wait_ge(p_ready, b * H0 + H0)
                    link(dve.reciprocal(prec[:], psums[:]))
                    dve.wait_ge(pv_ready, b * H0 + H0)
                    dve.tensor_tensor(on[:].rearrange("p t (h d) -> p (t h) d", h=H0),
                                      ps[4][:].rearrange("p (a d) -> p a d", d=D0),
                                      flat(prec[:]).unsqueeze(2).broadcast_to([P, TB * H0, D0]),
                                      ALU.mult).then_inc(o_out, 1)
                elif part == 1:
                    dve.wait_ge(oh_ready, b + 1)
                    dve.tensor_tensor(flat(ol[:]), ps[5][:], flat(oh[:]).bitcast(F32), ALU.subtract).then_inc(ol_ready, 1)
                    dve.wait_ge(adjT_ready, b + 1)
                    dve.tensor_tensor(flat(adj_sum[:]), ps[6][:], flat(adj[:]), ALU.add).then_inc(adj_summed, 1)
                elif part == 2:
                    dve.wait_ge(bo_added, B)
                    dve.wait_ge(wo_ready, b + 1)
                    ins = dve.tensor_tensor(xb, ps[5][:].rearrange("p (t e) -> p t e", t=TB), xb, ALU.add)
                    link(ins)
                    norm_stats(link, [x[:, ds(b * TB + t, 1), :] for t in range(TB)], 0)
                elif part == 3:
                    dve.wait_ge(rstd_ready, b * 2 + B + 1)
                    link(normalise([on[:, t, :] for t in range(TB)], [x[:, ds(b * TB + t, 1), :] for t in range(TB)], 0))
                    link(dve.scalar_tensor_tensor(xb, on[:], gam[:, 1:2], xb, ALU.mult, ALU.add))
                    link(dve.scalar_tensor_tensor(xb, adj_sum[:], gam[:, 3:4], xb, ALU.mult, ALU.add))
                    norm_stats(link, [x[:, ds(b * TB + t, 1), :] for t in range(TB)], 0)
                else:
                    dve.wait_ge(rstd_ready, b * 2 + B + 2)
                    normalise([xn[:, ds(b * TB + t, 1), :] for t in range(TB)],
                              [x[:, ds(b * TB + t, 1), :] for t in range(TB)], 0).then_inc(xn_ready, TB)

            def attention(b, with_epilogue):
                if with_epilogue:
                    link = Chain(dve, epi_step, (b - 1) * EPI_LINKS)
                for h in range(H0):
                    if with_epilogue and h in (1, 5, 8, 11, 14):
                        epilogue(b - 1, (1, 5, 8, 11, 14).index(h), link)
                    n = b * H0 + h
                    wait_past(dve, s_ready, n + 1)
                    wait_past(dve, pT_ready, n - 3)
                    dve.tensor_tensor_reduce(pr[:, h % 4, 0:P], ps[h % 2][:, 0:P], alibi[:, h, P:2 * P], 1.0, 3.0e38,
                                             ALU.add, ALU.min, nmax[:, h % 4, 0:1])
                    dve.tensor_tensor_reduce(pr[:, h % 4, P:3 * P], ps[h % 2][:, P:3 * P], alibi[:, h, :], 1.0, 3.0e38,
                                             ALU.add, ALU.min, nmax[:, h % 4, 1:2]).then_inc(max_ready, 1)
                    for r in range(TB * ROUNDS * h // H0, TB * ROUNDS * (h + 1) // H0):
                        topk_round(b, r)
                sparse_adjacency(b)
                if with_epilogue:
                    assert link.n == EPI_LINKS, link.n

            dve.wait_ge(alibi_ready, 1)
            for b in range(B):
                attention(b, b > 0)
            link = Chain(dve, epi_step, (B - 1) * EPI_LINKS)
            for part in range(5):
                epilogue(B - 1, part, link)

            for b in range(B):
                low_part(B + b, b)
            link = Chain(dve, route_step)
            dve.wait_ge(logits_ready, 1)
            link(dve.tensor_copy(lg[:], ps[0][:, 0:T * NEXP].rearrange("p (t e) -> p t e", t=T)))
            dve.tensor_reduce(toplg[:], lg[:], X, ALU.max).then_inc(top_ready, 1)
            dve.wait_ge(top_ready, 1)
            link(dve.tensor_tensor(hit[:], lg[:], toplg[:].unsqueeze(2).broadcast_to([P, T, NEXP]), ALU.is_equal))
            link(dve.tensor_tensor(hit[:], hit[:], rev[:].unsqueeze(1).broadcast_to([P, T, NEXP]), ALU.mult))
            link(dve.tensor_reduce(which[:], hit[:], X, ALU.max))
            dve.tensor_tensor(onehot[:].rearrange("p e t -> p t e"), rev[:].unsqueeze(1).broadcast_to([P, T, NEXP]),
                              which[:].unsqueeze(2).broadcast_to([P, T, NEXP]), ALU.is_equal).then_inc(onehot_ready, 1)

            def shared_hidden(i):
                dve.wait_ge(sgate_ready, i + 1)
                wait_past(dve, sdown_ready, (i // FB) * 2)
                dve.tensor_tensor(hT[:, i % FB, :], ps[2 + 2 * (i % 2)][:], gate[:, i % 2, :], ALU.mult)\
                    .then_inc(sh_ready, 1)

            def shared_added(b):
                dve.wait_ge(sdown_ready, b + 1)
                dve.tensor_tensor(x[:, TB * b:TB * b + TB, :], ps[5 + b % 2][:].rearrange("p (t e) -> p t e", t=TB),
                                  x[:, TB * b:TB * b + TB, :], ALU.add).then_inc(sdown_added, 1)

            shared_hidden(0)
            dve.wait_ge(counts_ready, 1)
            total = ps[0][:, 128:128 + T * NEXP]
            link(dve.tensor_tensor_scan(flat(upto[:]), flat(notfirst[:]), total, 0.0, ALU.mult, ALU.add))
            link(dve.tensor_tensor(flat(place[:]), flat(upto[:]), total, ALU.subtract))
            link(dve.tensor_tensor(flat(place[:]), ps[0][:, 64:64 + T * NEXP], flat(place[:]), ALU.add))
            link(dve.tensor_tensor(cmp[:], upto[:, :, T - 1:T].broadcast_to([P, NEXP, T]),
                                   steps128[:].unsqueeze(1).broadcast_to([P, NEXP, T]), ALU.is_gt))
            link(dve.tensor_reduce(ntiles[:], cmp[:], X, ALU.add))
            link(dve.tensor_tensor_scan(ends[:], ones[:, 0:NEXP], ntiles[:], 0.0, ALU.mult, ALU.add))
            link(dve.tensor_tensor(starts[:], ends[:], ntiles[:], ALU.subtract))
            link(dve.scalar_tensor_tensor(place[:], starts[:].unsqueeze(2).broadcast_to([P, NEXP, T]), float(P), place[:],
                                          ALU.mult, ALU.add))
            link(dve.tensor_tensor(place[:], place[:], onehot[:], ALU.mult))
            link(dve.tensor_reduce(slotf[:], place[:].rearrange("p e t -> p t e"), X, ALU.add))
            dve.tensor_copy(slot[:], slotf[:]).then_inc(slot_ready, 1)
            link(dve.tensor_tensor(cmp2[:], ends[0:1, :].unsqueeze(1).broadcast_to([1, NSLOT + 1, NEXP]),
                                   tile_no[:].unsqueeze(2).broadcast_to([1, NSLOT + 1, NEXP]), ALU.is_le))
            link(dve.tensor_reduce(tilef[:], cmp2[:], X, ALU.add))
            dve.tensor_scalar(tile_expert[:], tilef[:], float(NEXP - 1), None, ALU.min).then_inc(tile_ready, 1)
            for i in range(1, FB):
                shared_hidden(i)
            shared_added(0)
            shared_added(1)
            def routed_hidden(j):
                dve.wait_ge(rgate_ready, j + 1)
                wait_past(dve, rh_turned, j)
                dve.tensor_tensor(rh[:], ps[2][:], rgate[:], ALU.mult).then_inc(rh_ready, 1)

            def routed_out(j):
                dve.wait_ge(y_ready, j + 1)
                wait_past(dve, y_stored[j % 2], 16 * (j // 2))
                dve.tensor_copy(yb[:, j % 2, :], ps[4][:, 0:E]).then_inc(y_out, 1)

            for j in range(NSLOT):
                routed_hidden(j)
                if j >= 1:
                    routed_out(j - 1)
            routed_out(NSLOT - 1)
            for i in range(FB, 2 * FB):
                shared_hidden(i)
            shared_added(2)
            shared_added(3)
            ln3 = Chain(dve, ln3_step)

            def late_norm(n, stage, residual):
                for b in range(B + 1):
                    if b < B:
                        residual(b)
                        norm_stats(ln3, tiles(x, b), b % 2)
                    if b >= 1:
                        dve.wait_ge(rstd_ready, n + b)
                        normalise(tiles(xn, b - 1), tiles(x, b - 1), (b - 1) % 2).then_inc(xn_ready, TB)
                    if b >= 2:
                        low_part(stage * B + b - 2, b - 2)
                low_part(stage * B + B - 1, B - 1)

            def add_routed(b):
                for t in range(TB * b, TB * b + TB):
                    dve.wait_ge(yg_in[t], 16)
                dve.wait_ge(sdown_added, b + 1)
                dve.tensor_tensor(x[:, TB * b:TB * b + TB, :], x[:, TB * b:TB * b + TB, :],
                                  yg[:, TB * b:TB * b + TB, :], ALU.add).then_inc(yg_added, 1)
                dve.wait_ge(yg_added, b + 1)

            dve.wait_ge(slopes_in, 16)
            dve.tensor_scalar(slopes[:], slopes[:], -1.0, None, ALU.mult).then_inc(slopes_negated, 1)
            late_norm(3 * B, 2, add_routed)

            def mask_scores(h, i):
                for p in range(2):
                    dve.wait_ge(scores_ready, 2 * h + p + 1)
                    wait_past(dve, head_ready, 2 * h + p - 1)
                    dve.tensor_tensor(masked[:, p], banks[:, 4:6, 0:S + P],
                                      decay[:, ds(h, 1), :].broadcast_to([P, TB, S + P]), ALU.mult).then_inc(masked_ready, 1)

            def gate_head(h, i):
                dve.wait_ge(gd_out, h + 1)
                for p in range(2):
                    dve.wait_ge(head_ready, 2 * h + p + 1)
                    dve.scalar_tensor_tensor(heads[:, ds(h, 1), p * HALF:(p + 1) * HALF], gd[:, i, p * HALF:(p + 1) * HALF],
                                             1.0, ps[6 + p][:], ALU.add, ALU.mult).then_inc(head_out, 1)

            dve.wait_ge(decay_ready, 1)
            for h in (0, 1):
                mask_scores(h, h % 2)
                gate_head(h, h % 2)
            with dve.Fori(2, H1 - 2, 2) as h:
                for i in range(2):
                    mask_scores(h + i, i)
                    gate_head(h + i, i)
            for h in (H1 - 2, H1 - 1):
                mask_scores(h, h % 2)
                gate_head(h, h % 2)
            dve.wait_ge(ms_ready, 1)
            dve.tensor_scalar(ms[:], ps[2][:, 0:T], 1.0 / (H1 * D1), 1e-6, ALU.mult, ALU.add).then_inc(rms_step, 1)
            dve.wait_ge(late_in, 48)
            dve.tensor_scalar(wj[:], ones[0:C, :], ex[:, 1:2], None, ALU.mult).then_inc(ex_ready, 1)
            dve.wait_ge(pair_ready, 1)
            dve.tensor_scalar(si[:], ps[3][:, 0:T], eb[:, 0:1], None, ALU.add).then_inc(si_out, 1)
            dve.wait_ge(rms_ready, 1)
            l45 = Chain(dve, ln45_step)

            def add_linear(b):
                dve.wait_ge(y1_ready, b + 1)
                for t in range(TB):
                    last = dve.scalar_tensor_tensor(x[:, TB * b + t, :], ps[b % 2][:, t * E:(t + 1) * E],
                                                    rms[:, TB * b + t:TB * b + t + 1], x[:, TB * b + t, :], ALU.mult, ALU.add)
                last.then_inc(y1_added, 1)
                dve.wait_ge(y1_added, b + 1)


            def add_pair(b):
                dve.wait_ge(rstd_ready, 4 * B + 2 * b + 1)
                l45(normalise(tiles(xn, b), tiles(x, b), b % 2))
                xb = x[:, TB * b:TB * b + TB, :]
                l45(dve.scalar_tensor_tensor(xb, xn[:, TB * b:TB * b + TB, :], 1.0 - 0.6, xb, ALU.mult, ALU.add))
                dve.wait_ge(pair_out, TB * b + TB)
                l45(dve.scalar_tensor_tensor(xb, pair[:, TB * b:TB * b + TB, :], 0.6, xb, ALU.mult, ALU.add))


            def relu_hidden(b):
                dve.wait_ge(up_ready, 2 * b + 2)
                wait_past(dve, f_ready, 2 * b - 2)
                for m in range(FB):
                    last = dve.tensor_scalar(f1[:, b % 2, m, :], ps[4 + m // 2][:, (m % 2) * S:(m % 2 + 1) * S],
                                             facol[:, FB + m:FB + m + 1], 0.0, ALU.add, ALU.max)
                last.then_inc(f1_out, 1)

            def combine(b):
                link = Chain(dve, f_step, 3 * b)
                dve.wait_ge(f_ready, 2 * b + 2)
                brow2 = fbrow[:, 0:1, :].broadcast_to([P, TB, E]), fbrow[:, 1:2, :].broadcast_to([P, TB, E])
                link(dve.tensor_tensor(y0[:], ps[2][:].rearrange("p (t e) -> p t e", t=TB), brow2[0], ALU.add))
                link(dve.tensor_tensor(y1[:], ps[3][:].rearrange("p (t e) -> p t e", t=TB), brow2[1], ALU.add))
                for t in range(TB):
                    last = dve.scalar_tensor_tensor(x[:, TB * b + t, :], y0[:, t, :], choice[:, t, 0:1],
                                                    x[:, TB * b + t, :], ALU.mult, ALU.add)
                link(last)
                for t in range(TB):
                    last = dve.scalar_tensor_tensor(x[:, TB * b + t, :], y1[:, t, :], choice[:, t, 1:2],
                                                    x[:, TB * b + t, :], ALU.mult, ALU.add)
                last.then_inc(x_final, 1)

            def choose(b):
                dve.wait_ge(up_ready, 2 * b + 1)
                wait_past(dve, x_final, b)
                ch = Chain(dve, choice_step, 3 * b)
                ch(dve.tensor_copy(lg2[:], ps[7][:, 0:2 * TB].rearrange("p (t e) -> p t e", t=TB)))
                ch(dve.tensor_tensor(choice[:, :, 0:1], lg2[:, :, 0:1], lg2[:, :, 1:2], ALU.is_ge))
                ch(dve.tensor_scalar(choice[:, :, 1:2], choice[:, :, 0:1], -1.0, 1.0, ALU.mult, ALU.add))

            for b in range(B):
                add_linear(b)
                norm_stats(l45, tiles(x, b), b % 2)
                add_pair(b)
                norm_stats(l45, tiles(x, b), b % 2)
                dve.wait_ge(rstd_ready, 4 * B + 2 * b + 2)
                normalise(tiles(xn, b), tiles(x, b), b % 2).then_inc(xn_ready, TB)
                if b:
                    low_part(3 * B + b - 1, b - 1)
            low_part(4 * B - 1, B - 1)
            dve.wait_ge(facol_in, 32)
            for b in range(B):
                if b:
                    combine(b - 1)
                choose(b)
                relu_hidden(b)
            combine(B - 1)

        @block.scalar
        def _(act):
            def high_part(n, b):
                act.wait_ge(xT_ready, n + 1)
                act.activation(xh[:, :, b * S:(b + 1) * S], ps[7][:].rearrange("p (k s) -> p k s", k=K), ACT.Copy)\
                    .then_inc(xh_ready, 1)

            act.wait_ge(small_in, 48)
            act.activation(gam[:, 1:2], gam[:, 0:1], ACT.Exp, scale=-1.0).then_inc(gam_step, 1)
            for i, dst in enumerate((cQ, cQ, cK, cK)):
                act.wait_ge(ctx_qk, i + 1)
                act.activation(dst[:, (i % 2) * 512:(i % 2) * 512 + 512], ps[3 + i][0:C, :], ACT.Copy)\
                    .then_inc(ctx_qk_out, 1)

            def project_out(b):
                for bank, s_in, dst, s_out, col in ((0, q_ready, qT, q_out, 0), (1, k_ready, kT, k_out, K)):
                    act.wait_ge(s_in, b + 1)
                    for k in range(K):
                        last = act.activation(dst[:, k, b * S:(b + 1) * S], ps[bank][:, k * S:(k + 1) * S], ACT.Identity,
                                              bias=bcol[:, col + k:col + k + 1])
                    last.then_inc(s_out, 1)

            high_part(0, 0)
            for b in range(B):
                if b + 1 < B:
                    high_part(b + 1, b + 1)
                project_out(b)
            act.wait_ge(v_ready, B)
            for i in range(B):
                act.wait_ge(sim_ready, i + 1)
                act.activation(sim[:, TB * i:TB * i + TB, :], ps[3 + i][:].rearrange("p (t s) -> p t s", t=TB), ACT.Copy,
                               scale=1.0 / 16).then_inc(sim_out, 1)

            def oT_high(b):
                act.wait_ge(oT_ready, b + 1)
                act.activation(flat(oh[:]), ps[5][:], ACT.Copy).then_inc(oh_ready, 1)

            def attention(b, with_epilogue):
                for h in range(H0 + 2):
                    n = b * H0 + h
                    if h < H0:
                        if h == 0:
                            wait_past(act, o_out, b)
                        act.wait_ge(max_ready, n + 1)
                        act.activation(pr[:, h % 4, 0:P], pr[:, h % 4, 0:P], ACT.Exp, scale=-1.0,
                                       bias=nmax[:, h % 4, 0:1], accum_out=psums[:, 0, h:h + 1])
                        act.activation(pr[:, h % 4, P:3 * P], pr[:, h % 4, P:3 * P], ACT.Exp, scale=-1.0,
                                       bias=nmax[:, h % 4, 1:2], accum_out=psums[:, 1, h:h + 1]).then_inc(p_ready, 1)
                    if h >= 2:
                        act.wait_ge(pT_ready, n - 1)
                        wait_past(act, pv_ready, n - 3)
                        act.activation(prT[:, h % 2, :], ps[2 + h % 2][:, 0:3 * P], ACT.Copy).then_inc(pT_out, 1)
                    if h == 3 and with_epilogue:
                        oT_high(b - 1)
                    if h == 8:
                        wait_past(act, adj_ready, b)
                        act.activation(tanh_sim[:], sim[:, ds(b * TB, TB), :], ACT.Tanh, scale=0.5).then_inc(tanh_ready, 1)

            for b in range(B):
                attention(b, b > 0)
            oT_high(B - 1)

            for b in range(B):
                high_part(B + b, b)
            act.wait_ge(top_ready, 1)
            act.activation(score[:], toplg[:], ACT.Sigmoid).then_inc(score_ready, 1)
            act.wait_ge(score_ready, 1)
            for t in range(T):
                act.activation(xn[:, t, :], xn[:, t, :], ACT.Copy, scale=score[:, t:t + 1]).then_inc(xs_ready, 1)

            def shared_gate(i):
                act.wait_ge(sgu_ready, i + 1)
                wait_past(act, sh_ready, i - 1)
                act.activation(gate[:, i % 2, :], ps[1 + 2 * (i % 2)][:], ACT.Silu).then_inc(sgate_ready, 1)

            for i in range(FB):
                shared_gate(i)

            def turned_rows(j):
                act.wait_ge(xg_turned, j + 1)
                wait_past(act, gu_done, j - 1)
                act.activation(xgT[:, j % 2].rearrange("p k r -> p (k r)"), ps[0][:, 0:E], ACT.Copy).then_inc(xgT_out, 1)

            def routed_gate(j):
                act.wait_ge(gu_done, j + 1)
                wait_past(act, rh_ready, j)
                act.activation(rgate[:], ps[1][:], ACT.Silu).then_inc(rgate_ready, 1)

            def turned_hidden(j):
                act.wait_ge(rh_turned, j + 1)
                wait_past(act, y_ready, j)
                act.activation(flat(rhT[:]), ps[3][:], ACT.Copy).then_inc(rhT_out, 1)

            turned_rows(0)
            for j in range(NSLOT):
                if j + 1 < NSLOT:
                    turned_rows(j + 1)
                routed_gate(j)
                turned_hidden(j)
            for i in range(FB, 2 * FB):
                shared_gate(i)
            act.wait_ge(slopes_negated, 1)
            act.wait_ge(distance_ready, 1)
            for h in range(H1):
                act.activation(decay[:, h, :], distance[:], ACT.Exp, scale=slopes[:, h:h + 1]).then_inc(powers_ready, 1)
            for b in range(B):
                high_part(2 * B + b, b)

            def evacuate(h, i, what):
                pair_a, pair_b = banks[:, 0:2, :], banks[:, 2:4, :]
                if what == "q":
                    act.wait_ge(qd_ready, h + 1)
                    wait_past(act, scores_ready, 2 * h - 2)
                    act.activation(qd[:, i].rearrange("p (c n) -> p c n", c=2), pair_a, ACT.Silu).then_inc(qd_out, 1)
                elif what == "k":
                    act.wait_ge(kd_ready, h + 1)
                    wait_past(act, scores_ready, 2 * h - 2)
                    act.activation(kd[:, i].rearrange("p (c n) -> p c n", c=2), pair_b, ACT.Silu).then_inc(kd_out, 1)
                elif what == "v":
                    act.wait_ge(vd_ready, h + 1)
                    wait_past(act, head_ready, 2 * h - 2)
                    act.activation(vd[:, i].rearrange("p (c t) d -> p c (t d)", c=2), pair_a, ACT.Silu).then_inc(vd_out, 1)
                else:
                    act.wait_ge(gd_ready, h + 1)
                    wait_past(act, head_out, 2 * h - 2)
                    act.activation(gd[:, i].rearrange("p (c n) -> p c n", c=2), pair_b, ACT.Tanh, scale=0.5).then_inc(gd_out, 1)

            def square(h, p):
                act.wait_ge(head_out, 2 * h + p + 1)
                wait_past(act, square_added, 2 * h + p - 1)
                act.activation(squares[:, p, :], ps[6 + p][:], ACT.Square).then_inc(squared, 1)

            def unit(h, i):
                evacuate(h + 1, 1 - i, "q")
                evacuate(h + 1, 1 - i, "k")
                square(h, 0)
                evacuate(h + 1, 1 - i, "v")
                square(h, 1)
                evacuate(h + 1, 1 - i, "g")

            for what in "qkvg":
                evacuate(0, 0, what)
            unit(0, 0)
            unit(1, 1)
            with act.Fori(2, H1 - 2, 2) as h:
                unit(h, 0)
                unit(h + 1, 1)
            unit(H1 - 2, 0)
            square(H1 - 1, 0)
            square(H1 - 1, 1)
            act.wait_ge(si_out, 1)
            for t in range(T):
                act.wait_ge(pair_ready, 3 + 2 * (t // (2 * TB)))
                act.activation(pair[:, t, :], ps[4 + t // (2 * TB)][:, (t // TB % 2) * S:(t // TB % 2 + 1) * S], ACT.Sigmoid,
                               bias=si[:, t:t + 1]).then_inc(pair_out, 1)
            for b in range(B):
                high_part(3 * B + b, b)
            act.wait_ge(facol_in, 32)
            for b in range(B):
                act.wait_ge(up_ready, 2 * b + 1)
                wait_past(act, f_ready, 2 * b - 3)
                for m in range(FB):
                    last = act.activation(f0[:, b % 2, m, :], ps[m // 2][:, (m % 2) * S:(m % 2 + 1) * S], ACT.Gelu,
                                          bias=facol[:, m:m + 1])
                last.then_inc(f0_out, 1)

        @block.tensor
        def _(pe):
            def product3(dst, lh, ll, rh, rl, first, last):
                pe.matmul(dst, lh, rh, start=first, stop=False)
                pe.matmul(dst, lh, rl, start=False, stop=False)
                return pe.matmul(dst, ll, rh, start=False, stop=last)

            def transpose_norm(n, b):
                pe.wait_ge(xn_ready, TB * (n + 1))
                wait_past(pe, xl_ready, n)
                for k in range(K):
                    for t in range(TB):
                        last = pe.transpose(ps[7][:, (k * TB + t) * P:(k * TB + t + 1) * P],
                                            xn[:, TB * b + t, k * P:(k + 1) * P], ident[:])
                last.then_inc(xT_ready, 1)

            pe.wait_ge(consts, 1)
            pe.wait_ge(ctx_in, 32)
            for i in range(4):
                pe.matmul(ps[3 + i][0:C, :], xw[:, i // 2, :], ctxT[:, (i % 2) * 512:(i % 2) * 512 + 512],
                          start=True, stop=True).then_inc(ctx_qk, 1)

            def project(b):
                pe.wait_ge(xl_ready, b + 1)
                cols = slice(b * S, (b + 1) * S)
                for w, bank, s_ready_, s_free in ((0, 0, q_ready, q_out), (1, 1, k_ready, k_out)):
                    pe.wait_ge(aw_split, w + 1)
                    wait_past(pe, s_free, b)
                    for m in range(K):
                        mc = slice(m * P, (m + 1) * P)
                        for k in range(K):
                            last = product3(ps[bank][:, m * S:(m + 1) * S], awh[:, w, k, mc], awl[:, w, k, mc],
                                            xh[:, k, cols], xl[:, k, cols], k == 0, k == K - 1)
                    last.then_inc(s_ready_, 1)
                pe.wait_ge(aw_split, 3)
                wait_past(pe, v_out, b)
                for t in range(TB):
                    tc = slice(b * S + t * P, b * S + (t + 1) * P)
                    for k in range(K):
                        last = product3(ps[2][:, t * E:(t + 1) * E], xh[:, k, tc], xl[:, k, tc],
                                        awh[:, 2, k, :], awl[:, 2, k, :], k == 0, k == K - 1)
                last.then_inc(v_ready, 1)

            transpose_norm(0, 0)
            for b in range(B):
                if b + 1 < B:
                    transpose_norm(b + 1, b + 1)
                project(b)
            pe.wait_ge(ctx_qk_out, 4)
            for t in range(T):
                mm = pe.matmul(ps[3 + t // TB][:, (t % TB) * S:(t % TB + 1) * S], cQ[:, t * P:(t + 1) * P],
                               cK[:, (t // TB) * S:(t // TB + 1) * S], start=True, stop=True)
                if t % TB == TB - 1:
                    mm.then_inc(sim_ready, 1)

            def heads_transposed(b):
                pe.wait_ge(o_out, b + 1)
                for k in range(K):
                    for t in range(TB):
                        last = pe.transpose(ps[5][:, (k * TB + t) * P:(k * TB + t + 1) * P],
                                            on[:, t, k * P:(k + 1) * P], ident[:])
                last.then_inc(oT_ready, 1)
                pe.wait_ge(adj_ready, b + 1)
                for i in range(TB):
                    for j in range(TB):
                        last = pe.transpose(ps[6][:, (i * TB + j) * P:(i * TB + j + 1) * P],
                                            adj[:, j, i * P:(i + 1) * P], ident[:])
                last.then_inc(adjT_ready, 1)

            def heads_out(b):
                pe.wait_ge(ol_ready, b + 1)
                for t in range(TB):
                    for k in range(K):
                        tc = slice(t * P, (t + 1) * P)
                        last = product3(ps[5][:, t * E:(t + 1) * E], oh[:, k, tc], ol[:, k, tc],
                                        awh[:, 3, k, :], awl[:, 3, k, :], k == 0, k == K - 1)
                last.then_inc(wo_ready, 1)

            def attention(b, with_epilogue):
                for h in range(H0 + 4):
                    n = b * H0 + h
                    if h < H0:
                        pe.wait_ge(qm_ready, n + 1)
                        wait_past(pe, max_ready, n - 1)
                        pe.matmul(ps[h % 2][:, 0:P], qm[:, h % 2, 0:P], kT[:, h // HB, ds(b * S, P)],
                                  start=True, stop=True)
                        pe.matmul(ps[h % 2][:, P:3 * P], qm[:, h % 2, P:2 * P], kT[:, h // HB, ds(b * S, S)],
                                  start=True, stop=True).then_inc(s_ready, 1)
                    if 2 <= h < H0 + 2:
                        pe.wait_ge(p_ready, n - 1)
                        wait_past(pe, pT_out, n - 3)
                        for i in range(3):
                            last = pe.transpose(ps[2 + h % 2][:, i * P:(i + 1) * P], pr[:, (h - 2) % 4, i * P:(i + 1) * P],
                                                ident[:])
                        last.then_inc(pT_ready, 1)
                    if h >= 4:
                        g = h - 4
                        pe.wait_ge(pT_out, n - 3)
                        if g == 0:
                            wait_past(pe, o_out, b)
                        c0 = g * D0
                        pe.matmul(ps[4][:, c0:c0 + D0], prT[:, g % 2, 0:P], v[:, ds(b * TB, 1), c0:c0 + D0],
                                  start=True, stop=True)
                        pe.matmul(ps[4][:, E + c0:E + c0 + D0], prT[:, g % 2, P:2 * P],
                                  v[:, ds(b * TB, 1), c0:c0 + D0], start=True, stop=False)
                        pe.matmul(ps[4][:, E + c0:E + c0 + D0], prT[:, g % 2, 2 * P:3 * P],
                                  v[:, ds(b * TB + 1, 1), c0:c0 + D0], start=False, stop=True).then_inc(pv_ready, 1)
                    if with_epilogue and h == 2:
                        heads_transposed(b - 1)
                    if with_epilogue and h == 6:
                        heads_out(b - 1)

            pe.wait_ge(q_out, B)
            pe.wait_ge(k_out, B)
            pe.wait_ge(v_out, B)
            pe.wait_ge(sim_out, B)
            for b in range(B):
                attention(b, b > 0)
            heads_transposed(B - 1)
            heads_out(B - 1)

            for b in range(B):
                transpose_norm(B + b, b)
            pe.wait_ge(rw_split, 1)
            pe.wait_ge(xl_ready, 2 * B)
            for t in range(T):
                for k in range(K):
                    tc = slice(t * P, (t + 1) * P)
                    last = product3(ps[0][:, t * NEXP:(t + 1) * NEXP], xh[:, k, tc], xl[:, k, tc], rwh[:, k, :], rwl[:, k, :],
                                    k == 0, k == K - 1)
            last.then_inc(logits_ready, 1)

            def shared_up(i):
                half, m = divmod(i, FB)
                cols, mc = slice(half * HALF, (half + 1) * HALF), slice(m * P, (m + 1) * P)
                wait_past(pe, sh_ready, i - 1)
                for bank, hi, lo in ((1, sgh, sgl), (2, suh, sul)):
                    for k in range(K):
                        last = product3(ps[bank + 2 * (i % 2)][:], hi[:, k, mc], lo[:, k, mc], xh[:, k, cols], xl[:, k, cols],
                                        k == 0, k == K - 1)
                last.then_inc(sgu_ready, 1)

            def shared_down(half):
                pe.wait_ge(sd_in, 16)
                pe.wait_ge(sh_ready, FB * (half + 1))
                for b in range(2):
                    wait_past(pe, sdown_added, 2 * half)
                    for t in range(TB):
                        tc = slice((b * TB + t) * P, (b * TB + t + 1) * P)
                        for m in range(FB):
                            last = pe.matmul(ps[5 + b][:, t * E:(t + 1) * E], hT[:, m, tc], sd[:, m, :],
                                             start=(m == 0), stop=(m == FB - 1))
                    last.then_inc(sdown_ready, 1)

            pe.wait_ge(shared_split, 4)
            shared_up(0)
            pe.wait_ge(onehot_ready, 1)
            pe.matmul(ps[0][:, 64:64 + T * NEXP], before[:], flat(onehot[:]), start=True, stop=True)
            pe.matmul(ps[0][:, 128:128 + T * NEXP], ones[:], flat(onehot[:]), start=True, stop=True).then_inc(counts_ready, 1)
            for i in range(1, FB):
                shared_up(i)
            shared_down(0)

            def turn_rows(j):
                pe.wait_ge(xg_in[j % 3], 16 * (j // 3 + 1))
                if j == 0:
                    pe.wait_ge(slot_ready, 1)
                wait_past(pe, xgT_out, j)
                for k in range(K):
                    last = pe.transpose(ps[0][:, k * P:(k + 1) * P], xg[:, j % 3, k * P:(k + 1) * P], ident[:])
                last.then_inc(xg_turned, 1)

            def gate_up(j):
                e = pe.value_load(tile_expert[0:1, j:j + 1], min_val=0, max_val=NEXP - 1)
                pe.wait_ge(xgT_out, j + 1)
                wait_past(pe, rh_ready, j)
                for bank in range(2):
                    for k in range(K):
                        last = pe.matmul(ps[1 + bank][:], xgT[:, j % 2, k, :], gu[:, ds(e, 1), k, bank * FI:(bank + 1) * FI],
                                         start=(k == 0), stop=(k == K - 1))
                last.then_inc(gu_done, 1)
                return e

            def turn_hidden(j):
                pe.wait_ge(rh_ready, j + 1)
                wait_past(pe, rhT_out, j)
                for m in range(FB):
                    last = pe.transpose(ps[3][:, m * P:(m + 1) * P], rh[:, m * P:(m + 1) * P], ident[:])
                last.then_inc(rh_turned, 1)

            def down(j, e):
                pe.wait_ge(rhT_out, j + 1)
                wait_past(pe, y_out, j)
                for m in range(FB):
                    last = pe.matmul(ps[4][:, 0:E], rhT[:, m, :], dn[:, ds(e, 1), m, :], start=(m == 0), stop=(m == FB - 1))
                last.then_inc(y_ready, 1)

            pe.wait_ge(sh_ready, FB)
            pe.wait_ge(tile_ready, 1)
            pe.wait_ge(gu_in, 16 * NEXP)
            pe.wait_ge(dn_in, 16 * NEXP)
            turn_rows(0)
            for j in range(NSLOT):
                if j + 1 < NSLOT:
                    turn_rows(j + 1)
                expert_before = expert if j else None
                expert = gate_up(j)
                if j:
                    down(j - 1, expert_before)
                turn_hidden(j)
            down(NSLOT - 1, expert)
            pe.wait_ge(y_out, NSLOT)
            for i in range(FB, 2 * FB):
                shared_up(i)
            shared_down(1)
            for b in range(B):
                transpose_norm(2 * B + b, b)
            pe.wait_ge(xl_ready, 3 * B)

            def project_head(h, i, what):
                c = "qkvg".index(what) * D1
                if what == "q":
                    pe.wait_ge(w_split, h + 1)
                    wait_past(pe, vd_out, h)
                    dst, s_ = 0, qd_ready
                elif what == "k":
                    wait_past(pe, gd_out, h)
                    dst, s_ = 2, kd_ready
                elif what == "v":
                    pe.wait_ge(qd_out, h + 1)
                    dst, s_ = 0, vd_ready
                else:
                    pe.wait_ge(kd_out, h + 1)
                    dst, s_ = 2, gd_ready
                if what == "v":
                    for t in range(T):
                        tc = slice(t * P, (t + 1) * P)
                        for k in range(K):
                            last = product3(ps[dst + t // 4][:, (t % 4) * D1:(t % 4 + 1) * D1], xh[:, k, tc], xl[:, k, tc],
                                            wh[:, i, k, c:c + D1], wl[:, i, k, c:c + D1], k == 0, k == K - 1)
                else:
                    for half in range(2):
                        hc = slice(half * HALF, (half + 1) * HALF)
                        for k in range(K):
                            last = product3(ps[dst + half][:], wh[:, i, k, c:c + D1], wl[:, i, k, c:c + D1],
                                            xh[:, k, hc], xl[:, k, hc], k == 0, k == K - 1)
                last.then_inc(s_, 1)

            def score_pair(h, i, p):
                if p == 0:
                    pe.wait_ge(kd_out, h + 1)
                wait_past(pe, masked_ready, 2 * h + p)
                for j in range(2):
                    c0 = (2 * p + j) * S
                    pe.matmul(ps[4 + j][:, 0:S], kd[:, i, c0:c0 + P], qd[:, i, c0:c0 + S], start=True, stop=True)
                    last = pe.matmul(ps[4 + j][:, S:S + P], kd[:, i, c0 + P:c0 + S], qd[:, i, c0 + P:c0 + S],
                                     start=True, stop=True)
                last.then_inc(scores_ready, 1)

            def head_pair(h, i, p):
                pe.wait_ge(masked_ready, 2 * h + p + 1)
                if p == 0:
                    pe.wait_ge(vd_out, h + 1)
                wait_past(pe, squared, 2 * h + p - 1)
                for j in range(2):
                    t = (2 * p + j) * TB
                    pe.matmul(ps[6 + p][:, j * S:(j + 1) * S], vd[:, i, t, :], masked[:, p, j, 0:S], start=True, stop=False)
                    last = pe.matmul(ps[6 + p][:, j * S + P:(j + 1) * S], vd[:, i, t + 1, :], masked[:, p, j, S:S + P],
                                     start=False, stop=True)
                last.then_inc(head_ready, 1)

            def unit(h, i):
                project_head(h + 1, 1 - i, "q")
                score_pair(h, i, 0)
                project_head(h + 1, 1 - i, "k")
                score_pair(h, i, 1)
                head_pair(h, i, 0)
                project_head(h + 1, 1 - i, "v")
                head_pair(h, i, 1)
                project_head(h + 1, 1 - i, "g")

            for what in "qkvg":
                project_head(0, 0, what)
            unit(0, 0)
            unit(1, 1)
            with pe.Fori(2, H1 - 2, 2) as h:
                unit(h, 0)
                unit(h + 1, 1)
            unit(H1 - 2, 0)
            score_pair(H1 - 1, 1, 0)
            score_pair(H1 - 1, 1, 1)
            head_pair(H1 - 1, 1, 0)
            head_pair(H1 - 1, 1, 1)
            pe.wait_ge(wo_scaled, 1)
            pe.wait_ge(head_out, 2 * H1)
            pe.wait_ge(gd_out, H1)

            def project_heads(b):
                wait_past(pe, y1_added, b - 1)
                for t in range(TB):
                    tc = slice((TB * b + t) * P, (TB * b + t + 1) * P)
                    for h in range(H1):
                        last = pe.matmul(ps[b % 2][:, t * E:(t + 1) * E], heads[:, h, tc], wo[:, h, :],
                                         start=(h == 0), stop=(h == H1 - 1))
                last.then_inc(y1_ready, 1)

            project_heads(0)
            pe.wait_ge(square_added, 2 * H1)
            for t in range(T):
                last = pe.matmul(ps[2][:, t:t + 1], flat(square_sum[:])[:, t * P:(t + 1) * P], ones[:, 0:1], start=True, stop=True)
            last.then_inc(ms_ready, 1)
            pe.wait_ge(ex_ready, 1)
            for t in range(T):
                last = pe.matmul(ps[3][:, t:t + 1], ctx2[:, t * P:(t + 1) * P], ex[:, 0:1], start=True, stop=True)
            last.then_inc(pair_ready, 1)
            for b in range(B):
                pe.matmul(ps[4 + b // 2][:, (b % 2) * S:(b % 2 + 1) * S], wj[:], ctx2[:, b * S:(b + 1) * S],
                          start=True, stop=True).then_inc(pair_ready, 1)
            for b in range(1, B):
                project_heads(b)
                if b >= 1:
                    transpose_norm(3 * B + b - 1, b - 1)
            transpose_norm(4 * B - 1, B - 1)
            pe.wait_ge(xl_ready, 4 * B)
            pe.wait_ge(y1_added, B)
            pe.wait_ge(pair_out, T)
            pe.wait_ge(fa_split, 2)
            pe.wait_ge(fg_split, 1)
            pe.wait_ge(fb_in, 32)

            def choice_logits(b):
                wait_past(pe, choice_step, 3 * b)
                for t in range(TB):
                    tc = slice((TB * b + t) * P, (TB * b + t + 1) * P)
                    for k in range(K):
                        product3(ps[7][:, 2 * t:2 * t + 2], xh[:, k, tc], xl[:, k, tc], fgh[:, k, :], fgl[:, k, :],
                                 k == 0, k == K - 1)

            def up(b):
                cols = slice(b * S, (b + 1) * S)
                for i, s_free in enumerate((f0_out, f1_out)):
                    wait_past(pe, s_free, b)
                    for m in range(FB):
                        mc = slice(m * P, (m + 1) * P)
                        for k in range(K):
                            last = product3(ps[4 * i + m // 2][:, (m % 2) * S:(m % 2 + 1) * S], fah[:, i, k, mc],
                                            fal[:, i, k, mc], xh[:, k, cols], xl[:, k, cols], k == 0, k == K - 1)
                    last.then_inc(up_ready, 1)

            def down_experts(b):
                for i, (f, s_out) in enumerate(((f0, f0_out), (f1, f1_out))):
                    pe.wait_ge(s_out, b + 1)
                    wait_past(pe, x_final, b)
                    for t in range(TB):
                        tc = slice(t * P, (t + 1) * P)
                        for m in range(FB):
                            last = pe.matmul(ps[2 + i][:, t * E:(t + 1) * E], f[:, b % 2, m, tc], fb[:, i, m, :],
                                             start=(m == 0), stop=(m == FB - 1))
                    last.then_inc(f_ready, 1)

            for b in range(B):
                choice_logits(b)
                up(b)
                if b:
                    down_experts(b - 1)
            down_experts(B - 1)


def kernel(**inputs):
    import numpy as np
    import concourse.bacc as bacc
    from concourse.bass_utils import run_bass_kernel_spmd

    g = {k: np.asarray(v) for k, v in inputs.items()}
    ca = np.ascontiguousarray

    def cols(v):
        return v.reshape(-1, P).T

    w = g["L1_attn_w_qkv"].reshape(H1, 3, D1, E)
    wg = g["L1_attn_w_gate"].reshape(H1, 1, D1, E)
    heads = np.concatenate([w, wg], axis=1)
    arrays = {
        "x": g["x"],
        "ctxT": g["ctx_512"].reshape(B * S, C).T,
        "aw": np.stack([g[f"L0_attn_W{n}"].T for n in "qkvo"]),
        "abcol": np.concatenate([cols(g["L0_attn_bq"]), cols(g["L0_attn_bk"])], axis=1),
        "abrow": np.stack([g["L0_attn_bv"], g["L0_attn_bo"]]),
        "xw": np.stack([g["L0_xattn_Wq"].T, g["L0_xattn_Wk"].T], axis=1),
        "gamma": g["L0_xattn_gamma_raw"].reshape(1, 1),
        "rw": g["L0_ffn_router_w"].T.reshape(K, P, NEXP).transpose(1, 0, 2),
        "gu": g["L0_ffn_gate_up_proj"],
        "dn": g["L0_ffn_down_proj"],
        "sg": g["L0_ffn_shared_gate_w"],
        "su": g["L0_ffn_shared_up_w"],
        "sd": g["L0_ffn_shared_down_w"],
        "slopes": g["L1_attn_slope_rate"].reshape(1, H1),
        "heads": heads.reshape(H1, 4 * D1, K, P).transpose(0, 3, 2, 1),
        "nw": cols(g["L1_attn_norm_w"]),
        "wo": g["L1_attn_w_out"].T.reshape(H1, D1, E).transpose(1, 0, 2),
        "ex": g["L1_xattn_W"].reshape(2, C).T,
        "eb": g["L1_xattn_b"].reshape(1, 1),
        "fg": g["L1_ffn_Wg"].T.reshape(K, P, 2).transpose(1, 0, 2),
        "fa": np.stack([g["L1_ffn_W0a"].T, g["L1_ffn_W1a"].T]),
        "fb": np.stack([g["L1_ffn_W0b"].T, g["L1_ffn_W1b"].T]),
        "facol": np.concatenate([cols(g["L1_ffn_b0a"]), cols(g["L1_ffn_b1a"])], axis=1),
        "fbrow": np.stack([g["L1_ffn_b0b"], g["L1_ffn_b1b"]]),
    }
    nc = bacc.Bacc("TRN2", target_bir_lowering=False, num_devices=1)
    arrays = {f"in_{k}": ca(v) for k, v in arrays.items()}
    aps = {k[3:]: nc.dram_tensor(k, v.shape, mybir.dt.from_np(v.dtype), kind="ExternalInput").ap()
           for k, v in arrays.items()}
    out = nc.dram_tensor("out", (B, S, E), F32, kind="ExternalOutput").ap()
    sorted_in = nc.dram_tensor("sorted_in", (NSLOT * P, E), F32).ap()
    sorted_out = nc.dram_tensor("sorted_out", (NSLOT * P, E), F32).ap()
    decoder(nc, aps, sorted_in, sorted_out, out)
    return run_bass_kernel_spmd(nc, [arrays], core_ids=[0]).results[0]["out"]
```

```python
from contextlib import ExitStack

import concourse.bass as bass
from concourse import mybir
from concourse.alu_op_type import AluOpType as ALU

ACT = mybir.ActivationFunctionType
F32 = mybir.dt.float32
F32R = mybir.dt.float32r
U32 = mybir.dt.uint32
I32 = mybir.dt.int32
X = mybir.AxisListType.X

P = 128
B, S, E = 4, 256, 256
T = B * S // P
TB = S // P
K = E // P
H0, D0 = 16, 16
HB = P // D0
C = 64
TOPK = int(S * 0.3)
NEXP, FI = 8, 512
FB = FI // P
NSLOT = T + NEXP - 1
HALF = B * S // 2
H1, D1 = 16, 128
BIG = 1e30
EPS = 1e-5
ds = bass.ds


class Chain:

    def __init__(self, eng, sem, base=0):
        self.eng, self.sem, self.base, self.n = eng, sem, base, 0

    def __call__(self, ins):
        ins.then_inc(self.sem, 1)
        self.n += 1
        self.eng.wait_ge(self.sem, self.base + self.n)


def wait_past(eng, sem, value):
    if not isinstance(value, int) or value > 0:
        eng.wait_ge(sem, value)


def decoder(nc, a, sorted_in, sorted_out, out):
    ctx = ExitStack()
    with ctx:
        base = -(-nc.sbuf_base // 64) * 64
        cursor = [base]

        def sb(name, shape, dt=F32):
            n = 4
            for s in shape[1:]:
                n *= s
            at = cursor[0]
            cursor[0] = at + -(-n // 64) * 64
            assert cursor[0] <= nc.sbuf_usable_end, (name, cursor[0] - nc.sbuf_usable_end)
            return nc.alloc_sbuf_tensor_at(name, shape, dt, offset=at)

        def sem(name):
            return ctx.enter_context(nc.semaphore(name))

        banks = ctx.enter_context(nc.psum_tensor("banks", [P, 8, 512], F32))
        ps = [banks[:, i, :] for i in range(8)]

        x = sb("x", [P, T, E])
        at_xn = cursor[0]
        xn = sb("xn", [P, T, E])
        at_xh = cursor[0]
        xh = sb("xh", [P, K, B * S], F32R)
        at_xl = cursor[0]
        xl = sb("xl", [P, K, B * S], F32R)
        ident = sb("ident", [P, P])
        before = sb("before", [P, P])
        ones = sb("ones", [P, P])
        headmask = sb("headmask", [P, HB])
        mhalf = sb("mhalf", [P, TB])
        stats = sb("stats", [P, 2, TB, 6])
        mv = sb("mv", [P, 2, TB, 2])
        ve = sb("ve", [P, 2, TB])
        rstd = sb("rstd", [P, 2, TB])
        bcol = sb("bcol", [P, 4])
        gam = sb("gam", [P, 4])
        zero_row = sb("zero_row", [P, E])
        top8 = sb("top8", [P, T, 8])
        nmax = sb("nmax", [P, 4, 2])
        psums = sb("psums", [P, TB, H0])
        prec = sb("prec", [P, TB, H0])
        small_end = cursor[0] + 4096
        cursor[0] = small_end

        at_g = cursor[0]
        gu = sb("gu", [P, NEXP, K, 2 * FI])
        at_gu_tail = cursor[0] - 3 * K * 2 * FI * 4
        at_r = cursor[0]

        at_s = cursor[0]
        sgh, sgl, suh, sul = (sb(n, [P, K, FI], F32R) for n in ("sgh", "sgl", "suh", "sul"))
        at_c = cursor[0]
        qT = sb("qT", [P, K, B * S])
        kT = sb("kT", [P, K, B * S])
        v = sb("v", [P, T, E])
        awh = sb("awh", [P, 4, K, E], F32R)
        awl = sb("awl", [P, 4, K, E], F32R)
        alibi = sb("alibi", [P, H0, S])
        at_raw = cursor[0]
        aw = sb("aw", [P, 4, K, E])
        cursor[0] = at_raw
        on = sb("on", [P, TB, E])
        oh = sb("oh", [P, K, S], F32R)
        ol = sb("ol", [P, K, S], F32R)
        adj = sb("adj", [P, TB, S])
        qm = sb("qm", [P, 2, S])
        pr = sb("pr", [P, 4, 3 * P])
        prT = sb("prT", [P, 2, 3 * P])
        work = sb("work", [P, TB, S])
        tanh_sim = sb("tanh_sim", [P, TB, S])
        mask = sb("mask", [P, TB, S])
        span = mask[:, 0, :]
        adj_sum = sb("adj_sum", [P, TB, S])
        brow = sb("brow", [P, 2, E])
        cursor[0] = at_gu_tail
        sim = sb("sim", [P, T, S])
        ctxT = sb("ctxT", [C, B * S])
        xw = sb("xw", [C, 2, C])
        cQ = sb("cQ", [C, B * S])
        cK = sb("cK", [C, B * S])
        cursor[0] = at_xh
        shared_raw = sb("shared_raw", [P, 2, K, FI])


        cursor[0] = at_c
        head_raw = sb("head_raw", [P, 2, K, 3 * D1])
        v_raw = sb("v_raw", [P, K, 2 * D1])
        dn = sb("dn", [P, NEXP, FB, E])
        sd = sb("sd", [P, FB, E])
        hT = sb("hT", [P, FB, HALF])
        gate = sb("gate", [P, 2, HALF])
        xg = sb("xg", [P, 3, E])
        xgT = sb("xgT", [P, 2, K, P])
        rgate = sb("rgate", [P, 2, FI])
        rh = sb("rh", [P, 2, FI])
        rhT = sb("rhT", [P, 2, FB, P])
        yb = sb("yb", [P, 2, E])
        yg = sb("yg", [P, T, E])
        rw = sb("rw", [P, K, NEXP])
        rwh = sb("rwh", [P, K, NEXP], F32R)
        rwl = sb("rwl", [P, K, NEXP], F32R)
        lg = sb("lg", [P, T, NEXP])
        hit = sb("hit", [P, T, NEXP])
        toplg = sb("toplg", [P, T])
        score = sb("score", [P, T])
        which = sb("which", [P, T])
        onehot = sb("onehot", [P, NEXP, T])
        upto = sb("upto", [P, NEXP, T])
        place = sb("place", [P, NEXP, T])
        ntiles = sb("ntiles", [P, NEXP])
        ends = sb("ends", [P, NEXP])
        starts = sb("starts", [P, NEXP])
        slotf = sb("slotf", [P, T])
        slot = sb("slot", [P, T], U32)
        cmp = sb("cmp", [P, NEXP, T])
        cmp2 = sb("cmp2", [1, NSLOT + 1, NEXP])
        tilef = sb("tilef", [1, NSLOT + 1])
        tile_expert = sb("tile_expert", [1, NSLOT + 1], I32)
        end_c = cursor[0]

        cursor[0] = at_s
        wh = sb("wh", [P, 2, K, 3 * D1], F32R)
        wl = sb("wl", [P, 2, K, 3 * D1], F32R)
        vh = sb("vh", [P, K, 2 * D1], F32R)
        vl = sb("vl", [P, K, 2 * D1], F32R)
        cursor[0] = at_g
        heads = sb("heads", [P, H1, B * S])
        cursor[0] = at_c + K * 8 * D1 * 4
        decay = sb("decay", [P, H1, S + P])
        masked = sb("masked", [P, 2, TB, S + P])
        at_q = cursor[0]
        qd = sb("qd", [P, 2, B * S])
        kd = sb("kd", [P, 2, B * S])
        vd = sb("vd", [P, T, 2 * D1])
        gd = sb("gd", [P, 2, B * S])
        wo = sb("wo", [P, H1, E])
        distance = sb("distance", [P, S + P])
        cursor[0] = at_xn
        squares = sb("squares", [P, 2, HALF])
        square_sum = sb("square_sum", [P, 2, HALF])
        cursor[0] = at_q
        fa = sb("fa", [P, 2, K, FI])
        fah = sb("fah", [P, 2, K, FI], F32R)
        fal = sb("fal", [P, 2, K, FI], F32R)
        fbrow = sb("fbrow", [P, 2, E])
        fg = sb("fg", [P, K, 2])
        fgh = sb("fgh", [P, K, 2], F32R)
        fgl = sb("fgl", [P, K, 2], F32R)
        facol = sb("facol", [P, 2 * FB])
        assert cursor[0] <= at_q + 8 * B * S * 4
        cursor[0] = at_c + K * 8 * D1 * 4
        fb = sb("fb", [P, 2, FB, E])
        pair = sb("pair", [P, T, S])
        ctx2 = sb("ctx2", [C, B * S])
        ex = sb("ex", [C, 2])
        wj = sb("wj", [C, P])
        eb = sb("eb", [P, 1])
        si = sb("si", [P, T])
        assert cursor[0] <= at_q
        cursor[0] = at_g
        f0 = sb("f0", [P, 2, FB, S])
        f1 = sb("f1", [P, 2, FB, S])
        y0 = sb("y0", [P, TB, E])
        y1 = sb("y1", [P, TB, E])
        choice = sb("choice", [P, TB, 2])
        lg2 = sb("lg2", [P, TB, 2])
        cursor[0] = small_end - 2048
        rev = sb("rev", [P, NEXP])
        steps128 = sb("steps128", [P, T])
        notfirst = sb("notfirst", [P, NEXP, T])
        tile_no = sb("tile_no", [1, NSLOT + 1])
        slopes = sb("slopes", [P, H1])
        nw = sb("nw", [P, H1])
        ms = sb("ms", [P, T])
        rms = sb("rms", [P, T])
        rhalf = sb("rhalf", [P, T])

        x_in = [sem(f"x_in{b}") for b in range(B)]
        aw_in = [sem(f"aw_in{w}") for w in range(4)]
        ctx_in, small_in, shared_in = sem("ctx_in"), sem("small_in"), sem("shared_in")
        gu_in = sem("gu_in")
        consts, const_step = sem("consts"), sem("const_step")
        gam_step = sem("gam_step")
        span_ready, awh_ready, shared_hi = sem("span_ready"), sem("awh_ready"), sem("shared_hi")
        alibi_ready, aw_split, shared_split, bo_added = sem("alibi_ready"), sem("aw_split"), sem("shared_split"), sem("bo_added")
        ln_step = sem("ln_step")
        var_ready, rstd_ready, xn_ready = sem("var_ready"), sem("rstd_ready"), sem("xn_ready")
        xT_ready, xh_ready, xl_ready = sem("xT_ready"), sem("xh_ready"), sem("xl_ready")
        ctx_qk, ctx_qk_out, sim_ready, sim_out = sem("ctx_qk"), sem("ctx_qk_out"), sem("sim_ready"), sem("sim_out")
        q_ready, k_ready, v_ready = sem("q_ready"), sem("k_ready"), sem("v_ready")
        q_out, k_out, v_out = sem("q_out"), sem("k_out"), sem("v_out")
        qm_ready, s_ready, max_ready, p_ready = sem("qm_ready"), sem("s_ready"), sem("max_ready"), sem("p_ready")
        pT_ready, pT_out, pv_ready = sem("pT_ready"), sem("pT_out"), sem("pv_ready")
        prec_ready, o_out, oT_ready, oh_ready, ol_ready, wo_ready = (sem(n) for n in ("prec_ready", "o_out", "oT_ready", "oh_ready", "ol_ready", "wo_ready"))
        x_added, epi_step, topk_step, tanh_ready, adj_ready, adjT_ready, adj_summed, mask_step = (
            sem(n) for n in ("x_added", "epi_step", "topk_step", "tanh_ready", "adj_ready", "adjT_ready", "adj_summed", "mask_step"))
        ln3_step = sem("ln3_step")
        rw_in, sd_in, dn_in, zeroed = sem("rw_in"), sem("sd_in"), sem("dn_in"), sem("zeroed")
        rw_split, logits_ready, route_step, top_ready, score_ready = (sem(n) for n in ("rw_split", "logits_ready", "route_step", "top_ready", "score_ready"))
        xs_ready, onehot_ready, counts_ready, slot_ready, tile_ready = (sem(n) for n in ("xs_ready", "onehot_ready", "counts_ready", "slot_ready", "tile_ready"))
        sgu_ready, sgate_ready, sh_ready, sdown_ready, sdown_added = (sem(n) for n in ("sgu_ready", "sgate_ready", "sh_ready", "sdown_ready", "sdown_added"))
        scattered = sem("scattered")
        xg_in = [sem(f"xg_in{i}") for i in range(3)]
        y_stored = [sem(f"y_stored{i}") for i in range(2)]
        yg_in = [sem(f"yg_in{b}") for b in range(B)]
        xg_turned, xgT_out, gu_done, rgate_ready, rh_ready, rh_turned, rhT_out, y_ready, y_out = (
            sem(n) for n in ("xg_turned", "xgT_out", "gu_done", "rgate_ready", "rh_ready", "rh_turned", "rhT_out", "y_ready", "y_out"))
        yg_added = sem("yg_added")
        head_in = [sem(f"head_in{i}") for i in range(2)]
        slopes_in, nw_in, wo_in, late_in, fb_in = sem("slopes_in"), sem("nw_in"), sem("wo_in"), sem("late_in"), sem("fb_in")
        whi_ready, vhi_ready, v_split = sem("whi_ready"), sem("vhi_ready"), sem("v_split")
        v_in = sem("v_in")
        w_split, distance_ready, slopes_negated, powers_ready, decay_ready = (
            sem(n) for n in ("w_split", "distance_ready", "slopes_negated", "powers_ready", "decay_ready"))
        qd_ready, kd_ready, vd_ready, gd_ready = sem("qd_ready"), sem("kd_ready"), sem("vd_ready"), sem("gd_ready")
        qd_out, kd_out, vd_out, gd_out = sem("qd_out"), sem("kd_out"), sem("vd_out"), sem("gd_out")
        scores_ready, masked_ready, head_ready, head_out, squared, square_added = (
            sem(n) for n in ("scores_ready", "masked_ready", "head_ready", "head_out", "squared", "square_added"))
        squares_cleared, wo_scaled, ms_ready, rms_step, rms_ready, y1_ready, y1_added = (
            sem(n) for n in ("squares_cleared", "wo_scaled", "ms_ready", "rms_step", "rms_ready", "y1_ready", "y1_added"))
        ex_ready, pair_ready, si_out, pair_out, fa_split, fg_split = (
            sem(n) for n in ("ex_ready", "pair_ready", "si_out", "pair_out", "fa_split", "fg_split"))
        fa_in = [sem(f"fa_in{i}") for i in range(2)]
        fg_in, facol_in = sem("fg_in"), sem("facol_in")
        ln45_step = sem("ln45_step")
        up_ready, f0_out, f1_out, f_ready, f_step, choice_step, x_final = (
            sem(n) for n in ("up_ready", "f0_out", "f1_out", "f_ready", "f_step", "choice_step", "x_final"))
        done, out_done = sem("done"), sem("out_done")

        ROUNDS = -(-TOPK // 8)
        TOPK_LINKS = TB * (2 * ROUNDS - 1)
        TOPK_DONE = (10, 20, 27, 34, 40)
        EPI_LINKS = 9

        SLOPES = [2.0 ** (-0.5 * (i + 1)) for i in range(H0)]

        block = ctx.enter_context(nc.Block())

        def flat(ap):
            return ap.rearrange("p a b -> p (a b)")

        @block.sync
        def _(sp):
            xv = a["x"].rearrange("b (t p) e -> b p t e", p=P)
            sp.dma_start(ctxT[:], a["ctxT"]).then_inc(ctx_in, 16)
            sp.dma_start(xw[:], a["xw"]).then_inc(ctx_in, 16)
            for b in range(B):
                sp.dma_start(x[:, TB * b:TB * b + TB, :], xv[b]).then_inc(x_in[b], 16)
            for w in range(4):
                sp.dma_start(aw[:, w, :, :], a["aw"][w].rearrange("(k p) n -> p k n", p=P)).then_inc(aw_in[w], 16)
            sp.dma_start(bcol[:], a["abcol"]).then_inc(small_in, 16)
            sp.dma_start(brow[:], a["abrow"].rearrange("(o r) n -> o r n", o=1).broadcast_to([P, 2, E])).then_inc(small_in, 16)
            sp.dma_start(gam[:, 0:1], a["gamma"].broadcast_to([P, 1])).then_inc(small_in, 16)
            for e in range(NEXP - 3):
                sp.dma_start(gu[:, e], a["gu"][e].rearrange("(k p) n -> p k n", p=P)).then_inc(gu_in, 16)
            sp.wait_ge(sim_ready, B)
            for e in range(NEXP - 2, NEXP):
                sp.dma_start(gu[:, e], a["gu"][e].rearrange("(k p) n -> p k n", p=P)).then_inc(gu_in, 16)
            sp.wait_ge(v_ready, B)
            sp.dma_start(shared_raw[:, 0], a["sg"].rearrange("(k p) n -> p k n", p=P)).then_inc(shared_in, 16)
            sp.dma_start(shared_raw[:, 1], a["su"].rearrange("(k p) n -> p k n", p=P)).then_inc(shared_in, 16)
            sp.wait_ge(consts, 1)
            for j in range(NSLOT):
                sp.dma_start(sorted_in[j * P:(j + 1) * P, :], zero_row[:]).then_inc(zeroed, 16)
            sp.wait_ge(wo_ready, B)
            sp.wait_ge(adj_summed, B)
            sp.dma_start(gu[:, NEXP - 3], a["gu"][NEXP - 3].rearrange("(k p) n -> p k n", p=P)).then_inc(gu_in, 16)
            sp.dma_start(rw[:], a["rw"]).then_inc(rw_in, 16)
            sp.dma_start(sd[:], a["sd"].rearrange("(f p) n -> p f n", p=P)).then_inc(sd_in, 16)
            for e in range(NEXP):
                sp.dma_start(dn[:, e], a["dn"][e].rearrange("(f p) n -> p f n", p=P)).then_inc(dn_in, 16)

            def load_tile(j):
                wait_past(sp, xg_turned, j - 2)
                sp.dma_start(xg[:, j % 3, :], sorted_in[j * P:(j + 1) * P, :]).then_inc(xg_in[j % 3], 16)

            sp.wait_ge(scattered, 16 * T)
            for j in range(3):
                load_tile(j)
            for j in range(NSLOT):
                if j + 3 < NSLOT:
                    load_tile(j + 3)
                sp.wait_ge(y_out, j + 1)
                sp.dma_start(sorted_out[j * P:(j + 1) * P, :], yb[:, j % 2, :]).then_inc(y_stored[j % 2], 16)
            sp.dma_start(slopes[:], a["slopes"].broadcast_to([P, H1])).then_inc(slopes_in, 16)
            sp.dma_start(nw[:], a["nw"]).then_inc(nw_in, 16)

            def load_head(h, i):
                if not isinstance(h, int) or h >= 2:
                    sp.wait_ge(w_split, h - 1)
                sp.dma_start(head_raw[:, i], a["heads"][ds(h, 1)].rearrange("o p k n -> p (o k) n")).then_inc(head_in[i], 16)

            def load_v(h):
                if not isinstance(h, int) or h >= 2:
                    sp.wait_ge(v_split, h)
                pair_no = h // 2
                sp.dma_start(v_raw[:], a["vpairs"][ds(pair_no, 1)].rearrange("o p k n -> p (o k) n")).then_inc(v_in, 16)

            load_head(0, 0)
            load_v(0)
            load_head(1, 1)
            sp.wait_ge(yg_added, B)
            sp.wait_ge(xl_ready, 3 * B)
            sp.dma_start(wo[:], a["wo"]).then_inc(wo_in, 16)
            with sp.Fori(2, H1 - 1, 2) as h:
                load_head(h, 0)
                load_v(h)
                load_head(h + 1, 1)
            sp.wait_ge(masked_ready, 2 * H1)
            sp.dma_start(ex[:], a["ex"]).then_inc(late_in, 16)
            sp.dma_start(eb[:], a["eb"].broadcast_to([P, 1])).then_inc(late_in, 16)
            sp.dma_start(ctx2[:], a["ctxT"]).then_inc(late_in, 16)
            sp.dma_start(fb[:, 0], a["fb"][0].rearrange("(f p) n -> p f n", p=P)).then_inc(fb_in, 16)
            sp.dma_start(fb[:, 1], a["fb"][1].rearrange("(f p) n -> p f n", p=P)).then_inc(fb_in, 16)
            sp.wait_ge(head_ready, 2 * H1)
            sp.wait_ge(head_out, 2 * H1)
            for i in range(2):
                sp.dma_start(fa[:, i], a["fa"][i].rearrange("(k p) n -> p k n", p=P)).then_inc(fa_in[i], 16)
            sp.dma_start(fg[:], a["fg"]).then_inc(fg_in, 16)
            sp.dma_start(facol[:], a["facol"]).then_inc(facol_in, 16)
            sp.dma_start(fbrow[:], a["fbrow"].rearrange("(o r) n -> o r n", o=1).broadcast_to([P, 2, E])).then_inc(facol_in, 16)
            ov = out.rearrange("b (t p) e -> b p t e", p=P)
            for b in range(B):
                sp.wait_ge(x_final, b + 1)
                sp.dma_start(ov[b], x[:, TB * b:TB * b + TB, :]).then_inc(out_done, 16)
            sp.wait_ge(out_done, 16 * B)

        @block.gpsimd
        def _(pool):
            step = Chain(pool, const_step)
            step(pool.memset(ones[:], 1.0))
            pool.memset(mhalf[:], -0.5)
            pool.memset(zero_row[:], 0.0)
            pool.affine_select(ident[:], ones[:], [[-1, P]], ALU.is_equal, 0.0, base=0, channel_multiplier=1)
            step(pool.memset(headmask[:], -1.0 / D0 ** 0.5))
            step(pool.affine_select(headmask[:], headmask[:], [[-D0, HB]], ALU.is_ge, 0.0, base=0, channel_multiplier=1))
            pool.affine_select(headmask[:], headmask[:], [[D0, HB]], ALU.is_ge, 0.0, base=D0 - 1, channel_multiplier=-1)
            pool.iota(rev[:], [[-1, NEXP]], base=NEXP, channel_multiplier=0, allow_small_or_imprecise_dtypes=True)
            pool.iota(steps128[:], [[P, T]], base=0, channel_multiplier=0, allow_small_or_imprecise_dtypes=True)
            pool.iota(tile_no[:], [[1, NSLOT + 1]], base=0, channel_multiplier=0, allow_small_or_imprecise_dtypes=True)
            step(pool.memset(notfirst[:], 1.0))
            pool.memset(notfirst[:, :, 0:1], 0.0)
            pool.affine_select(before[:], ones[:], [[1, P]], ALU.is_gt, 0.0, base=0, channel_multiplier=-1)\
                .then_inc(consts, 1)
            step(pool.iota(span[:], [[-1, S]], base=P, channel_multiplier=1, allow_small_or_imprecise_dtypes=True))
            pool.affine_select(span[:], span[:], [[-1, S]], ALU.is_ge, BIG, base=P, channel_multiplier=1)\
                .then_inc(span_ready, 1)

            def root(n, slot):
                pool.wait_ge(var_ready, n + 1)
                pool.tensor_tensor(rstd[:, slot], ve[:, slot], mhalf[:], ALU.pow).then_inc(rstd_ready, 1)

            root(0, 0)
            root(1, 1)
            root(2, 0)
            root(3, 1)
            for w in range(4):
                pool.wait_ge(awh_ready, w + 1)
                pool.tensor_tensor(awl[:, w], aw[:, w], awh[:, w].bitcast(F32), ALU.subtract).then_inc(aw_split, 1)

            def split_shared(i):
                w, part, k = i // (2 * K), i // K % 2, i % K
                hi, lo = ((sgh, sgl), (suh, sul))[w]
                if part == 0:
                    pool.tensor_tensor(hi[:, k], shared_raw[:, w, k], ones[:, 0:1].broadcast_to([P, FI]), ALU.mult)\
                        .then_inc(shared_hi, 1)
                else:
                    pool.wait_ge(shared_hi, w * K + K)
                    pool.tensor_tensor(lo[:, k], shared_raw[:, w, k], hi[:, k].bitcast(F32), ALU.subtract)\
                        .then_inc(shared_split, 1)

            def attention(b, epilogue):
                pool.wait_ge(q_out, b + 1)
                for h in range(H0):
                    wait_past(pool, s_ready, b * H0 + h - 1)
                    pool.tensor_tensor(qm[:, h % 2, :], qT[:, h // HB, ds(b * S, S)],
                                       headmask[:, h % HB:h % HB + 1].broadcast_to([P, S]), ALU.mult)\
                        .then_inc(qm_ready, 1)
                    if h == 3:
                        pool.wait_ge(small_in, 48)
                        pool.wait_ge(xn_ready, TB * (b + 1))
                        pool.tensor_tensor(x[:, TB * b:TB * b + TB, :], x[:, TB * b:TB * b + TB, :],
                                           brow[:, 1:2, :].broadcast_to([P, TB, E]), ALU.add).then_inc(bo_added, 1)
                    if b == 1 and h == 0:
                        pool.wait_ge(shared_in, 32)
                    if b == 1 and h % 2 == 0:
                        split_shared(h // 2)
                    if epilogue and h == 9:
                        roots_of(b - 1, 0)
                    if epilogue and h == 12:
                        roots_of(b - 1, 1)

            def roots_of(b, n):
                pool.wait_ge(var_ready, b * 2 + B + 1 + n)
                pool.tensor_tensor(rstd[:, 0], ve[:, 0], mhalf[:], ALU.pow).then_inc(rstd_ready, 1)

            attention(0, False)
            for b in range(1, B):
                attention(b, True)
            roots_of(B - 1, 0)
            roots_of(B - 1, 1)
            pool.wait_ge(rw_in, 16)
            step(pool.tensor_copy(rwh[:], rw[:]))
            pool.tensor_tensor(rwl[:], rw[:], rwh[:].bitcast(F32), ALU.subtract).then_inc(rw_split, 1)
            pool.wait_ge(zeroed, 16 * NSLOT)
            pool.wait_ge(slot_ready, 1)
            for t in range(T):
                pool.wait_ge(xs_ready, t + 1)
                pool.indirect_dma_start(out=sorted_in, out_offset=bass.IndirectOffsetOnAxis(ap=slot[:, t:t + 1], axis=0),
                                        in_=xn[:, t, :], in_offset=None).then_inc(scattered, 16)
            for i in range(2):
                pool.wait_ge(y_stored[i], 16 * ((NSLOT + 1 - i) // 2))
            for t in range(T):
                pool.indirect_dma_start(out=yg[:, t, :], out_offset=None, in_=sorted_out,
                                        in_offset=bass.IndirectOffsetOnAxis(ap=slot[:, t:t + 1], axis=0))\
                    .then_inc(yg_in[t // TB], 16)

            pool.wait_ge(y_ready, NSLOT)
            pool.iota(distance[:, 0:S], [[1, S]], base=0, channel_multiplier=-1, allow_small_or_imprecise_dtypes=True)
            step(pool.iota(distance[:, S:S + P], [[1, P]], base=0, channel_multiplier=-1, allow_small_or_imprecise_dtypes=True))
            pool.tensor_scalar(distance[:], distance[:], 0.0, None, ALU.max).then_inc(distance_ready, 1)
            for b in range(B):
                root(3 * B + b, b % 2)

            def split_head(h, i):
                if isinstance(h, int) and h < 2:
                    pool.wait_ge(head_in[i], 16)
                    if h == 0:
                        pool.wait_ge(sdown_ready, B)
                else:
                    pool.wait_ge(head_in[i], 8 * (h - i) + 16)
                    pool.wait_ge(gd_ready, h - 1)
                pool.tensor_tensor(wh[:, i].rearrange("p k n -> p (k n)"), head_raw[:, i].rearrange("p k n -> p (k n)"),
                                   ones[:, 0:1].broadcast_to([P, K * 3 * D1]), ALU.mult).then_inc(whi_ready, 1)
                pool.wait_ge(whi_ready, h + 1)
                pool.tensor_tensor(wl[:, i], head_raw[:, i], wh[:, i].bitcast(F32), ALU.subtract).then_inc(w_split, 1)

            def split_v(h):
                pool.wait_ge(v_in, 8 * h + 16)
                if not isinstance(h, int) or h >= 2:
                    pool.wait_ge(vd_ready, h)
                pool.tensor_tensor(vh[:].rearrange("p k n -> p (k n)"), v_raw[:].rearrange("p k n -> p (k n)"),
                                   ones[:, 0:1].broadcast_to([P, K * 2 * D1]), ALU.mult).then_inc(vhi_ready, 2)
                pool.wait_ge(vhi_ready, h + 2)
                pool.tensor_tensor(vl[:], v_raw[:], vh[:].bitcast(F32), ALU.subtract).then_inc(v_split, 2)

            def add_squares(h):
                for half in range(2):
                    pool.wait_ge(squared, 2 * h + half + 1)
                    pool.tensor_tensor(square_sum[:, half], square_sum[:, half], squares[:, half], ALU.add)\
                        .then_inc(square_added, 1)

            split_head(0, 0)
            split_v(0)
            split_head(1, 1)
            pool.wait_ge(powers_ready, H1)
            pool.affine_select(decay[:, :, 0:S], decay[:, :, 0:S], [[0, H1], [1, S]], ALU.is_ge, 0.0, base=0, channel_multiplier=-1)
            pool.affine_select(decay[:, :, S:S + P], decay[:, :, S:S + P], [[0, H1], [1, P]], ALU.is_ge, 0.0, base=0,
                               channel_multiplier=-1).then_inc(decay_ready, 1)
            pool.wait_ge(xl_ready, 3 * B)
            step(pool.memset(square_sum[:], 0.0))
            pool.wait_ge(wo_in, 16)
            pool.wait_ge(nw_in, 16)
            step(pool.tensor_scalar(nw[:], nw[:], 0.5, None, ALU.mult))
            pool.tensor_tensor(wo[:], wo[:], nw[:].unsqueeze(2).broadcast_to([P, H1, E]), ALU.mult).then_inc(wo_scaled, 1)
            split_head(2, 0)
            split_v(2)
            add_squares(0)
            split_head(3, 1)
            add_squares(1)
            with pool.Fori(2, H1 - 2, 2) as h:
                split_head(h + 2, 0)
                split_v(h + 2)
                add_squares(h)
                split_head(h + 3, 1)
                add_squares(h + 1)
            add_squares(H1 - 2)
            add_squares(H1 - 1)
            pool.wait_ge(rms_step, 1)
            pool.memset(rhalf[:], -0.5).then_inc(rms_step, 1)
            pool.wait_ge(rms_step, 2)
            pool.tensor_tensor(rms[:], ms[:], rhalf[:], ALU.pow).then_inc(rms_ready, 1)
            for i in range(2):
                pool.wait_ge(fa_in[i], 16)
                step(pool.tensor_copy(fah[:, i], fa[:, i]))
                pool.tensor_tensor(fal[:, i], fa[:, i], fah[:, i].bitcast(F32), ALU.subtract).then_inc(fa_split, 1)
            for b in range(B):
                root(4 * B + 2 * b, b % 2)
                root(4 * B + 2 * b + 1, b % 2)
                if b == 0:
                    pool.wait_ge(fg_in, 16)
                    step(pool.tensor_copy(fgh[:], fg[:]))
                    pool.tensor_tensor(fgl[:], fg[:], fgh[:].bitcast(F32), ALU.subtract).then_inc(fg_split, 1)

        @block.vector
        def _(dve):
            ln = Chain(dve, ln_step)

            def norm_stats(link, src, slot, n_sem=var_ready):
                for t in range(TB):
                    last = dve.bn_stats(stats[:, slot, t, :], src[t])
                link(last)
                for t in range(TB):
                    last = dve.bn_aggr(mv[:, slot, t, :], stats[:, slot, t, :])
                link(last)
                dve.tensor_scalar(ve[:, slot, :], mv[:, slot, :, 1], EPS, None, ALU.add).then_inc(var_ready, 1)

            def normalise(dst, src, slot):
                for t in range(TB):
                    last = dve.tensor_scalar(dst[t], src[t], mv[:, slot, t, 0:1], rstd[:, slot, t:t + 1],
                                             ALU.subtract, ALU.mult)
                return last

            def tiles(buf, b):
                return [buf[:, TB * b + t, :] for t in range(TB)]

            def low_part(n, b):
                dve.wait_ge(xh_ready, n + 1)
                dve.tensor_tensor(xl[:, :, b * S:(b + 1) * S], ps[7][:].rearrange("p (k s) -> p k s", k=K),
                                  xh[:, :, b * S:(b + 1) * S].bitcast(F32), ALU.subtract).then_inc(xl_ready, 1)

            def topk_round(b, r):
                base = b * TOPK_LINKS + 2 * TB * r
                if r == 0:
                    dve.wait_ge(sim_out, b + 1)
                wait_past(dve, topk_step, base)
                for j in range(TB):
                    left = sim[:, b * TB + j, :] if r == 0 else work[:, j, :]
                    dve.max(top8[:, b * TB + j, :], left).then_inc(topk_step, 1)
                if r < ROUNDS - 1:
                    for j in range(TB):
                        left = sim[:, b * TB + j, :] if r == 0 else work[:, j, :]
                        dve.wait_ge(topk_step, base + 1 + j)
                        dve.match_replace(work[:, j, :], top8[:, b * TB + j, :], left, -3.0e38).then_inc(topk_step, 1)

            def topk_rounds(first, last):
                for r in range(first, last):
                    topk_round(*divmod(r, ROUNDS))

            for b in range(B + 1):
                if b < B:
                    dve.wait_ge(x_in[b], 16)
                    norm_stats(ln, tiles(x, b), b % 2)
                if b >= 1:
                    dve.wait_ge(rstd_ready, b)
                    normalise(tiles(xn, b - 1), tiles(x, b - 1), (b - 1) % 2).then_inc(xn_ready, TB)
            dve.wait_ge(small_in, 48)
            low_part(0, 0)
            for b in range(B):
                if b + 1 < B:
                    low_part(b + 1, b + 1)
                topk_rounds(TOPK_DONE[0] * b // B, TOPK_DONE[0] * (b + 1) // B)
                dve.wait_ge(v_ready, b + 1)
                dve.tensor_tensor(v[:, TB * b:TB * b + TB, :], ps[2][:].rearrange("p (t e) -> p t e", t=TB),
                                  brow[:, 0:1, :].broadcast_to([P, TB, E]), ALU.add).then_inc(v_out, 1)
            gs = Chain(dve, gam_step, 1)
            dve.wait_ge(gam_step, 1)
            gs(dve.tensor_scalar(gam[:, 1:2], gam[:, 1:2], 1.0, None, ALU.add))
            gs(dve.reciprocal(gam[:, 2:3], gam[:, 1:2]))
            dve.tensor_scalar(gam[:, 1:2], gam[:, 2:3], -1.0, 1.0, ALU.mult, ALU.add)
            gs(dve.tensor_scalar(gam[:, 3:4], gam[:, 2:3], 0.25, None, ALU.mult))

            def sparse_adjacency(b):
                at = (TOPK - 1) % 8
                dve.wait_ge(topk_step, (b + 1) * TOPK_LINKS)
                for t in range(TB):
                    last = dve.tensor_scalar(mask[:, t, :], sim[:, ds(b * TB + t, 1), :], top8[:, b * TB + t, at:at + 1], None,
                                             ALU.is_ge)
                last.then_inc(mask_step, 1)
                dve.wait_ge(mask_step, b + 1)
                dve.wait_ge(tanh_ready, b + 1)
                dve.scalar_tensor_tensor(flat(adj[:]), flat(tanh_sim[:]), 1.0, flat(mask[:]), ALU.add, ALU.mult)\
                    .then_inc(adj_ready, 1)

            def epilogue(b, part, link):
                xb = x[:, ds(b * TB, TB), :]
                if part == 0:
                    dve.wait_ge(p_ready, b * H0 + H0)
                    link(dve.reciprocal(prec[:], psums[:]))
                    dve.wait_ge(pv_ready, b * H0 + H0)
                    dve.tensor_tensor(on[:].rearrange("p t (h d) -> p (t h) d", h=H0),
                                      ps[4][:].rearrange("p (a d) -> p a d", d=D0),
                                      flat(prec[:]).unsqueeze(2).broadcast_to([P, TB * H0, D0]),
                                      ALU.mult).then_inc(o_out, 1)
                elif part == 1:
                    dve.wait_ge(oh_ready, b + 1)
                    dve.tensor_tensor(flat(ol[:]), ps[5][:], flat(oh[:]).bitcast(F32), ALU.subtract).then_inc(ol_ready, 1)
                    dve.wait_ge(adjT_ready, b + 1)
                    dve.tensor_tensor(flat(adj_sum[:]), ps[6][:], flat(adj[:]), ALU.add).then_inc(adj_summed, 1)
                elif part == 2:
                    dve.wait_ge(bo_added, b + 1)
                    dve.wait_ge(wo_ready, b + 1)
                    ins = dve.tensor_tensor(xb, ps[5][:].rearrange("p (t e) -> p t e", t=TB), xb, ALU.add)
                    link(ins)
                    norm_stats(link, [x[:, ds(b * TB + t, 1), :] for t in range(TB)], 0)
                elif part == 3:
                    dve.wait_ge(rstd_ready, b * 2 + B + 1)
                    link(normalise([on[:, t, :] for t in range(TB)], [x[:, ds(b * TB + t, 1), :] for t in range(TB)], 0))
                    link(dve.scalar_tensor_tensor(xb, on[:], gam[:, 1:2], xb, ALU.mult, ALU.add))
                    link(dve.scalar_tensor_tensor(xb, adj_sum[:], gam[:, 3:4], xb, ALU.mult, ALU.add))
                    norm_stats(link, [x[:, ds(b * TB + t, 1), :] for t in range(TB)], 0)
                else:
                    dve.wait_ge(rstd_ready, b * 2 + B + 2)
                    normalise([xn[:, ds(b * TB + t, 1), :] for t in range(TB)],
                              [x[:, ds(b * TB + t, 1), :] for t in range(TB)], 0).then_inc(xn_ready, TB)

            def attention(b, with_epilogue):
                if with_epilogue:
                    link = Chain(dve, epi_step, (b - 1) * EPI_LINKS)
                for h in range(H0):
                    if with_epilogue and h in (1, 5, 8, 11, 14):
                        epilogue(b - 1, (1, 5, 8, 11, 14).index(h), link)
                    n = b * H0 + h
                    wait_past(dve, s_ready, n + 1)
                    wait_past(dve, pT_ready, n - 3)
                    if b == 0:
                        dve.wait_ge(alibi_ready, h + 1)
                    dve.tensor_tensor_reduce(pr[:, h % 4, 0:P], ps[h % 2][:, 0:P], alibi[:, h, P:2 * P], 1.0, 3.0e38,
                                             ALU.add, ALU.min, nmax[:, h % 4, 0:1])
                    dve.tensor_tensor_reduce(pr[:, h % 4, P:3 * P], ps[h % 2][:, P:3 * P], alibi[:, h, :], 1.0, 3.0e38,
                                             ALU.add, ALU.min, nmax[:, h % 4, 1:2]).then_inc(max_ready, 1)
                    if h < H0 - 2:
                        first, n_rounds = TOPK_DONE[b], TOPK_DONE[b + 1] - TOPK_DONE[b]
                        topk_rounds(first + n_rounds * h // (H0 - 2), first + n_rounds * (h + 1) // (H0 - 2))
                    elif h == H0 - 2:
                        sparse_adjacency(b)
                if with_epilogue:
                    assert link.n == EPI_LINKS, link.n

            for b in range(B):
                attention(b, b > 0)
            link = Chain(dve, epi_step, (B - 1) * EPI_LINKS)
            for part in range(5):
                epilogue(B - 1, part, link)

            for b in range(B):
                low_part(B + b, b)
            link = Chain(dve, route_step)
            dve.wait_ge(logits_ready, 1)
            link(dve.tensor_copy(lg[:], ps[0][:, 0:T * NEXP].rearrange("p (t e) -> p t e", t=T)))
            dve.tensor_reduce(toplg[:], lg[:], X, ALU.max).then_inc(top_ready, 1)
            dve.wait_ge(top_ready, 1)
            link(dve.tensor_tensor(hit[:], lg[:], toplg[:].unsqueeze(2).broadcast_to([P, T, NEXP]), ALU.is_equal))
            link(dve.tensor_tensor(hit[:], hit[:], rev[:].unsqueeze(1).broadcast_to([P, T, NEXP]), ALU.mult))
            link(dve.tensor_reduce(which[:], hit[:], X, ALU.max))
            dve.tensor_tensor(onehot[:].rearrange("p e t -> p t e"), rev[:].unsqueeze(1).broadcast_to([P, T, NEXP]),
                              which[:].unsqueeze(2).broadcast_to([P, T, NEXP]), ALU.is_equal).then_inc(onehot_ready, 1)

            def shared_hidden(i):
                dve.wait_ge(sgate_ready, i + 1)
                wait_past(dve, sdown_ready, (i // FB) * 2)
                dve.tensor_tensor(hT[:, i % FB, :], ps[2 + 2 * (i % 2)][:], gate[:, i % 2, :], ALU.mult)\
                    .then_inc(sh_ready, 1)

            def shared_added(b):
                dve.wait_ge(sdown_ready, b + 1)
                dve.tensor_tensor(x[:, TB * b:TB * b + TB, :], ps[5 + b % 2][:].rearrange("p (t e) -> p t e", t=TB),
                                  x[:, TB * b:TB * b + TB, :], ALU.add).then_inc(sdown_added, 1)

            shared_hidden(0)
            dve.wait_ge(counts_ready, 1)
            total = ps[0][:, 128:128 + T * NEXP]
            link(dve.tensor_tensor_scan(flat(upto[:]), flat(notfirst[:]), total, 0.0, ALU.mult, ALU.add))
            link(dve.tensor_tensor(flat(place[:]), flat(upto[:]), total, ALU.subtract))
            link(dve.tensor_tensor(flat(place[:]), ps[0][:, 64:64 + T * NEXP], flat(place[:]), ALU.add))
            link(dve.tensor_tensor(cmp[:], upto[:, :, T - 1:T].broadcast_to([P, NEXP, T]),
                                   steps128[:].unsqueeze(1).broadcast_to([P, NEXP, T]), ALU.is_gt))
            link(dve.tensor_reduce(ntiles[:], cmp[:], X, ALU.add))
            link(dve.tensor_tensor_scan(ends[:], ones[:, 0:NEXP], ntiles[:], 0.0, ALU.mult, ALU.add))
            link(dve.tensor_tensor(starts[:], ends[:], ntiles[:], ALU.subtract))
            link(dve.scalar_tensor_tensor(place[:], starts[:].unsqueeze(2).broadcast_to([P, NEXP, T]), float(P), place[:],
                                          ALU.mult, ALU.add))
            link(dve.tensor_tensor(place[:], place[:], onehot[:], ALU.mult))
            link(dve.tensor_reduce(slotf[:], place[:].rearrange("p e t -> p t e"), X, ALU.add))
            dve.tensor_copy(slot[:], slotf[:]).then_inc(slot_ready, 1)
            link(dve.tensor_tensor(cmp2[:], ends[0:1, :].unsqueeze(1).broadcast_to([1, NSLOT + 1, NEXP]),
                                   tile_no[:].unsqueeze(2).broadcast_to([1, NSLOT + 1, NEXP]), ALU.is_le))
            link(dve.tensor_reduce(tilef[:], cmp2[:], X, ALU.add))
            dve.tensor_scalar(tile_expert[:], tilef[:], float(NEXP - 1), None, ALU.min).then_inc(tile_ready, 1)
            for i in range(1, FB):
                shared_hidden(i)
            shared_added(0)
            shared_added(1)
            def routed_hidden(j):
                dve.wait_ge(rgate_ready, j + 1)
                wait_past(dve, rh_turned, j - 1)
                dve.tensor_tensor(rh[:, j % 2], ps[2 + 4 * (j % 2)][:], rgate[:, j % 2], ALU.mult).then_inc(rh_ready, 1)

            def routed_out(j):
                dve.wait_ge(y_ready, j + 1)
                wait_past(dve, y_stored[j % 2], 16 * (j // 2))
                dve.tensor_copy(yb[:, j % 2, :], ps[4][:, 0:E]).then_inc(y_out, 1)

            for j in range(NSLOT + 2):
                if j < NSLOT:
                    routed_hidden(j)
                if j >= 2:
                    routed_out(j - 2)
            for i in range(FB, 2 * FB):
                shared_hidden(i)
            shared_added(2)
            shared_added(3)
            ln3 = Chain(dve, ln3_step)

            def late_norm(n, stage, residual):
                for b in range(B + 1):
                    if b < B:
                        residual(b)
                        norm_stats(ln3, tiles(x, b), b % 2)
                    if b >= 1:
                        dve.wait_ge(rstd_ready, n + b)
                        normalise(tiles(xn, b - 1), tiles(x, b - 1), (b - 1) % 2).then_inc(xn_ready, TB)
                    if b >= 2:
                        low_part(stage * B + b - 2, b - 2)
                low_part(stage * B + B - 1, B - 1)

            def add_routed(b):
                dve.wait_ge(yg_in[b], 16 * TB)
                dve.wait_ge(sdown_added, b + 1)
                dve.tensor_tensor(x[:, TB * b:TB * b + TB, :], x[:, TB * b:TB * b + TB, :],
                                  yg[:, TB * b:TB * b + TB, :], ALU.add).then_inc(yg_added, 1)
                dve.wait_ge(yg_added, b + 1)

            dve.wait_ge(slopes_in, 16)
            dve.tensor_scalar(slopes[:], slopes[:], -1.0, None, ALU.mult).then_inc(slopes_negated, 1)
            late_norm(3 * B, 2, add_routed)

            def mask_scores(h, i):
                for p in range(2):
                    dve.wait_ge(scores_ready, 2 * h + p + 1)
                    wait_past(dve, head_ready, 2 * h + p - 1)
                    dve.tensor_tensor(masked[:, p], banks[:, 4:6, 0:S + P],
                                      decay[:, ds(h, 1), :].broadcast_to([P, TB, S + P]), ALU.mult).then_inc(masked_ready, 1)

            def gate_head(h, i):
                dve.wait_ge(gd_out, h + 1)
                for p in range(2):
                    dve.wait_ge(head_ready, 2 * h + p + 1)
                    dve.scalar_tensor_tensor(heads[:, ds(h, 1), p * HALF:(p + 1) * HALF], gd[:, i, p * HALF:(p + 1) * HALF],
                                             1.0, ps[6 + p][:], ALU.add, ALU.mult).then_inc(head_out, 1)

            dve.wait_ge(decay_ready, 1)
            for h in (0, 1):
                mask_scores(h, h % 2)
                gate_head(h, h % 2)
            with dve.Fori(2, H1 - 2, 2) as h:
                for i in range(2):
                    mask_scores(h + i, i)
                    gate_head(h + i, i)
            for h in (H1 - 2, H1 - 1):
                mask_scores(h, h % 2)
                gate_head(h, h % 2)
            dve.wait_ge(ms_ready, 1)
            dve.tensor_scalar(ms[:], ps[2][:, 0:T], 1.0 / (H1 * D1), 1e-6, ALU.mult, ALU.add).then_inc(rms_step, 1)
            dve.wait_ge(late_in, 48)
            dve.tensor_scalar(wj[:], ones[0:C, :], ex[:, 1:2], None, ALU.mult).then_inc(ex_ready, 1)
            dve.wait_ge(pair_ready, 1)
            dve.tensor_scalar(si[:], ps[3][:, 0:T], eb[:, 0:1], None, ALU.add).then_inc(si_out, 1)
            dve.wait_ge(rms_ready, 1)
            l45 = Chain(dve, ln45_step)

            def add_linear(b):
                dve.wait_ge(y1_ready, b + 1)
                for t in range(TB):
                    last = dve.scalar_tensor_tensor(x[:, TB * b + t, :], ps[b % 2][:, t * E:(t + 1) * E],
                                                    rms[:, TB * b + t:TB * b + t + 1], x[:, TB * b + t, :], ALU.mult, ALU.add)
                last.then_inc(y1_added, 1)
                dve.wait_ge(y1_added, b + 1)


            def add_pair(b):
                dve.wait_ge(rstd_ready, 4 * B + 2 * b + 1)
                l45(normalise(tiles(xn, b), tiles(x, b), b % 2))
                xb = x[:, TB * b:TB * b + TB, :]
                l45(dve.scalar_tensor_tensor(xb, xn[:, TB * b:TB * b + TB, :], 1.0 - 0.6, xb, ALU.mult, ALU.add))
                dve.wait_ge(pair_out, TB * b + TB)
                l45(dve.scalar_tensor_tensor(xb, pair[:, TB * b:TB * b + TB, :], 0.6, xb, ALU.mult, ALU.add))


            def relu_hidden(b):
                dve.wait_ge(up_ready, 2 * b + 2)
                wait_past(dve, f_ready, 2 * b - 2)
                for m in range(FB):
                    last = dve.tensor_scalar(f1[:, b % 2, m, :], ps[4 + m // 2][:, (m % 2) * S:(m % 2 + 1) * S],
                                             facol[:, FB + m:FB + m + 1], 0.0, ALU.add, ALU.max)
                last.then_inc(f1_out, 1)

            def combine(b):
                link = Chain(dve, f_step, 3 * b)
                dve.wait_ge(f_ready, 2 * b + 2)
                brow2 = fbrow[:, 0:1, :].broadcast_to([P, TB, E]), fbrow[:, 1:2, :].broadcast_to([P, TB, E])
                link(dve.tensor_tensor(y0[:], ps[2][:].rearrange("p (t e) -> p t e", t=TB), brow2[0], ALU.add))
                link(dve.tensor_tensor(y1[:], ps[3][:].rearrange("p (t e) -> p t e", t=TB), brow2[1], ALU.add))
                for t in range(TB):
                    last = dve.scalar_tensor_tensor(x[:, TB * b + t, :], y0[:, t, :], choice[:, t, 0:1],
                                                    x[:, TB * b + t, :], ALU.mult, ALU.add)
                link(last)
                for t in range(TB):
                    last = dve.scalar_tensor_tensor(x[:, TB * b + t, :], y1[:, t, :], choice[:, t, 1:2],
                                                    x[:, TB * b + t, :], ALU.mult, ALU.add)
                last.then_inc(x_final, 1)

            def choose(b):
                dve.wait_ge(up_ready, 2 * b + 1)
                wait_past(dve, x_final, b)
                ch = Chain(dve, choice_step, 3 * b)
                ch(dve.tensor_copy(lg2[:], ps[7][:, 0:2 * TB].rearrange("p (t e) -> p t e", t=TB)))
                ch(dve.tensor_tensor(choice[:, :, 0:1], lg2[:, :, 0:1], lg2[:, :, 1:2], ALU.is_ge))
                ch(dve.tensor_scalar(choice[:, :, 1:2], choice[:, :, 0:1], -1.0, 1.0, ALU.mult, ALU.add))

            for b in range(B):
                add_linear(b)
                norm_stats(l45, tiles(x, b), b % 2)
                add_pair(b)
                norm_stats(l45, tiles(x, b), b % 2)
                dve.wait_ge(rstd_ready, 4 * B + 2 * b + 2)
                normalise(tiles(xn, b), tiles(x, b), b % 2).then_inc(xn_ready, TB)
                if b:
                    low_part(3 * B + b - 1, b - 1)
            low_part(4 * B - 1, B - 1)
            dve.wait_ge(facol_in, 32)
            for b in range(B):
                if b:
                    combine(b - 1)
                choose(b)
                relu_hidden(b)
            combine(B - 1)

        @block.scalar
        def _(act):
            def high_part(n, b):
                act.wait_ge(xT_ready, n + 1)
                act.activation(xh[:, :, b * S:(b + 1) * S], ps[7][:].rearrange("p (k s) -> p k s", k=K), ACT.Copy)\
                    .then_inc(xh_ready, 1)

            def distances(first, last):
                for h in range(first, last):
                    act.activation(alibi[:, h, :], span[:], ACT.Copy, scale=SLOPES[h]).then_inc(alibi_ready, 1)

            act.wait_ge(span_ready, 1)
            distances(0, 8)
            for i, dst in enumerate((cQ, cQ, cK, cK)):
                act.wait_ge(ctx_qk, i + 1)
                act.activation(dst[:, (i % 2) * 512:(i % 2) * 512 + 512], ps[3 + i][0:C, :], ACT.Copy)\
                    .then_inc(ctx_qk_out, 1)

            def weight_high(w):
                act.wait_ge(aw_in[w], 16)
                act.activation(awh[:, w], aw[:, w], ACT.Copy).then_inc(awh_ready, 1)

            for w in range(3):
                weight_high(w)
            act.wait_ge(small_in, 48)
            act.activation(gam[:, 1:2], gam[:, 0:1], ACT.Exp, scale=-1.0).then_inc(gam_step, 1)

            def project_out(b):
                for bank, s_in, dst, s_out, col in ((0, q_ready, qT, q_out, 0), (1, k_ready, kT, k_out, K)):
                    act.wait_ge(s_in, b + 1)
                    for k in range(K):
                        last = act.activation(dst[:, k, b * S:(b + 1) * S], ps[bank][:, k * S:(k + 1) * S], ACT.Identity,
                                              bias=bcol[:, col + k:col + k + 1])
                    last.then_inc(s_out, 1)

            high_part(0, 0)
            for i in range(B):
                act.wait_ge(sim_ready, i + 1)
                act.activation(sim[:, TB * i:TB * i + TB, :], ps[3 + i][:].rearrange("p (t s) -> p t s", t=TB), ACT.Copy,
                               scale=1.0 / 16).then_inc(sim_out, 1)
            for b in range(B):
                if b + 1 < B:
                    high_part(b + 1, b + 1)
                project_out(b)
            weight_high(3)
            distances(8, H0)

            def oT_high(b):
                act.wait_ge(oT_ready, b + 1)
                act.activation(flat(oh[:]), ps[5][:], ACT.Copy).then_inc(oh_ready, 1)

            def attention(b, with_epilogue):
                for h in range(H0 + 2):
                    n = b * H0 + h
                    if h < H0:
                        if h == 0:
                            wait_past(act, o_out, b)
                        act.wait_ge(max_ready, n + 1)
                        act.activation(pr[:, h % 4, 0:P], pr[:, h % 4, 0:P], ACT.Exp, scale=-1.0,
                                       bias=nmax[:, h % 4, 0:1], accum_out=psums[:, 0, h:h + 1])
                        act.activation(pr[:, h % 4, P:3 * P], pr[:, h % 4, P:3 * P], ACT.Exp, scale=-1.0,
                                       bias=nmax[:, h % 4, 1:2], accum_out=psums[:, 1, h:h + 1]).then_inc(p_ready, 1)
                    if h >= 2:
                        act.wait_ge(pT_ready, n - 1)
                        wait_past(act, pv_ready, n - 3)
                        act.activation(prT[:, h % 2, :], ps[2 + h % 2][:, 0:3 * P], ACT.Copy).then_inc(pT_out, 1)
                    if h == 3 and with_epilogue:
                        oT_high(b - 1)
                    if h == 8:
                        wait_past(act, adj_ready, b)
                        act.activation(tanh_sim[:], sim[:, ds(b * TB, TB), :], ACT.Tanh, scale=0.5).then_inc(tanh_ready, 1)

            for b in range(B):
                attention(b, b > 0)
            oT_high(B - 1)

            for b in range(B):
                high_part(B + b, b)
            act.wait_ge(top_ready, 1)
            act.activation(score[:], toplg[:], ACT.Sigmoid).then_inc(score_ready, 1)
            act.wait_ge(score_ready, 1)
            for t in range(T):
                act.activation(xn[:, t, :], xn[:, t, :], ACT.Copy, scale=score[:, t:t + 1]).then_inc(xs_ready, 1)

            def shared_gate(i):
                act.wait_ge(sgu_ready, i + 1)
                wait_past(act, sh_ready, i - 1)
                act.activation(gate[:, i % 2, :], ps[1 + 2 * (i % 2)][:], ACT.Silu).then_inc(sgate_ready, 1)

            for i in range(FB):
                shared_gate(i)

            def turned_rows(j):
                act.wait_ge(xg_turned, j + 1)
                wait_past(act, gu_done, j - 1)
                act.activation(xgT[:, j % 2].rearrange("p k r -> p (k r)"), ps[0][:, 0:E], ACT.Copy).then_inc(xgT_out, 1)

            def routed_gate(j):
                act.wait_ge(gu_done, j + 1)
                wait_past(act, rh_ready, j - 1)
                act.activation(rgate[:, j % 2], ps[1 + 4 * (j % 2)][:], ACT.Silu).then_inc(rgate_ready, 1)

            def turned_hidden(j):
                act.wait_ge(rh_turned, j + 1)
                wait_past(act, y_ready, j - 1)
                act.activation(flat(rhT[:, j % 2]), ps[3 + 4 * (j % 2)][:], ACT.Copy).then_inc(rhT_out, 1)

            turned_rows(0)
            for j in range(NSLOT + 1):
                if j < NSLOT:
                    routed_gate(j)
                if j + 1 < NSLOT:
                    turned_rows(j + 1)
                if j >= 1:
                    turned_hidden(j - 1)
            for i in range(FB, 2 * FB):
                shared_gate(i)
            act.wait_ge(slopes_negated, 1)
            act.wait_ge(distance_ready, 1)
            for h in range(H1):
                act.activation(decay[:, h, :], distance[:], ACT.Exp, scale=slopes[:, h:h + 1]).then_inc(powers_ready, 1)
            for b in range(B):
                high_part(2 * B + b, b)

            def evacuate(h, i, what):
                pair_a, pair_b = banks[:, 0:2, :], banks[:, 2:4, :]
                if what == "q":
                    act.wait_ge(qd_ready, h + 1)
                    wait_past(act, scores_ready, 2 * h - 2)
                    act.activation(qd[:, i].rearrange("p (c n) -> p c n", c=2), pair_a, ACT.Silu).then_inc(qd_out, 1)
                elif what == "k":
                    act.wait_ge(kd_ready, h + 1)
                    wait_past(act, scores_ready, 2 * h - 2)
                    act.activation(kd[:, i].rearrange("p (c n) -> p c n", c=2), pair_b, ACT.Silu).then_inc(kd_out, 1)
                else:
                    act.wait_ge(gd_ready, h + 1)
                    wait_past(act, head_out, 2 * h - 2)
                    act.activation(gd[:, i].rearrange("p (c n) -> p c n", c=2), pair_b, ACT.Tanh, scale=0.5).then_inc(gd_out, 1)

            def evacuate_v(h, u):
                act.wait_ge(vd_ready, h + u + 1)
                wait_past(act, head_ready, 2 * h - 1 + u)
                act.activation(vd[:, 4 * u:4 * u + 4, :].rearrange("p (c t) d -> p c (t d)", c=2), banks[:, 0:2, :],
                               ACT.Silu).then_inc(vd_out, 1)

            def square(h, p):
                act.wait_ge(head_out, 2 * h + p + 1)
                wait_past(act, square_added, 2 * h + p - 1)
                act.activation(squares[:, p, :], ps[6 + p][:], ACT.Square).then_inc(squared, 1)

            def unit(h, i):
                evacuate(h + 1, 1 - i, "q")
                evacuate(h + 1, 1 - i, "k")
                square(h, 0)
                if i == 0:
                    evacuate(h + 1, 1 - i, "g")
                    square(h, 1)
                else:
                    evacuate_v(h + 1, 0)
                    square(h, 1)
                    evacuate_v(h + 1, 1)
                    evacuate(h + 1, 1 - i, "g")

            evacuate(0, 0, "q")
            evacuate(0, 0, "k")
            evacuate_v(0, 0)
            evacuate_v(0, 1)
            evacuate(0, 0, "g")
            unit(0, 0)
            unit(1, 1)
            with act.Fori(2, H1 - 2, 2) as h:
                unit(h, 0)
                unit(h + 1, 1)
            unit(H1 - 2, 0)
            square(H1 - 1, 0)
            square(H1 - 1, 1)
            act.wait_ge(si_out, 1)
            for t in range(T):
                act.wait_ge(pair_ready, 3 + 2 * (t // (2 * TB)))
                act.activation(pair[:, t, :], ps[4 + t // (2 * TB)][:, (t // TB % 2) * S:(t // TB % 2 + 1) * S], ACT.Sigmoid,
                               bias=si[:, t:t + 1]).then_inc(pair_out, 1)
            for b in range(B):
                high_part(3 * B + b, b)
            act.wait_ge(facol_in, 32)
            for b in range(B):
                act.wait_ge(up_ready, 2 * b + 1)
                wait_past(act, f_ready, 2 * b - 3)
                for m in range(FB):
                    last = act.activation(f0[:, b % 2, m, :], ps[m // 2][:, (m % 2) * S:(m % 2 + 1) * S], ACT.Gelu,
                                          bias=facol[:, m:m + 1])
                last.then_inc(f0_out, 1)

        @block.tensor
        def _(pe):
            def product3(dst, lh, ll, rh, rl, first, last):
                pe.matmul(dst, lh, rh, start=first, stop=False)
                pe.matmul(dst, lh, rl, start=False, stop=False)
                return pe.matmul(dst, ll, rh, start=False, stop=last)

            def transpose_norm(n, b):
                pe.wait_ge(xn_ready, TB * (n + 1))
                wait_past(pe, xl_ready, n)
                for k in range(K):
                    for t in range(TB):
                        last = pe.transpose(ps[7][:, (k * TB + t) * P:(k * TB + t + 1) * P],
                                            xn[:, TB * b + t, k * P:(k + 1) * P], ident[:])
                last.then_inc(xT_ready, 1)

            pe.wait_ge(consts, 1)
            pe.wait_ge(ctx_in, 32)
            for i in range(4):
                pe.matmul(ps[3 + i][0:C, :], xw[:, i // 2, :], ctxT[:, (i % 2) * 512:(i % 2) * 512 + 512],
                          start=True, stop=True).then_inc(ctx_qk, 1)

            def project(b):
                pe.wait_ge(xl_ready, b + 1)
                cols = slice(b * S, (b + 1) * S)
                for w, bank, s_ready_, s_free in ((0, 0, q_ready, q_out), (1, 1, k_ready, k_out)):
                    pe.wait_ge(aw_split, w + 1)
                    wait_past(pe, s_free, b)
                    for m in range(K):
                        mc = slice(m * P, (m + 1) * P)
                        for k in range(K):
                            last = product3(ps[bank][:, m * S:(m + 1) * S], awh[:, w, k, mc], awl[:, w, k, mc],
                                            xh[:, k, cols], xl[:, k, cols], k == 0, k == K - 1)
                    last.then_inc(s_ready_, 1)
                pe.wait_ge(aw_split, 3)
                wait_past(pe, v_out, b)
                for t in range(TB):
                    tc = slice(b * S + t * P, b * S + (t + 1) * P)
                    for k in range(K):
                        last = product3(ps[2][:, t * E:(t + 1) * E], xh[:, k, tc], xl[:, k, tc],
                                        awh[:, 2, k, :], awl[:, 2, k, :], k == 0, k == K - 1)
                last.then_inc(v_ready, 1)

            transpose_norm(0, 0)
            pe.wait_ge(ctx_qk_out, 4)
            for t in range(T):
                mm = pe.matmul(ps[3 + t // TB][:, (t % TB) * S:(t % TB + 1) * S], cQ[:, t * P:(t + 1) * P],
                               cK[:, (t // TB) * S:(t // TB + 1) * S], start=True, stop=True)
                if t % TB == TB - 1:
                    mm.then_inc(sim_ready, 1)
            for b in range(B):
                if b + 1 < B:
                    transpose_norm(b + 1, b + 1)
                project(b)

            def heads_transposed(b):
                pe.wait_ge(o_out, b + 1)
                for k in range(K):
                    for t in range(TB):
                        last = pe.transpose(ps[5][:, (k * TB + t) * P:(k * TB + t + 1) * P],
                                            on[:, t, k * P:(k + 1) * P], ident[:])
                last.then_inc(oT_ready, 1)
                pe.wait_ge(adj_ready, b + 1)
                for i in range(TB):
                    for j in range(TB):
                        last = pe.transpose(ps[6][:, (i * TB + j) * P:(i * TB + j + 1) * P],
                                            adj[:, j, i * P:(i + 1) * P], ident[:])
                last.then_inc(adjT_ready, 1)

            def heads_out(b):
                pe.wait_ge(ol_ready, b + 1)
                for t in range(TB):
                    for k in range(K):
                        tc = slice(t * P, (t + 1) * P)
                        last = product3(ps[5][:, t * E:(t + 1) * E], oh[:, k, tc], ol[:, k, tc],
                                        awh[:, 3, k, :], awl[:, 3, k, :], k == 0, k == K - 1)
                last.then_inc(wo_ready, 1)

            def attention(b, with_epilogue):
                for h in range(H0 + 4):
                    n = b * H0 + h
                    if h < H0:
                        pe.wait_ge(qm_ready, n + 1)
                        wait_past(pe, max_ready, n - 1)
                        pe.matmul(ps[h % 2][:, 0:P], qm[:, h % 2, 0:P], kT[:, h // HB, ds(b * S, P)],
                                  start=True, stop=True)
                        pe.matmul(ps[h % 2][:, P:3 * P], qm[:, h % 2, P:2 * P], kT[:, h // HB, ds(b * S, S)],
                                  start=True, stop=True).then_inc(s_ready, 1)
                    if 2 <= h < H0 + 2:
                        pe.wait_ge(p_ready, n - 1)
                        wait_past(pe, pT_out, n - 3)
                        for i in range(3):
                            last = pe.transpose(ps[2 + h % 2][:, i * P:(i + 1) * P], pr[:, (h - 2) % 4, i * P:(i + 1) * P],
                                                ident[:])
                        last.then_inc(pT_ready, 1)
                    if h >= 4:
                        g = h - 4
                        pe.wait_ge(pT_out, n - 3)
                        if g == 0:
                            wait_past(pe, o_out, b)
                        c0 = g * D0
                        pe.matmul(ps[4][:, c0:c0 + D0], prT[:, g % 2, 0:P], v[:, ds(b * TB, 1), c0:c0 + D0],
                                  start=True, stop=True)
                        pe.matmul(ps[4][:, E + c0:E + c0 + D0], prT[:, g % 2, P:2 * P],
                                  v[:, ds(b * TB, 1), c0:c0 + D0], start=True, stop=False)
                        pe.matmul(ps[4][:, E + c0:E + c0 + D0], prT[:, g % 2, 2 * P:3 * P],
                                  v[:, ds(b * TB + 1, 1), c0:c0 + D0], start=False, stop=True).then_inc(pv_ready, 1)
                    if with_epilogue and h == 2:
                        heads_transposed(b - 1)
                    if with_epilogue and h == 6:
                        heads_out(b - 1)

            pe.wait_ge(q_out, B)
            pe.wait_ge(k_out, B)
            pe.wait_ge(v_out, B)
            pe.wait_ge(sim_out, B)
            for b in range(B):
                attention(b, b > 0)
            heads_transposed(B - 1)
            heads_out(B - 1)

            for b in range(B):
                transpose_norm(B + b, b)
            pe.wait_ge(rw_split, 1)
            pe.wait_ge(xl_ready, 2 * B)
            for t in range(T):
                for k in range(K):
                    tc = slice(t * P, (t + 1) * P)
                    last = product3(ps[0][:, t * NEXP:(t + 1) * NEXP], xh[:, k, tc], xl[:, k, tc], rwh[:, k, :], rwl[:, k, :],
                                    k == 0, k == K - 1)
            last.then_inc(logits_ready, 1)

            def shared_up(i):
                half, m = divmod(i, FB)
                cols, mc = slice(half * HALF, (half + 1) * HALF), slice(m * P, (m + 1) * P)
                wait_past(pe, sh_ready, i - 1)
                for bank, hi, lo in ((1, sgh, sgl), (2, suh, sul)):
                    for k in range(K):
                        last = product3(ps[bank + 2 * (i % 2)][:], hi[:, k, mc], lo[:, k, mc], xh[:, k, cols], xl[:, k, cols],
                                        k == 0, k == K - 1)
                last.then_inc(sgu_ready, 1)

            def shared_down(half):
                pe.wait_ge(sd_in, 16)
                pe.wait_ge(sh_ready, FB * (half + 1))
                for b in range(2):
                    wait_past(pe, sdown_added, 2 * half)
                    for t in range(TB):
                        tc = slice((b * TB + t) * P, (b * TB + t + 1) * P)
                        for m in range(FB):
                            last = pe.matmul(ps[5 + b][:, t * E:(t + 1) * E], hT[:, m, tc], sd[:, m, :],
                                             start=(m == 0), stop=(m == FB - 1))
                    last.then_inc(sdown_ready, 1)

            pe.wait_ge(shared_split, 4)
            shared_up(0)
            pe.wait_ge(onehot_ready, 1)
            pe.matmul(ps[0][:, 64:64 + T * NEXP], before[:], flat(onehot[:]), start=True, stop=True)
            pe.matmul(ps[0][:, 128:128 + T * NEXP], ones[:], flat(onehot[:]), start=True, stop=True).then_inc(counts_ready, 1)
            for i in range(1, FB):
                shared_up(i)
            shared_down(0)

            def turn_rows(j):
                pe.wait_ge(xg_in[j % 3], 16 * (j // 3 + 1))
                if j == 0:
                    pe.wait_ge(slot_ready, 1)
                wait_past(pe, xgT_out, j)
                for k in range(K):
                    last = pe.transpose(ps[0][:, k * P:(k + 1) * P], xg[:, j % 3, k * P:(k + 1) * P], ident[:])
                last.then_inc(xg_turned, 1)

            def gate_up(j):
                e = pe.value_load(tile_expert[0:1, j:j + 1], min_val=0, max_val=NEXP - 1)
                pe.wait_ge(xgT_out, j + 1)
                wait_past(pe, rh_ready, j - 1)
                if j == 1:
                    pe.wait_ge(sdown_added, 2)
                for bank in range(2):
                    for k in range(K):
                        last = pe.matmul(ps[1 + 4 * (j % 2) + bank][:], xgT[:, j % 2, k, :], gu[:, ds(e, 1), k, bank * FI:(bank + 1) * FI],
                                         start=(k == 0), stop=(k == K - 1))
                last.then_inc(gu_done, 1)
                return e

            def turn_hidden(j):
                pe.wait_ge(rh_ready, j + 1)
                wait_past(pe, rhT_out, j - 1)
                for m in range(FB):
                    last = pe.transpose(ps[3 + 4 * (j % 2)][:, m * P:(m + 1) * P], rh[:, j % 2, m * P:(m + 1) * P], ident[:])
                last.then_inc(rh_turned, 1)

            def down(j, e):
                pe.wait_ge(rhT_out, j + 1)
                wait_past(pe, y_out, j)
                for m in range(FB):
                    last = pe.matmul(ps[4][:, 0:E], rhT[:, j % 2, m, :], dn[:, ds(e, 1), m, :], start=(m == 0), stop=(m == FB - 1))
                last.then_inc(y_ready, 1)

            pe.wait_ge(sh_ready, FB)
            pe.wait_ge(tile_ready, 1)
            pe.wait_ge(gu_in, 16 * NEXP)
            pe.wait_ge(dn_in, 16 * NEXP)
            turn_rows(0)
            experts = {}
            for j in range(NSLOT + 2):
                if j < NSLOT:
                    experts[j] = gate_up(j)
                if j + 1 < NSLOT:
                    turn_rows(j + 1)
                if 1 <= j <= NSLOT:
                    turn_hidden(j - 1)
                if j >= 2:
                    down(j - 2, experts.pop(j - 2))
            pe.wait_ge(y_out, NSLOT)
            for i in range(FB, 2 * FB):
                shared_up(i)
            shared_down(1)
            for b in range(B):
                transpose_norm(2 * B + b, b)
            pe.wait_ge(xl_ready, 3 * B)

            def project_head(h, i, what):
                c = "qkg".index(what) * D1
                if what == "q":
                    pe.wait_ge(w_split, h + 1)
                    if i == 1:
                        pe.wait_ge(vd_out, h + 1)
                    else:
                        wait_past(pe, qd_out, h)
                    dst, s_ = 0, qd_ready
                elif what == "k":
                    wait_past(pe, gd_out, h)
                    dst, s_ = 2, kd_ready
                else:
                    pe.wait_ge(kd_out, h + 1)
                    dst, s_ = 2, gd_ready
                for half in range(2):
                    hc = slice(half * HALF, (half + 1) * HALF)
                    for k in range(K):
                        last = product3(ps[dst + half][:], wh[:, i, k, c:c + D1], wl[:, i, k, c:c + D1],
                                        xh[:, k, hc], xl[:, k, hc], k == 0, k == K - 1)
                last.then_inc(s_, 1)

            def project_v(h, u):
                if u == 0:
                    pe.wait_ge(v_split, h + 2)
                    pe.wait_ge(qd_out, h + 1)
                else:
                    pe.wait_ge(vd_out, h + 1)
                for t in range(4):
                    tc = slice((4 * u + t) * P, (4 * u + t + 1) * P)
                    for k in range(K):
                        last = product3(ps[t // 2][:, (t % 2) * 2 * D1:(t % 2 + 1) * 2 * D1], xh[:, k, tc], xl[:, k, tc],
                                        vh[:, k, :], vl[:, k, :], k == 0, k == K - 1)
                last.then_inc(vd_ready, 1)

            def score_pair(h, i, p):
                if p == 0:
                    pe.wait_ge(kd_out, h + 1)
                wait_past(pe, masked_ready, 2 * h + p)
                for j in range(2):
                    c0 = (2 * p + j) * S
                    pe.matmul(ps[4 + j][:, 0:S], kd[:, i, c0:c0 + P], qd[:, i, c0:c0 + S], start=True, stop=True)
                    last = pe.matmul(ps[4 + j][:, S:S + P], kd[:, i, c0 + P:c0 + S], qd[:, i, c0 + P:c0 + S],
                                     start=True, stop=True)
                last.then_inc(scores_ready, 1)

            def head_pair(h, i, p):
                pe.wait_ge(masked_ready, 2 * h + p + 1)
                pe.wait_ge(vd_out, h - i + p + 1)
                wait_past(pe, squared, 2 * h + p - 1)
                for j in range(2):
                    t = (2 * p + j) * TB
                    pe.matmul(ps[6 + p][:, j * S:(j + 1) * S], vd[:, t, i * D1:(i + 1) * D1], masked[:, p, j, 0:S], start=True, stop=False)
                    last = pe.matmul(ps[6 + p][:, j * S + P:(j + 1) * S], vd[:, t + 1, i * D1:(i + 1) * D1], masked[:, p, j, S:S + P],
                                     start=False, stop=True)
                last.then_inc(head_ready, 1)

            def unit(h, i):
                project_head(h + 1, 1 - i, "q")
                score_pair(h, i, 0)
                project_head(h + 1, 1 - i, "k")
                score_pair(h, i, 1)
                head_pair(h, i, 0)
                if i == 0:
                    project_head(h + 1, 1 - i, "g")
                    head_pair(h, i, 1)
                else:
                    project_v(h + 1, 0)
                    head_pair(h, i, 1)
                    project_v(h + 1, 1)
                    project_head(h + 1, 1 - i, "g")

            project_head(0, 0, "q")
            project_head(0, 0, "k")
            project_v(0, 0)
            project_v(0, 1)
            project_head(0, 0, "g")
            unit(0, 0)
            unit(1, 1)
            with pe.Fori(2, H1 - 2, 2) as h:
                unit(h, 0)
                unit(h + 1, 1)
            unit(H1 - 2, 0)
            score_pair(H1 - 1, 1, 0)
            score_pair(H1 - 1, 1, 1)
            head_pair(H1 - 1, 1, 0)
            head_pair(H1 - 1, 1, 1)
            pe.wait_ge(wo_scaled, 1)
            pe.wait_ge(head_out, 2 * H1)
            pe.wait_ge(gd_out, H1)

            def project_heads(b):
                wait_past(pe, y1_added, b - 1)
                for t in range(TB):
                    tc = slice((TB * b + t) * P, (TB * b + t + 1) * P)
                    for h in range(H1):
                        last = pe.matmul(ps[b % 2][:, t * E:(t + 1) * E], heads[:, h, tc], wo[:, h, :],
                                         start=(h == 0), stop=(h == H1 - 1))
                last.then_inc(y1_ready, 1)

            project_heads(0)
            pe.wait_ge(square_added, 2 * H1)
            for t in range(T):
                last = pe.matmul(ps[2][:, t:t + 1], flat(square_sum[:])[:, t * P:(t + 1) * P], ones[:, 0:1], start=True, stop=True)
            last.then_inc(ms_ready, 1)
            pe.wait_ge(ex_ready, 1)
            for t in range(T):
                last = pe.matmul(ps[3][:, t:t + 1], ctx2[:, t * P:(t + 1) * P], ex[:, 0:1], start=True, stop=True)
            last.then_inc(pair_ready, 1)
            for b in range(B):
                pe.matmul(ps[4 + b // 2][:, (b % 2) * S:(b % 2 + 1) * S], wj[:], ctx2[:, b * S:(b + 1) * S],
                          start=True, stop=True).then_inc(pair_ready, 1)
            for b in range(1, B):
                project_heads(b)
                if b >= 1:
                    transpose_norm(3 * B + b - 1, b - 1)
            transpose_norm(4 * B - 1, B - 1)
            pe.wait_ge(xl_ready, 4 * B)
            pe.wait_ge(y1_added, B)
            pe.wait_ge(pair_out, T)
            pe.wait_ge(fa_split, 2)
            pe.wait_ge(fg_split, 1)
            pe.wait_ge(fb_in, 32)

            def choice_logits(b):
                wait_past(pe, choice_step, 3 * b)
                for t in range(TB):
                    tc = slice((TB * b + t) * P, (TB * b + t + 1) * P)
                    for k in range(K):
                        product3(ps[7][:, 2 * t:2 * t + 2], xh[:, k, tc], xl[:, k, tc], fgh[:, k, :], fgl[:, k, :],
                                 k == 0, k == K - 1)

            def up(b):
                cols = slice(b * S, (b + 1) * S)
                for i, s_free in enumerate((f0_out, f1_out)):
                    wait_past(pe, s_free, b)
                    for m in range(FB):
                        mc = slice(m * P, (m + 1) * P)
                        for k in range(K):
                            last = product3(ps[4 * i + m // 2][:, (m % 2) * S:(m % 2 + 1) * S], fah[:, i, k, mc],
                                            fal[:, i, k, mc], xh[:, k, cols], xl[:, k, cols], k == 0, k == K - 1)
                    last.then_inc(up_ready, 1)

            def down_experts(b):
                for i, (f, s_out) in enumerate(((f0, f0_out), (f1, f1_out))):
                    pe.wait_ge(s_out, b + 1)
                    wait_past(pe, x_final, b)
                    for t in range(TB):
                        tc = slice(t * P, (t + 1) * P)
                        for m in range(FB):
                            last = pe.matmul(ps[2 + i][:, t * E:(t + 1) * E], f[:, b % 2, m, tc], fb[:, i, m, :],
                                             start=(m == 0), stop=(m == FB - 1))
                    last.then_inc(f_ready, 1)

            for b in range(B):
                choice_logits(b)
                up(b)
                if b:
                    down_experts(b - 1)
            down_experts(B - 1)


def kernel(**inputs):
    import numpy as np
    import concourse.bacc as bacc
    from concourse.bass_utils import run_bass_kernel_spmd

    g = {k: np.asarray(v) for k, v in inputs.items()}
    ca = np.ascontiguousarray

    def cols(v):
        return v.reshape(-1, P).T

    w = g["L1_attn_w_qkv"].reshape(H1, 3, D1, E)
    wg = g["L1_attn_w_gate"].reshape(H1, 1, D1, E)
    heads = np.concatenate([w[:, :2], wg], axis=1)
    arrays = {
        "x": g["x"],
        "ctxT": g["ctx_512"].reshape(B * S, C).T,
        "aw": np.stack([g[f"L0_attn_W{n}"].T for n in "qkvo"]),
        "abcol": np.concatenate([cols(g["L0_attn_bq"]), cols(g["L0_attn_bk"])], axis=1),
        "abrow": np.stack([g["L0_attn_bv"], g["L0_attn_bo"]]),
        "xw": np.stack([g["L0_xattn_Wq"].T, g["L0_xattn_Wk"].T], axis=1),
        "gamma": g["L0_xattn_gamma_raw"].reshape(1, 1),
        "rw": g["L0_ffn_router_w"].T.reshape(K, P, NEXP).transpose(1, 0, 2),
        "gu": g["L0_ffn_gate_up_proj"],
        "dn": g["L0_ffn_down_proj"],
        "sg": g["L0_ffn_shared_gate_w"],
        "su": g["L0_ffn_shared_up_w"],
        "sd": g["L0_ffn_shared_down_w"],
        "slopes": g["L1_attn_slope_rate"].reshape(1, H1),
        "heads": heads.reshape(H1, 3 * D1, K, P).transpose(0, 3, 2, 1),
        "vpairs": w[:, 2].reshape(H1 // 2, 2 * D1, K, P).transpose(0, 3, 2, 1),
        "nw": cols(g["L1_attn_norm_w"]),
        "wo": g["L1_attn_w_out"].T.reshape(H1, D1, E).transpose(1, 0, 2),
        "ex": g["L1_xattn_W"].reshape(2, C).T,
        "eb": g["L1_xattn_b"].reshape(1, 1),
        "fg": g["L1_ffn_Wg"].T.reshape(K, P, 2).transpose(1, 0, 2),
        "fa": np.stack([g["L1_ffn_W0a"].T, g["L1_ffn_W1a"].T]),
        "fb": np.stack([g["L1_ffn_W0b"].T, g["L1_ffn_W1b"].T]),
        "facol": np.concatenate([cols(g["L1_ffn_b0a"]), cols(g["L1_ffn_b1a"])], axis=1),
        "fbrow": np.stack([g["L1_ffn_b0b"], g["L1_ffn_b1b"]]),
    }
    nc = bacc.Bacc("TRN2", target_bir_lowering=False, num_devices=1)
    arrays = {f"in_{k}": ca(v) for k, v in arrays.items()}
    aps = {k[3:]: nc.dram_tensor(k, v.shape, mybir.dt.from_np(v.dtype), kind="ExternalInput").ap()
           for k, v in arrays.items()}
    out = nc.dram_tensor("out", (B, S, E), F32, kind="ExternalOutput").ap()
    sorted_in = nc.dram_tensor("sorted_in", (NSLOT * P, E), F32).ap()
    sorted_out = nc.dram_tensor("sorted_out", (NSLOT * P, E), F32).ap()
    decoder(nc, aps, sorted_in, sorted_out, out)
    return run_bass_kernel_spmd(nc, [arrays], core_ids=[0]).results[0]["out"]
```

```python
from contextlib import ExitStack

import concourse.bass as bass
from concourse import mybir
from concourse.alu_op_type import AluOpType as ALU

ACT = mybir.ActivationFunctionType
F32 = mybir.dt.float32
F32R = mybir.dt.float32r
U32 = mybir.dt.uint32
I32 = mybir.dt.int32
X = mybir.AxisListType.X

P = 128
B, S, E = 4, 256, 256
T = B * S // P
TB = S // P
K = E // P
H0, D0 = 16, 16
HB = P // D0
C = 64
TOPK = int(S * 0.3)
NEXP, FI = 8, 512
FB = FI // P
NSLOT = T + NEXP - 1
HALF = B * S // 2
H1, D1 = 16, 128
PR = 6
QM = 4
BIG = 1e30
EPS = 1e-5
ds = bass.ds


class Chain:

    def __init__(self, eng, sem, base=0):
        self.eng, self.sem, self.base, self.n = eng, sem, base, 0

    def __call__(self, ins):
        ins.then_inc(self.sem, 1)
        self.n += 1
        self.eng.wait_ge(self.sem, self.base + self.n)


def wait_past(eng, sem, value):
    if not isinstance(value, int) or value > 0:
        eng.wait_ge(sem, value)


def decoder(nc, a, sorted_in, sorted_out, out):
    ctx = ExitStack()
    with ctx:
        base = -(-nc.sbuf_base // 64) * 64
        cursor = [base]

        def sb(name, shape, dt=F32):
            n = 4
            for s in shape[1:]:
                n *= s
            at = cursor[0]
            cursor[0] = at + -(-n // 64) * 64
            assert cursor[0] <= nc.sbuf_usable_end, (name, cursor[0] - nc.sbuf_usable_end)
            return nc.alloc_sbuf_tensor_at(name, shape, dt, offset=at)

        def sem(name):
            return ctx.enter_context(nc.semaphore(name))

        banks = ctx.enter_context(nc.psum_tensor("banks", [P, 8, 512], F32))
        ps = [banks[:, i, :] for i in range(8)]

        x = sb("x", [P, T, E])
        at_xn = cursor[0]
        xn = sb("xn", [P, T, E])
        at_xh = cursor[0]
        xh = sb("xh", [P, K, B * S], F32R)
        at_xl = cursor[0]
        xl = sb("xl", [P, K, B * S], F32R)
        ident = sb("ident", [P, P])
        before = sb("before", [P, P])
        ones = sb("ones", [P, P])
        headmask = sb("headmask", [P, HB])
        mhalf = sb("mhalf", [P, TB])
        stats = sb("stats", [P, 2, TB, 6])
        mv = sb("mv", [P, 2, TB, 2])
        ve = sb("ve", [P, 2, TB])
        rstd = sb("rstd", [P, 2, TB])
        bcol = sb("bcol", [P, 4])
        gam = sb("gam", [P, 4])
        zero_row = sb("zero_row", [P, E])
        top8 = sb("top8", [P, T, 8])
        nmax = sb("nmax", [P, PR, 2])
        psums = sb("psums", [P, 2, TB, H0])
        prec = sb("prec", [P, TB, H0])
        small_end = cursor[0] + 4096
        cursor[0] = small_end

        at_g = cursor[0]
        gu = sb("gu", [P, NEXP, K, 2 * FI])
        at_gu_tail = cursor[0] - 3 * K * 2 * FI * 4
        at_r = cursor[0]

        at_s = cursor[0]
        sgh, sgl, suh, sul = (sb(n, [P, K, FI], F32R) for n in ("sgh", "sgl", "suh", "sul"))
        at_c = cursor[0]
        qT = sb("qT", [P, K, B * S])
        kT = sb("kT", [P, K, B * S])
        v = sb("v", [P, T, E])
        awh = sb("awh", [P, 4, K, E], F32R)
        awl = sb("awl", [P, 4, K, E], F32R)
        alibi = sb("alibi", [P, H0, S])
        at_raw = cursor[0]
        aw = sb("aw", [P, 4, K, E])
        cursor[0] = at_raw
        on = sb("on", [P, TB, E])
        oh = sb("oh", [P, K, S], F32R)
        ol = sb("ol", [P, K, S], F32R)
        adj = sb("adj", [P, TB, S])
        pr = sb("pr", [P, PR, 3 * P])
        prT = sb("prT", [P, 2, 3 * P])
        work = sb("work", [P, TB, S])
        tanh_sim = sb("tanh_sim", [P, TB, S])
        mask = sb("mask", [P, TB, S])
        span = mask[:, 0, :]
        adj_sum = sb("adj_sum", [P, TB, S])
        brow = sb("brow", [P, 2, E])
        cursor[0] = at_gu_tail
        sim = sb("sim", [P, T, S])
        at_ctx = cursor[0]
        ctxT = sb("ctxT", [C, B * S])
        xw = sb("xw", [C, 2, C])
        cQ = sb("cQ", [C, B * S])
        cK = sb("cK", [C, B * S])
        cursor[0] = at_ctx
        qm = sb("qm", [P, QM, S])
        cursor[0] = at_xh
        shared_raw = sb("shared_raw", [P, 2, K, FI])

        cursor[0] = at_c
        head_raw = sb("head_raw", [P, 2, K, 3 * D1])
        v_raw = sb("v_raw", [P, K, 2 * D1])
        dn = sb("dn", [P, NEXP, FB, E])
        sd = sb("sd", [P, FB, E])
        hT = sb("hT", [P, FB, HALF])
        gate = sb("gate", [P, 2, HALF])
        xg = sb("xg", [P, 3, E])
        xgT = sb("xgT", [P, 2, K, P])
        rgate = sb("rgate", [P, 2, FI])
        rh = sb("rh", [P, 2, FI])
        rhT = sb("rhT", [P, 2, FB, P])
        yb = sb("yb", [P, 2, E])
        at_yg = cursor[0]
        yg = sb("yg", [P, T, E])
        lg = sb("lg", [P, T, NEXP])
        hit = sb("hit", [P, T, NEXP])
        toplg = sb("toplg", [P, T])
        score = sb("score", [P, T])
        which = sb("which", [P, T])
        onehot = sb("onehot", [P, NEXP, T])
        upto = sb("upto", [P, NEXP, T])
        place = sb("place", [P, NEXP, T])
        ntiles = sb("ntiles", [P, NEXP])
        ends = sb("ends", [P, NEXP])
        starts = sb("starts", [P, NEXP])
        slotf = sb("slotf", [P, T])
        slot = sb("slot", [P, T], U32)
        cmp = sb("cmp", [P, NEXP, T])
        cmp2 = sb("cmp2", [1, NSLOT + 1, NEXP])
        tilef = sb("tilef", [1, NSLOT + 1])
        tile_expert = sb("tile_expert", [1, NSLOT + 1], I32)
        end_c = cursor[0]
        cursor[0] = at_yg
        lgT = sb("lgT", [NEXP, B * S])

        cursor[0] = at_s
        wh = sb("wh", [P, 2, K, 3 * D1], F32R)
        wl = sb("wl", [P, 2, K, 3 * D1], F32R)
        vh = sb("vh", [P, K, 2 * D1], F32R)
        vl = sb("vl", [P, K, 2 * D1], F32R)
        cursor[0] = at_g
        heads = sb("heads", [P, H1, B * S])
        cursor[0] = at_c + K * 8 * D1 * 4
        decay = sb("decay", [P, H1, S + P])
        masked = sb("masked", [P, 2, TB, S + P])
        at_q = cursor[0]
        qd = sb("qd", [P, 2, B * S])
        kd = sb("kd", [P, 2, B * S])
        vd = sb("vd", [P, T, 2 * D1])
        gd = sb("gd", [P, 2, B * S])
        at_wo = cursor[0]
        wo = sb("wo", [P, H1, E])
        distance = sb("distance", [P, S + P])
        cursor[0] = at_xn
        squares = sb("squares", [P, 2, HALF])
        square_sum = sb("square_sum", [P, 2, HALF])
        cursor[0] = at_q
        fa = sb("fa", [P, 2, K, FI])
        fah = sb("fah", [P, 2, K, FI], F32R)
        fal = sb("fal", [P, 2, K, FI], F32R)
        fbrow = sb("fbrow", [P, 2, E])
        fgrow = sb("fgrow", [P, 2, E])
        fbl0 = sb("fbl0", [P, FB, E], F32R)
        assert cursor[0] <= at_q + 8 * B * S * 4
        cursor[0] = at_c + K * 8 * D1 * 4
        fb = sb("fb", [P, 2, FB, E])
        pair = sb("pair", [P, T, S])
        ctx2 = sb("ctx2", [C, B * S])
        ex = sb("ex", [C, 2])
        wj = sb("wj", [C, P])
        eb = sb("eb", [P, 1])
        si = sb("si", [P, T])
        fbh = sb("fbh", [P, 2, FB, E], F32R)
        junk = sb("junk", [P, E])
        choice = sb("choice", [P, T, 2])
        lg2 = sb("lg2", [P, T, 2])
        facol = sb("facol", [P, 2 * FB])
        assert cursor[0] <= at_q
        cursor[0] = at_s
        hidden = sb("hidden", [P, 2, 2, FB, S])
        f0, f1 = hidden[:, :, 0], hidden[:, :, 1]
        y = sb("y", [P, TB, 2, E])
        assert cursor[0] <= at_c + K * 8 * D1 * 4
        cursor[0] = at_s + 2 * FB * S * 4
        woh = sb("woh", [P, H1, E], F32R)
        assert cursor[0] <= at_c + K * 8 * D1 * 4
        cursor[0] = at_wo
        wol = sb("wol", [P, H1, E], F32R)
        cursor[0] = at_g
        head_parts = sb("head_parts", [P, H1, B * S], F32R)
        cursor[0] = at_q
        fbl = (fbl0, sb("fbl1", [P, FB, E], F32R))
        cursor[0] = at_g
        fh = sb("fh", [P, 2, 2, FB, S], F32R)
        fl = sb("fl", [P, 2, 2, FB, S], F32R)
        cursor[0] = small_end - 2048
        rev = sb("rev", [P, NEXP])
        steps128 = sb("steps128", [P, T])
        notfirst = sb("notfirst", [P, NEXP, T])
        tile_no = sb("tile_no", [1, NSLOT + 1])
        rw = sb("rw", [P, K, NEXP])
        rwh = sb("rwh", [P, K, NEXP], F32R)
        rwl = sb("rwl", [P, K, NEXP], F32R)
        slopes = sb("slopes", [P, H1])
        nw = sb("nw", [P, H1])
        ms = sb("ms", [P, T])
        rms = sb("rms", [P, T])
        rhalf = sb("rhalf", [P, T])

        x_in = [sem(f"x_in{b}") for b in range(B)]
        aw_in = [sem(f"aw_in{w}") for w in range(4)]
        ctx_in, small_in, shared_in = sem("ctx_in"), sem("small_in"), sem("shared_in")
        gu_in = sem("gu_in")
        consts, const_step = sem("consts"), sem("const_step")
        gam_step = sem("gam_step")
        span_ready, awh_ready, shared_hi = sem("span_ready"), sem("awh_ready"), sem("shared_hi")
        alibi_ready, aw_split, shared_split, bo_added = sem("alibi_ready"), sem("aw_split"), sem("shared_split"), sem("bo_added")
        ln_step = sem("ln_step")
        var_ready, rstd_ready, xn_ready = sem("var_ready"), sem("rstd_ready"), sem("xn_ready")
        xT_ready, xh_ready, xl_ready = sem("xT_ready"), sem("xh_ready"), sem("xl_ready")
        ctx_qk, ctx_qk_out, sim_ready, sim_out = sem("ctx_qk"), sem("ctx_qk_out"), sem("sim_ready"), sem("sim_out")
        q_ready, k_ready, v_ready = sem("q_ready"), sem("k_ready"), sem("v_ready")
        q_out, k_out, v_out = sem("q_out"), sem("k_out"), sem("v_out")
        qm_ready, s_ready, max_ready, p_ready = sem("qm_ready"), sem("s_ready"), sem("max_ready"), sem("p_ready")
        pT_ready, pT_out, pv_ready = sem("pT_ready"), sem("pT_out"), sem("pv_ready")
        o_out, oT_ready, oh_ready, ol_ready, wo_ready = (sem(n) for n in ("o_out", "oT_ready", "oh_ready", "ol_ready", "wo_ready"))
        epi_step, topk_step, tanh_ready, adj_ready, adjT_ready, adj_summed, mask_step = (
            sem(n) for n in ("epi_step", "topk_step", "tanh_ready", "adj_ready", "adjT_ready", "adj_summed", "mask_step"))
        ln3_step = sem("ln3_step")
        rw_in, sd_in, dn_in, zeroed = sem("rw_in"), sem("sd_in"), sem("dn_in"), sem("zeroed")
        lgT_out = sem("lgT_out")
        rw_split, logits_ready, route_step, top_ready, score_ready = (
            sem(n) for n in ("rw_split", "logits_ready", "route_step", "top_ready", "score_ready"))
        xs_ready, onehot_ready, counts_ready, slot_ready, tile_ready = (
            sem(n) for n in ("xs_ready", "onehot_ready", "counts_ready", "slot_ready", "tile_ready"))
        sgu_ready, sgate_ready, sh_ready, sdown_ready, sdown_added = (
            sem(n) for n in ("sgu_ready", "sgate_ready", "sh_ready", "sdown_ready", "sdown_added"))
        scattered = sem("scattered")
        xg_in = [sem(f"xg_in{i}") for i in range(3)]
        y_stored = [sem(f"y_stored{i}") for i in range(2)]
        yg_in = [sem(f"yg_in{b}") for b in range(B)]
        xg_turned, xgT_out, gu_done, rgate_ready, rh_ready, rh_turned, rhT_out, y_ready, y_out = (
            sem(n) for n in ("xg_turned", "xgT_out", "gu_done", "rgate_ready", "rh_ready", "rh_turned", "rhT_out", "y_ready", "y_out"))
        yg_added = sem("yg_added")
        head_in = [sem(f"head_in{i}") for i in range(2)]
        slopes_in, nw_in, wo_in, late_in, fb_in = sem("slopes_in"), sem("nw_in"), sem("wo_in"), sem("late_in"), sem("fb_in")
        whi_ready, vhi_ready, v_split = sem("whi_ready"), sem("vhi_ready"), sem("v_split")
        v_in = sem("v_in")
        w_split, distance_ready, slopes_negated, powers_ready, decay_ready = (
            sem(n) for n in ("w_split", "distance_ready", "slopes_negated", "powers_ready", "decay_ready"))
        qd_ready, kd_ready, vd_ready, gd_ready = sem("qd_ready"), sem("kd_ready"), sem("vd_ready"), sem("gd_ready")
        qd_out, kd_out, vd_out, gd_out = sem("qd_out"), sem("kd_out"), sem("vd_out"), sem("gd_out")
        scores_ready, masked_ready, head_ready, head_out, squared, square_added = (
            sem(n) for n in ("scores_ready", "masked_ready", "head_ready", "head_out", "squared", "square_added"))
        wo_scaled, ms_ready, rms_step, rms_ready, y1_ready, y1_added = (
            sem(n) for n in ("wo_scaled", "ms_ready", "rms_step", "rms_ready", "y1_ready", "y1_added"))
        ex_ready, pair_ready, pair_out, fa_split, late_high = (
            sem(n) for n in ("ex_ready", "pair_ready", "pair_out", "fa_split", "late_high"))
        fa_in = [sem(f"fa_in{i}") for i in range(2)]
        wo_used = sem("wo_used")
        fg_in, facol_in = sem("fg_in"), sem("facol_in")
        ln45_step = sem("ln45_step")
        fh_ready, late_low, fl1_ready = (
            sem(n) for n in ("fh_ready", "late_low", "fl1_ready"))
        up_ready, f0_out, f1_out, f_ready, f_step, choice_step, x_final = (
            sem(n) for n in ("up_ready", "f0_out", "f1_out", "f_ready", "f_step", "choice_step", "x_final"))
        out_done = sem("out_done")

        ROUNDS = -(-TOPK // 8)
        TOPK_PARTS = 2 * ROUNDS - 1
        TOPK_LINKS = TB * TOPK_PARTS
        TOPK_START = 4
        TOPK_DONE = (18, 34, 50, 64, 76)
        STEPS = B * H0
        LOW_BEFORE = 8
        TAIL = 5
        SCORE_BANKS = (0, 1, 6)
        def shared_banks(i):
            return (1, 6) if i == 0 else (1 + 2 * (i % 2), 2 + 2 * (i % 2))

        def out_bank(b, t):
            return (t, 6, 2, 6)[b]

        def norm_bank(n):
            return 6 if n == 2 * B - 2 else 4 if 2 * B <= n < 3 * B and n % 2 else 7

        EPILOGUE = ((7, "heads"), (10, "low"), (11, "adjacency"), (12, "residual"), (13, "statistics"), (15, "norm"),
                    (16, "add norm"), (17, "add adjacency"), (18, "statistics"), (21, "third norm"))

        BEFORE = 3

        SLOPES = [2.0 ** (-0.5 * (i + 1)) for i in range(H0)]

        def batch_at(n, offset):
            b, rest = divmod(n - offset, H0)
            return b - 1 if rest == 0 and 1 <= b <= B else None

        block = ctx.enter_context(nc.Block())

        def flat(ap):
            return ap.rearrange("p a b -> p (a b)")

        @block.sync
        def _(sp):
            xv = a["x"].rearrange("b (t p) e -> b p t e", p=P)
            sp.dma_start(ctxT[:], a["ctxT"]).then_inc(ctx_in, 16)
            sp.dma_start(xw[:], a["xw"]).then_inc(ctx_in, 16)
            for b in range(B):
                sp.dma_start(x[:, TB * b:TB * b + TB, :], xv[b]).then_inc(x_in[b], 16)
            for w in range(4):
                sp.dma_start(aw[:, w, :, :], a["aw"][w].rearrange("(k p) n -> p k n", p=P)).then_inc(aw_in[w], 16)
            sp.dma_start(bcol[:], a["abcol"]).then_inc(small_in, 16)
            sp.dma_start(brow[:], a["abrow"].rearrange("(o r) n -> o r n", o=1).broadcast_to([P, 2, E])).then_inc(small_in, 16)
            sp.dma_start(gam[:, 0:1], a["gamma"].broadcast_to([P, 1])).then_inc(small_in, 16)
            sp.dma_start(rw[:], a["rw"]).then_inc(rw_in, 16)
            sp.dma_start(slopes[:], a["slopes"].broadcast_to([P, H1])).then_inc(slopes_in, 16)
            sp.dma_start(nw[:], a["nw"]).then_inc(nw_in, 16)
            for e in range(NEXP - 3):
                sp.dma_start(gu[:, e], a["gu"][e].rearrange("(k p) n -> p k n", p=P)).then_inc(gu_in, 16)
            sp.wait_ge(v_ready, B)
            sp.dma_start(shared_raw[:, 0], a["sg"].rearrange("(k p) n -> p k n", p=P)).then_inc(shared_in, 16)
            sp.dma_start(shared_raw[:, 1], a["su"].rearrange("(k p) n -> p k n", p=P)).then_inc(shared_in, 16)
            sp.wait_ge(consts, 1)
            for j in range(NSLOT):
                sp.dma_start(sorted_in[j * P:(j + 1) * P, :], zero_row[:]).then_inc(zeroed, 16)
            sp.wait_ge(wo_ready, B)
            sp.wait_ge(adj_summed, B)
            for e in range(NEXP - 3, NEXP):
                sp.dma_start(gu[:, e], a["gu"][e].rearrange("(k p) n -> p k n", p=P)).then_inc(gu_in, 16)
            sp.dma_start(sd[:], a["sd"].rearrange("(f p) n -> p f n", p=P)).then_inc(sd_in, 16)
            for e in range(NEXP):
                sp.dma_start(dn[:, e], a["dn"][e].rearrange("(f p) n -> p f n", p=P)).then_inc(dn_in, 16)

            def load_head(h, i):
                if not isinstance(h, int) or h >= 2:
                    sp.wait_ge(w_split, h - 1)
                sp.dma_start(head_raw[:, i], a["heads"][ds(h, 1)].rearrange("o p k n -> p (o k) n")).then_inc(head_in[i], 16)

            def load_v(h):
                if not isinstance(h, int) or h >= 2:
                    sp.wait_ge(v_split, h)
                pair_no = h // 2
                sp.dma_start(v_raw[:], a["vpairs"][ds(pair_no, 1)].rearrange("o p k n -> p (o k) n")).then_inc(v_in, 16)

            load_head(0, 0)
            load_v(0)
            load_head(1, 1)
            def load_tile(j):
                wait_past(sp, xg_turned, j - 2)
                sp.dma_start(xg[:, j % 3, :], sorted_in[j * P:(j + 1) * P, :]).then_inc(xg_in[j % 3], 16)

            sp.wait_ge(scattered, 16 * T)
            for j in range(3):
                load_tile(j)
            for j in range(NSLOT):
                if j + 3 < NSLOT:
                    load_tile(j + 3)
                sp.wait_ge(y_out, j + 1)
                sp.dma_start(sorted_out[j * P:(j + 1) * P, :], yb[:, j % 2, :]).then_inc(y_stored[j % 2], 16)

            sp.wait_ge(yg_added, B)
            sp.wait_ge(xl_ready, 3 * B)
            sp.dma_start(wo[:], a["wo"]).then_inc(wo_in, 16)
            with sp.Fori(2, H1 - 1, 2) as h:
                load_head(h, 0)
                load_v(h)
                load_head(h + 1, 1)
            sp.wait_ge(masked_ready, 2 * H1)
            sp.dma_start(ex[:], a["ex"]).then_inc(late_in, 16)
            sp.dma_start(eb[:], a["eb"].broadcast_to([P, 1])).then_inc(late_in, 16)
            sp.dma_start(ctx2[:], a["ctxT"]).then_inc(late_in, 16)
            sp.dma_start(fb[:, 0], a["fb"][0].rearrange("(f p) n -> p f n", p=P)).then_inc(fb_in, 16)
            sp.dma_start(fb[:, 1], a["fb"][1].rearrange("(f p) n -> p f n", p=P)).then_inc(fb_in, 16)
            sp.wait_ge(head_ready, 2 * H1)
            sp.wait_ge(head_out, 2 * H1)
            for i in range(2):
                sp.dma_start(fa[:, i], a["fa"][i].rearrange("(k p) n -> p k n", p=P)).then_inc(fa_in[i], 16)
            sp.dma_start(fgrow[:], a["fg"].rearrange("(o r) n -> o r n", o=1).broadcast_to([P, 2, E])).then_inc(fg_in, 16)
            sp.dma_start(facol[:], a["facol"]).then_inc(facol_in, 16)
            sp.dma_start(fbrow[:], a["fbrow"].rearrange("(o r) n -> o r n", o=1).broadcast_to([P, 2, E])).then_inc(facol_in, 16)
            ov = out.rearrange("b (t p) e -> (b t) p e", p=P)
            for t in range(T):
                sp.wait_ge(x_final, t + 1)
                sp.dma_start(ov[t], x[:, t, :]).then_inc(out_done, 16)
            sp.wait_ge(out_done, 16 * T)

        @block.gpsimd
        def _(pool):
            step = Chain(pool, const_step)
            step(pool.memset(ones[:], 1.0))
            pool.memset(mhalf[:], -0.5)
            pool.memset(zero_row[:], 0.0)
            pool.affine_select(ident[:], ones[:], [[-1, P]], ALU.is_equal, 0.0, base=0, channel_multiplier=1)
            step(pool.memset(headmask[:], -1.0 / D0 ** 0.5))
            step(pool.affine_select(headmask[:], headmask[:], [[-D0, HB]], ALU.is_ge, 0.0, base=0, channel_multiplier=1))
            pool.affine_select(headmask[:], headmask[:], [[D0, HB]], ALU.is_ge, 0.0, base=D0 - 1, channel_multiplier=-1)
            pool.iota(rev[:], [[-1, NEXP]], base=NEXP, channel_multiplier=0, allow_small_or_imprecise_dtypes=True)
            pool.iota(steps128[:], [[P, T]], base=0, channel_multiplier=0, allow_small_or_imprecise_dtypes=True)
            pool.iota(tile_no[:], [[1, NSLOT + 1]], base=0, channel_multiplier=0, allow_small_or_imprecise_dtypes=True)
            step(pool.memset(notfirst[:], 1.0))
            pool.memset(notfirst[:, :, 0:1], 0.0)
            pool.affine_select(before[:], ones[:], [[1, P]], ALU.is_gt, 0.0, base=0, channel_multiplier=-1)\
                .then_inc(consts, 1)
            step(pool.iota(span[:], [[-1, S]], base=P, channel_multiplier=1, allow_small_or_imprecise_dtypes=True))
            pool.affine_select(span[:], span[:], [[-1, S]], ALU.is_ge, BIG, base=P, channel_multiplier=1)\
                .then_inc(span_ready, 1)

            def root(n, slot):
                pool.wait_ge(var_ready, n + 1)
                pool.tensor_tensor(rstd[:, slot], ve[:, slot], mhalf[:], ALU.pow).then_inc(rstd_ready, 1)

            root(0, 0)
            root(1, 1)
            root(2, 0)
            root(3, 1)
            for w in range(4):
                pool.wait_ge(awh_ready, w + 1)
                pool.tensor_tensor(awl[:, w], aw[:, w], awh[:, w].bitcast(F32), ALU.subtract).then_inc(aw_split, 1)

            pool.wait_ge(rw_in, 16)
            step(pool.tensor_copy(rwh[:], rw[:]))
            pool.tensor_tensor(rwl[:], rw[:], rwh[:].bitcast(F32), ALU.subtract).then_inc(rw_split, 1)
            def split_shared(i):
                w, part, k = i // (2 * K), i // K % 2, i % K
                hi, lo = ((sgh, sgl), (suh, sul))[w]
                if part == 0:
                    pool.tensor_tensor(hi[:, k], shared_raw[:, w, k], ones[:, 0:1].broadcast_to([P, FI]), ALU.mult)\
                        .then_inc(shared_hi, 1)
                else:
                    pool.wait_ge(shared_hi, w * K + K)
                    pool.tensor_tensor(lo[:, k], shared_raw[:, w, k], hi[:, k].bitcast(F32), ALU.subtract)\
                        .then_inc(shared_split, 1)

            def roots_of(b, n):
                pool.wait_ge(var_ready, b * 2 + B + 1 + n)
                pool.tensor_tensor(rstd[:, 0], ve[:, 0], mhalf[:], ALU.pow).then_inc(rstd_ready, 1)

            for n in range(STEPS + TAIL):
                b, h = divmod(n, H0)
                if n < STEPS:
                    if h == 0:
                        pool.wait_ge(q_out, b + 1)
                    wait_past(pool, s_ready, n - QM + 1)
                    pool.tensor_tensor(qm[:, n % QM, :], qT[:, h // HB, ds(b * S, S)],
                                       headmask[:, h % HB:h % HB + 1].broadcast_to([P, S]), ALU.mult)\
                        .then_inc(qm_ready, 1)
                    if h in (5, 7):
                        t = TB * b + (h - 5) // 2
                        pool.wait_ge(small_in, 48)
                        pool.wait_ge(xn_ready, TB * (b + 1))
                        pool.tensor_tensor(x[:, t, :], x[:, t, :], brow[:, 1, :], ALU.add).then_inc(bo_added, 1)
                    if b == 1 and h == 0:
                        pool.wait_ge(shared_in, 32)
                    if b == 1 and h % 2 == 0:
                        split_shared(h // 2)
                for i, offset in enumerate((17, 23)):
                    if batch_at(n, offset) is not None:
                        roots_of(batch_at(n, offset), i)
            roots_of(B - 2, 1)
            roots_of(B - 1, 0)
            roots_of(B - 1, 1)

            pool.wait_ge(zeroed, 16 * NSLOT)
            pool.wait_ge(slot_ready, 1)
            for t in range(T):
                pool.wait_ge(xs_ready, t + 1)
                pool.indirect_dma_start(out=sorted_in, out_offset=bass.IndirectOffsetOnAxis(ap=slot[:, t:t + 1], axis=0),
                                        in_=xn[:, t, :], in_offset=None).then_inc(scattered, 16)
            pool.wait_ge(y_ready, NSLOT)
            pool.iota(distance[:, 0:S], [[1, S]], base=0, channel_multiplier=-1, allow_small_or_imprecise_dtypes=True)
            step(pool.iota(distance[:, S:S + P], [[1, P]], base=0, channel_multiplier=-1, allow_small_or_imprecise_dtypes=True))
            pool.tensor_scalar(distance[:], distance[:], 0.0, None, ALU.max).then_inc(distance_ready, 1)
            for i in range(2):
                pool.wait_ge(y_stored[i], 16 * ((NSLOT + 1 - i) // 2))

            def gather(first, last):
                for t in range(first, last):
                    pool.indirect_dma_start(out=yg[:, t, :], out_offset=None, in_=sorted_out,
                                            in_offset=bass.IndirectOffsetOnAxis(ap=slot[:, t:t + 1], axis=0))\
                        .then_inc(yg_in[t // TB], 16)

            gather(0, 4)
            root(3 * B, 0)
            gather(4, 6)
            root(3 * B + 1, 1)
            gather(6, T)

            def split_head(h, i):
                if isinstance(h, int) and h < 2:
                    pool.wait_ge(head_in[i], 16)
                    if h == 0:
                        pool.wait_ge(sdown_ready, B)
                else:
                    pool.wait_ge(head_in[i], 8 * (h - i) + 16)
                    pool.wait_ge(gd_ready, h - 1)
                if not isinstance(h, int) or h > 0:
                    pool.tensor_tensor(wh[:, i].rearrange("p k n -> p (k n)"), head_raw[:, i].rearrange("p k n -> p (k n)"),
                                       ones[:, 0:1].broadcast_to([P, K * 3 * D1]), ALU.mult).then_inc(whi_ready, 1)
                pool.wait_ge(whi_ready, h + 1)
                pool.tensor_tensor(wl[:, i], head_raw[:, i], wh[:, i].bitcast(F32), ALU.subtract).then_inc(w_split, 1)

            def split_v(h):
                pool.wait_ge(v_in, 8 * h + 16)
                if not isinstance(h, int) or h >= 2:
                    pool.wait_ge(vd_ready, h)
                if not isinstance(h, int) or h > 0:
                    pool.tensor_tensor(vh[:].rearrange("p k n -> p (k n)"), v_raw[:].rearrange("p k n -> p (k n)"),
                                       ones[:, 0:1].broadcast_to([P, K * 2 * D1]), ALU.mult).then_inc(vhi_ready, 2)
                pool.wait_ge(vhi_ready, h + 2)
                pool.tensor_tensor(vl[:], v_raw[:], vh[:].bitcast(F32), ALU.subtract).then_inc(v_split, 2)

            def add_squares(h):
                for half in range(2):
                    pool.wait_ge(squared, 2 * h + half + 1)
                    pool.tensor_tensor(square_sum[:, half], square_sum[:, half], squares[:, half], ALU.add)\
                        .then_inc(square_added, 1)

            split_head(0, 0)
            root(3 * B + 2, 0)
            split_v(0)
            root(3 * B + 3, 1)
            pool.wait_ge(powers_ready, H1)
            pool.affine_select(decay[:, :, 0:S], decay[:, :, 0:S], [[0, H1], [1, S]], ALU.is_ge, 0.0, base=0, channel_multiplier=-1)
            pool.affine_select(decay[:, :, S:S + P], decay[:, :, S:S + P], [[0, H1], [1, P]], ALU.is_ge, 0.0, base=0,
                               channel_multiplier=-1).then_inc(decay_ready, 1)
            split_head(1, 1)
            pool.wait_ge(xl_ready, 3 * B)
            step(pool.memset(square_sum[:], 0.0))
            split_head(2, 0)
            split_v(2)
            add_squares(0)
            split_head(3, 1)
            add_squares(1)
            pool.wait_ge(wo_in, 16)
            pool.wait_ge(nw_in, 16)
            step(pool.tensor_scalar(nw[:], nw[:], 0.5, None, ALU.mult))
            pool.tensor_tensor(wo[:], wo[:], nw[:].unsqueeze(2).broadcast_to([P, H1, E]), ALU.mult).then_inc(wo_scaled, 1)
            with pool.Fori(2, H1 - 2, 2) as h:
                split_head(h + 2, 0)
                split_v(h + 2)
                add_squares(h)
                split_head(h + 3, 1)
                add_squares(h + 1)
            add_squares(H1 - 2)
            add_squares(H1 - 1)
            def split_up(i):
                pool.wait_ge(late_high, i + 2)
                pool.tensor_tensor(fal[:, i], fa[:, i], fah[:, i].bitcast(F32), ALU.subtract).then_inc(fa_split, 1)

            split_up(0)
            pool.wait_ge(rms_step, 1)
            pool.memset(rhalf[:], -0.5).then_inc(rms_step, 1)
            pool.wait_ge(rms_step, 2)
            pool.tensor_tensor(rms[:], ms[:], rhalf[:], ALU.pow).then_inc(rms_ready, 1)
            split_up(1)

            def split_down(i):
                pool.wait_ge(late_high, 5)
                pool.tensor_tensor(fbl[i][:], fb[:, i], fbh[:, i].bitcast(F32), ALU.subtract).then_inc(fa_split, 1)

            def relu_low(b):
                pool.wait_ge(fh_ready, 2 * b + 2)
                wait_past(pool, f_ready, 2 * b - 2)
                pool.tensor_tensor(fl[:, b % 2, 1], f1[:, b % 2], fh[:, b % 2, 1].bitcast(F32), ALU.subtract)\
                    .then_inc(fl1_ready, 1)

            for b in range(B):
                if b == 2:
                    split_down(0)
                    split_down(1)
                root(4 * B + 2 * b, b % 2)
                if b == B - 1:
                    relu_low(0)
                root(4 * B + 2 * b + 1, b % 2)
            relu_low(1)
            relu_low(2)

        @block.vector
        def _(dve):
            ln = Chain(dve, ln_step)

            def norm_stats(link, src, slot, n_sem=var_ready):
                for t in range(TB):
                    last = dve.bn_stats(stats[:, slot, t, :], src[t])
                link(last)
                for t in range(TB):
                    last = dve.bn_aggr(mv[:, slot, t, :], stats[:, slot, t, :])
                link(last)
                dve.tensor_scalar(ve[:, slot, :], mv[:, slot, :, 1], EPS, None, ALU.add).then_inc(var_ready, 1)

            def normalise(dst, src, slot):
                for t in range(TB):
                    last = dve.tensor_scalar(dst[t], src[t], mv[:, slot, t, 0:1], rstd[:, slot, t:t + 1],
                                             ALU.subtract, ALU.mult)
                return last

            def tiles(buf, b):
                return [buf[:, TB * b + t, :] for t in range(TB)]

            def low_part(n, b):
                dve.wait_ge(xh_ready, n + 1)
                dve.tensor_tensor(xl[:, :, b * S:(b + 1) * S], ps[norm_bank(n)][:].rearrange("p (k s) -> p k s", k=K),
                                  xh[:, :, b * S:(b + 1) * S].bitcast(F32), ALU.subtract).then_inc(xl_ready, 1)

            def topk_part(b, r):
                base = b * TOPK_LINKS + TB * r
                if r == 0:
                    dve.wait_ge(sim_out, b + 1)
                for j in range(TB):
                    left = sim[:, b * TB + j, :] if r < 2 else work[:, j, :]
                    if r % 2 == 0:
                        wait_past(dve, topk_step, base if j == 0 else 0)
                        dve.max(top8[:, b * TB + j, :], left).then_inc(topk_step, 1)
                    else:
                        dve.wait_ge(topk_step, base - 1 + j)
                        dve.match_replace(work[:, j, :], top8[:, b * TB + j, :], left, -3.0e38).then_inc(topk_step, 1)

            def topk_parts(first, last):
                for r in range(first, last):
                    topk_part(*divmod(r, TOPK_PARTS))

            for b in range(B + 1):
                if b < B:
                    dve.wait_ge(x_in[b], 16)
                    norm_stats(ln, tiles(x, b), b % 2)
                if b >= 1:
                    dve.wait_ge(rstd_ready, b)
                    normalise(tiles(xn, b - 1), tiles(x, b - 1), (b - 1) % 2).then_inc(xn_ready, TB)
            dve.wait_ge(small_in, 48)
            low_part(0, 0)
            for b in range(B):
                if b + 1 < B:
                    low_part(b + 1, b + 1)
                if b < B - 1:
                    topk_parts(TOPK_DONE[0] * b // (B - 1), TOPK_DONE[0] * (b + 1) // (B - 1))
                dve.wait_ge(v_ready, b + 1)
                dve.tensor_tensor(v[:, TB * b:TB * b + TB, :], ps[2][:].rearrange("p (t e) -> p t e", t=TB),
                                  brow[:, 0:1, :].broadcast_to([P, TB, E]), ALU.add).then_inc(v_out, 1)
            dve.wait_ge(slopes_in, 16)
            dve.tensor_scalar(slopes[:], slopes[:], -1.0, None, ALU.mult).then_inc(slopes_negated, 1)
            gs = Chain(dve, gam_step, 1)
            dve.wait_ge(gam_step, 1)
            gs(dve.tensor_scalar(gam[:, 1:2], gam[:, 1:2], 1.0, None, ALU.add))
            gs(dve.reciprocal(gam[:, 2:3], gam[:, 1:2]))
            dve.tensor_scalar(gam[:, 1:2], gam[:, 2:3], -1.0, 1.0, ALU.mult, ALU.add)
            gs(dve.tensor_scalar(gam[:, 3:4], gam[:, 2:3], 0.25, None, ALU.mult))

            def reached_threshold(b):
                at = (TOPK - 1) % 8
                dve.wait_ge(topk_step, (b + 1) * TOPK_LINKS)
                for t in range(TB):
                    last = dve.tensor_scalar(mask[:, t, :], sim[:, ds(b * TB + t, 1), :], top8[:, b * TB + t, at:at + 1], None,
                                             ALU.is_ge)
                last.then_inc(mask_step, 1)

            def sparse_adjacency(b):
                dve.wait_ge(mask_step, b + 1)
                dve.wait_ge(tanh_ready, b + 1)
                dve.scalar_tensor_tensor(flat(adj[:]), flat(tanh_sim[:]), 1.0, flat(mask[:]), ALU.add, ALU.mult)\
                    .then_inc(adj_ready, 1)

            def epilogue(b, part, link):
                xb = x[:, ds(b * TB, TB), :]
                if part == "heads":
                    dve.wait_ge(p_ready, b * H0 + H0)
                    link(dve.reciprocal(prec[:], psums[:, b % 2]))
                    dve.wait_ge(pv_ready, b * H0 + H0)
                    dve.tensor_tensor(on[:].rearrange("p t (h d) -> p (t h) d", h=H0),
                                      ps[4 + b % 2][:].rearrange("p (a d) -> p a d", d=D0),
                                      flat(prec[:]).unsqueeze(2).broadcast_to([P, TB * H0, D0]),
                                      ALU.mult).then_inc(o_out, 1)
                elif part == "low":
                    dve.wait_ge(oh_ready, b + 1)
                    dve.tensor_tensor(flat(ol[:]), ps[7][:], flat(oh[:]).bitcast(F32), ALU.subtract).then_inc(ol_ready, 1)
                elif part == "adjacency":
                    dve.wait_ge(adjT_ready, b + 1)
                    dve.tensor_tensor(flat(adj_sum[:]), ps[4 + b % 2][:], flat(adj[:]), ALU.add)\
                        .then_inc(adj_summed, 1)
                elif part == "residual":
                    dve.wait_ge(bo_added, TB * (b + 1))
                    dve.wait_ge(wo_ready, b + 1)
                    link(dve.tensor_tensor(xb, ps[7][:].rearrange("p (t e) -> p t e", t=TB), xb, ALU.add))
                elif part == "statistics":
                    norm_stats(link, [x[:, ds(b * TB + t, 1), :] for t in range(TB)], 0)
                elif part == "norm":
                    dve.wait_ge(rstd_ready, b * 2 + B + 1)
                    link(normalise([on[:, t, :] for t in range(TB)], [x[:, ds(b * TB + t, 1), :] for t in range(TB)], 0))
                elif part == "add norm":
                    link(dve.scalar_tensor_tensor(xb, on[:], gam[:, 1:2], xb, ALU.mult, ALU.add))
                elif part == "add adjacency":
                    link(dve.scalar_tensor_tensor(xb, adj_sum[:], gam[:, 3:4], xb, ALU.mult, ALU.add))
                else:
                    dve.wait_ge(rstd_ready, b * 2 + B + 2)
                    normalise([xn[:, ds(b * TB + t, 1), :] for t in range(TB)],
                              [x[:, ds(b * TB + t, 1), :] for t in range(TB)], 0).then_inc(xn_ready, TB)

            def shared_hidden(i):
                dve.wait_ge(sgate_ready, i + 1)
                wait_past(dve, sdown_ready, (i // FB) * 2)
                dve.tensor_tensor(hT[:, i % FB, :], ps[shared_banks(i)[1]][:], gate[:, i % 2, :], ALU.mult)\
                    .then_inc(sh_ready, 1)

            def shared_added(b):
                dve.wait_ge(sdown_ready, b + 1)
                dve.tensor_tensor(x[:, TB * b:TB * b + TB, :], ps[5 + b % 2][:].rearrange("p (t e) -> p t e", t=TB),
                                  x[:, TB * b:TB * b + TB, :], ALU.add).then_inc(sdown_added, 1)

            link = Chain(dve, epi_step)
            for n in range(STEPS + TAIL):
                b, h = divmod(n, H0)
                for offset, part in EPILOGUE:
                    if batch_at(n, offset) is not None:
                        epilogue(batch_at(n, offset), part, link)
                if batch_at(n, 24) is not None:
                    low_part(B + batch_at(n, 24), batch_at(n, 24))
                if n >= STEPS:
                    continue
                dve.wait_ge(s_ready, n + 1)
                wait_past(dve, pT_ready, n - PR + 1)
                if b == 0:
                    dve.wait_ge(alibi_ready, h + 1)
                bank = ps[SCORE_BANKS[n % 3]]
                dve.tensor_tensor_reduce(pr[:, n % PR, 0:P], bank[:, 0:P], alibi[:, h, P:2 * P], 1.0, 3.0e38,
                                         ALU.add, ALU.min, nmax[:, n % PR, 0:1])
                dve.tensor_tensor_reduce(pr[:, n % PR, P:3 * P], bank[:, P:3 * P], alibi[:, h, :], 1.0, 3.0e38,
                                         ALU.add, ALU.min, nmax[:, n % PR, 1:2]).then_inc(max_ready, 1)
                if h < H0 - 2:
                    start = 0 if b else TOPK_START
                    first, parts, steps = TOPK_DONE[b], TOPK_DONE[b + 1] - TOPK_DONE[b], H0 - 2 - start
                    if h >= start:
                        topk_parts(first + parts * (h - start) // steps, first + parts * (h - start + 1) // steps)
                elif h == H0 - 2:
                    reached_threshold(b)
                else:
                    sparse_adjacency(b)

            epilogue(B - 1, "heads", link)
            epilogue(B - 2, "third norm", link)
            epilogue(B - 1, "low", link)
            shared_hidden(0)
            low_part(2 * B - 2, B - 2)
            for part in ("adjacency", "residual", "statistics", "norm", "add norm"):
                epilogue(B - 1, part, link)
            shared_hidden(1)
            for part in ("add adjacency", "statistics"):
                epilogue(B - 1, part, link)
            shared_hidden(2)
            epilogue(B - 1, "third norm", link)
            shared_hidden(3)
            low_part(2 * B - 1, B - 1)

            dve.wait_ge(logits_ready, 2)
            dve.tensor_copy(lgT[:, HALF:2 * HALF], ps[7][0:NEXP, :]).then_inc(lgT_out, 1)
            link = Chain(dve, route_step)
            dve.wait_ge(logits_ready, 3)
            link(dve.tensor_copy(lg[:], ps[0][:, 0:T * NEXP].rearrange("p (t e) -> p t e", t=T)))
            dve.tensor_reduce(toplg[:], lg[:], X, ALU.max).then_inc(top_ready, 1)
            dve.wait_ge(top_ready, 1)
            link(dve.tensor_tensor(hit[:], lg[:], toplg[:].unsqueeze(2).broadcast_to([P, T, NEXP]), ALU.is_equal))
            link(dve.tensor_tensor(hit[:], hit[:], rev[:].unsqueeze(1).broadcast_to([P, T, NEXP]), ALU.mult))
            link(dve.tensor_reduce(which[:], hit[:], X, ALU.max))
            dve.tensor_tensor(onehot[:].rearrange("p e t -> p t e"), rev[:].unsqueeze(1).broadcast_to([P, T, NEXP]),
                              which[:].unsqueeze(2).broadcast_to([P, T, NEXP]), ALU.is_equal).then_inc(onehot_ready, 1)

            dve.wait_ge(counts_ready, 1)
            total = ps[0][:, 128:128 + T * NEXP]
            link(dve.tensor_tensor_scan(flat(upto[:]), flat(notfirst[:]), total, 0.0, ALU.mult, ALU.add))
            link(dve.tensor_tensor(flat(place[:]), flat(upto[:]), total, ALU.subtract))
            link(dve.tensor_tensor(flat(place[:]), ps[0][:, 64:64 + T * NEXP], flat(place[:]), ALU.add))
            link(dve.tensor_tensor(cmp[:], upto[:, :, T - 1:T].broadcast_to([P, NEXP, T]),
                                   steps128[:].unsqueeze(1).broadcast_to([P, NEXP, T]), ALU.is_gt))
            link(dve.tensor_reduce(ntiles[:], cmp[:], X, ALU.add))
            link(dve.tensor_tensor_scan(ends[:], ones[:, 0:NEXP], ntiles[:], 0.0, ALU.mult, ALU.add))
            link(dve.tensor_tensor(starts[:], ends[:], ntiles[:], ALU.subtract))
            link(dve.scalar_tensor_tensor(place[:], starts[:].unsqueeze(2).broadcast_to([P, NEXP, T]), float(P), place[:],
                                          ALU.mult, ALU.add))
            link(dve.tensor_tensor(place[:], place[:], onehot[:], ALU.mult))
            link(dve.tensor_reduce(slotf[:], place[:].rearrange("p e t -> p t e"), X, ALU.add))
            dve.tensor_copy(slot[:], slotf[:]).then_inc(slot_ready, 1)
            link(dve.tensor_tensor(cmp2[:], ends[0:1, :].unsqueeze(1).broadcast_to([1, NSLOT + 1, NEXP]),
                                   tile_no[:].unsqueeze(2).broadcast_to([1, NSLOT + 1, NEXP]), ALU.is_le))
            link(dve.tensor_reduce(tilef[:], cmp2[:], X, ALU.add))
            dve.tensor_scalar(tile_expert[:], tilef[:], float(NEXP - 1), None, ALU.min).then_inc(tile_ready, 1)
            shared_added(0)
            shared_added(1)
            for i in range(FB, FB + BEFORE):
                shared_hidden(i)
            def routed_hidden(j):
                dve.wait_ge(rgate_ready, j + 1)
                wait_past(dve, rh_turned, j - 1)
                dve.tensor_tensor(rh[:, j % 2], ps[2 + 4 * (j % 2)][:], rgate[:, j % 2], ALU.mult).then_inc(rh_ready, 1)

            def routed_out(j):
                dve.wait_ge(y_ready, j + 1)
                wait_past(dve, y_stored[j % 2], 16 * (j // 2))
                dve.tensor_copy(yb[:, j % 2, :], ps[4][:, 0:E]).then_inc(y_out, 1)

            for j in range(NSLOT + 2):
                if j < NSLOT:
                    routed_hidden(j)
                if j >= 2:
                    routed_out(j - 2)
            for i in range(FB + BEFORE, 2 * FB):
                shared_hidden(i)
            ln3 = Chain(dve, ln3_step)

            def add_routed(b):
                if b >= 2:
                    shared_added(b)
                dve.wait_ge(yg_in[b], 16 * TB)
                dve.wait_ge(sdown_added, b + 1)
                dve.tensor_tensor(x[:, TB * b:TB * b + TB, :], x[:, TB * b:TB * b + TB, :],
                                  yg[:, TB * b:TB * b + TB, :], ALU.add).then_inc(yg_added, 1)
                dve.wait_ge(yg_added, b + 1)

            def routed_statistics(b):
                add_routed(b)
                norm_stats(ln3, tiles(x, b), b % 2)

            def fourth_norm(b):
                dve.wait_ge(rstd_ready, 3 * B + b + 1)
                normalise(tiles(xn, b), tiles(x, b), b % 2).then_inc(xn_ready, TB)

            routed_statistics(0)
            routed_statistics(1)
            fourth_norm(0)
            fourth_norm(1)
            low_part(2 * B, 0)
            routed_statistics(2)
            low_part(2 * B + 1, 1)
            fourth_norm(2)
            routed_statistics(3)
            low_part(2 * B + 2, 2)
            fourth_norm(3)
            low_part(2 * B + 3, 3)

            def mask_scores(h, i):
                for p in range(2):
                    dve.wait_ge(scores_ready, 2 * h + p + 1)
                    wait_past(dve, head_ready, 2 * h + p - 1)
                    dve.tensor_tensor(masked[:, p], banks[:, 4:6, 0:S + P],
                                      decay[:, ds(h, 1), :].broadcast_to([P, TB, S + P]), ALU.mult).then_inc(masked_ready, 1)

            def gate_head(h, i):
                dve.wait_ge(gd_out, h + 1)
                for p in range(2):
                    dve.wait_ge(head_ready, 2 * h + p + 1)
                    dve.scalar_tensor_tensor(heads[:, ds(h, 1), p * HALF:(p + 1) * HALF], gd[:, i, p * HALF:(p + 1) * HALF],
                                             1.0, ps[6 + p][:], ALU.add, ALU.mult).then_inc(head_out, 1)

            dve.wait_ge(decay_ready, 1)
            for h in (0, 1):
                mask_scores(h, h % 2)
                gate_head(h, h % 2)
            with dve.Fori(2, H1 - 2, 2) as h:
                for i in range(2):
                    mask_scores(h + i, i)
                    gate_head(h + i, i)
            for h in (H1 - 2, H1 - 1):
                mask_scores(h, h % 2)
                gate_head(h, h % 2)
            dve.wait_ge(late_in, 48)
            dve.tensor_scalar(wj[:], ones[0:C, :], ex[:, 1:2], None, ALU.mult).then_inc(ex_ready, 1)
            dve.wait_ge(pair_ready, T)
            dve.tensor_scalar(si[:], ps[3][:, 0:T], eb[:, 0:1], None, ALU.add).then_inc(ex_ready, 1)

            def heads_low(b, half):
                hs = slice(half * H1 // 2, (half + 1) * H1 // 2)
                own, high = slice(b * S, (b + 1) * S), slice((b - 2) * S, (b - 1) * S)
                dve.tensor_tensor(head_parts[:, hs, own], heads[:, hs, own], head_parts[:, hs, high].bitcast(F32), ALU.subtract)\
                    .then_inc(late_low, 1)

            dve.wait_ge(late_high, 4)
            heads_low(2, 0)
            dve.wait_ge(ms_ready, T)
            dve.tensor_scalar(ms[:], ps[2][:, 0:T], 1.0 / (H1 * D1), 1e-6, ALU.mult, ALU.add).then_inc(rms_step, 1)
            heads_low(2, 1)
            dve.wait_ge(rms_ready, 1)
            l45 = Chain(dve, ln45_step)

            def add_linear(b):
                dve.wait_ge(y1_ready, b + 1)
                for t in range(TB):
                    last = dve.scalar_tensor_tensor(x[:, TB * b + t, :], ps[out_bank(b, t)][:, t * E:(t + 1) * E],
                                                    rms[:, TB * b + t:TB * b + t + 1], x[:, TB * b + t, :], ALU.mult, ALU.add)
                last.then_inc(y1_added, 1)
                dve.wait_ge(y1_added, b + 1)

            def add_pair(b):
                dve.wait_ge(rstd_ready, 4 * B + 2 * b + 1)
                l45(normalise(tiles(xn, b), tiles(x, b), b % 2))
                xb = x[:, TB * b:TB * b + TB, :]
                l45(dve.scalar_tensor_tensor(xb, xn[:, TB * b:TB * b + TB, :], 1.0 - 0.6, xb, ALU.mult, ALU.add))
                dve.wait_ge(pair_out, TB * b + TB)
                l45(dve.scalar_tensor_tensor(xb, pair[:, TB * b:TB * b + TB, :], 0.6, xb, ALU.mult, ALU.add))

            def relu_hidden(b):
                dve.wait_ge(up_ready, 2 * b + 2)
                wait_past(dve, fl1_ready, b - 1)
                for m in range(FB):
                    last = dve.tensor_scalar(f1[:, b % 2, m, :], ps[4 + m // 2][:, (m % 2) * S:(m % 2 + 1) * S],
                                             facol[:, FB + m:FB + m + 1], 0.0, ALU.add, ALU.max)
                last.then_inc(f1_out, 1)

            def combine(b):
                for t in range(TB):
                    dve.wait_ge(f_ready, 2 * b + t + 1)
                    bank, xt, pick = ps[2 + 4 * (b % 2) + t], x[:, TB * b + t, :], choice[:, TB * b + t, :]
                    f_link(dve.tensor_tensor(y[:, t], bank.rearrange("p (i e) -> p i e", i=2), fbrow[:], ALU.add))
                    f_link(dve.scalar_tensor_tensor(xt, y[:, t, 0, :], pick[:, 0:1], xt, ALU.mult, ALU.add))
                    dve.scalar_tensor_tensor(xt, y[:, t, 1, :], pick[:, 1:2], xt, ALU.mult, ALU.add).then_inc(x_final, 1)

            def choose(b):
                dve.wait_ge(xn_ready, TB * (3 * B + b + 1))
                dve.wait_ge(fg_in, 16)
                for t in range(TB * b, TB * b + TB):
                    for e in range(2):
                        last = dve.tensor_tensor_reduce(junk[:], xn[:, t, :], fgrow[:, e, :], 1.0, 0.0, ALU.mult, ALU.add,
                                                        lg2[:, t, e:e + 1])
                        ch(last)
                tb = slice(TB * b, TB * b + TB)
                ch(dve.tensor_tensor(choice[:, tb, 0:1], lg2[:, tb, 0:1], lg2[:, tb, 1:2], ALU.is_ge))
                ch(dve.tensor_scalar(choice[:, tb, 1:2], choice[:, tb, 0:1], -1.0, 1.0, ALU.mult, ALU.add))

            def gelu_low(b):
                dve.wait_ge(fh_ready, 2 * b + 1)
                wait_past(dve, f_ready, 2 * b - 2)
                dve.tensor_tensor(fl[:, b % 2, 0], f0[:, b % 2], fh[:, b % 2, 0].bitcast(F32), ALU.subtract)\
                    .then_inc(late_low, 1)
                if b == B - 1:
                    dve.wait_ge(fh_ready, 2 * B)
                    dve.wait_ge(fl1_ready, B - 1)
                    dve.tensor_tensor(fl[:, b % 2, 1], f1[:, b % 2], fh[:, b % 2, 1].bitcast(F32), ALU.subtract)\
                        .then_inc(fl1_ready, 1)

            f_link, ch = Chain(dve, f_step), Chain(dve, choice_step)
            def weights_low(q):
                if q < 3:
                    dve.wait_ge(wo_used, q + 1)
                else:
                    dve.wait_ge(y1_ready, 2)
                part = slice(q * H1 // 4, (q + 1) * H1 // 4)
                dve.tensor_tensor(wol[:, part, :], wo[:, part, :], woh[:, part, :].bitcast(F32), ALU.subtract).then_inc(late_low, 1)

            def second_norms(n):
                add_linear(n)
                norm_stats(l45, tiles(x, n), n % 2)
                if n == 0:
                    weights_low(0)
                if n == B - 1:
                    low_part(3 * B + n - 1, n - 1)
                    gelu_low(0)
                add_pair(n)
                norm_stats(l45, tiles(x, n), n % 2)
                if n == 0:
                    weights_low(1)
                if n == 1:
                    low_part(3 * B, 0)
                dve.wait_ge(rstd_ready, 4 * B + 2 * n + 2)
                normalise(tiles(xn, n), tiles(x, n), n % 2).then_inc(xn_ready, TB)

            second_norms(0)
            for q in (2, 3):
                weights_low(q)
            second_norms(1)
            dve.wait_ge(late_high, 6)
            heads_low(3, 0)
            heads_low(3, 1)
            choose(0)
            dve.wait_ge(facol_in, 32)
            second_norms(2)
            low_part(3 * B + 1, 1)
            relu_hidden(0)
            second_norms(3)
            relu_hidden(1)
            gelu_low(1)
            low_part(3 * B + 3, 3)
            choose(1)
            choose(2)
            combine(0)
            choose(3)
            relu_hidden(2)
            gelu_low(2)
            combine(1)
            relu_hidden(3)
            gelu_low(3)
            combine(2)
            combine(3)

        @block.scalar
        def _(act):
            def high_part(n, b):
                act.wait_ge(xT_ready, n + 1)
                act.activation(xh[:, :, b * S:(b + 1) * S], ps[norm_bank(n)][:].rearrange("p (k s) -> p k s", k=K), ACT.Copy)\
                    .then_inc(xh_ready, 1)

            def distances(first, last):
                for h in range(first, last):
                    act.activation(alibi[:, h, :], span[:], ACT.Copy, scale=SLOPES[h]).then_inc(alibi_ready, 1)

            act.wait_ge(span_ready, 1)
            distances(0, 8)
            for i, dst in enumerate((cQ, cQ, cK, cK)):
                act.wait_ge(ctx_qk, i + 1)
                act.activation(dst[:, (i % 2) * 512:(i % 2) * 512 + 512], ps[3 + i][0:C, :], ACT.Copy)\
                    .then_inc(ctx_qk_out, 1)

            def weight_high(w):
                act.wait_ge(aw_in[w], 16)
                act.activation(awh[:, w], aw[:, w], ACT.Copy).then_inc(awh_ready, 1)

            for w in range(3):
                weight_high(w)
            act.wait_ge(small_in, 48)
            act.activation(gam[:, 1:2], gam[:, 0:1], ACT.Exp, scale=-1.0).then_inc(gam_step, 1)

            def project_out(b):
                for bank, s_in, dst, s_out, col in ((0, q_ready, qT, q_out, 0), (1, k_ready, kT, k_out, K)):
                    act.wait_ge(s_in, b + 1)
                    for k in range(K):
                        last = act.activation(dst[:, k, b * S:(b + 1) * S], ps[bank][:, k * S:(k + 1) * S], ACT.Identity,
                                              bias=bcol[:, col + k:col + k + 1])
                    last.then_inc(s_out, 1)

            high_part(0, 0)
            for i in range(B):
                act.wait_ge(sim_ready, i + 1)
                act.activation(sim[:, TB * i:TB * i + TB, :], ps[3 + i][:].rearrange("p (t s) -> p t s", t=TB), ACT.Copy,
                               scale=1.0 / 16).then_inc(sim_out, 1)
            for b in range(B):
                if b + 1 < B:
                    high_part(b + 1, b + 1)
                project_out(b)
            weight_high(3)
            distances(8, H0)

            def oT_high(b):
                act.wait_ge(oT_ready, b + 1)
                act.activation(flat(oh[:]), ps[7][:], ACT.Copy).then_inc(oh_ready, 1)

            def shared_gate(i):
                act.wait_ge(sgu_ready, i + 1)
                wait_past(act, sh_ready, i - 1)
                act.activation(gate[:, i % 2, :], ps[shared_banks(i)[0]][:], ACT.Silu).then_inc(sgate_ready, 1)

            for n in range(STEPS + TAIL):
                b, h = divmod(n, H0)
                if batch_at(n, 9) is not None:
                    oT_high(batch_at(n, 9))
                if batch_at(n, 23) is not None:
                    act.wait_ge(shared_split, 2 * K)
                    high_part(B + batch_at(n, 23), batch_at(n, 23))
                if n < STEPS:
                    if h == 0:
                        wait_past(act, o_out, b - 1)
                    act.wait_ge(max_ready, n + 1)
                    act.activation(pr[:, n % PR, 0:P], pr[:, n % PR, 0:P], ACT.Exp, scale=-1.0,
                                   bias=nmax[:, n % PR, 0:1], accum_out=psums[:, b % 2, 0, h:h + 1])
                    act.activation(pr[:, n % PR, P:3 * P], pr[:, n % PR, P:3 * P], ACT.Exp, scale=-1.0,
                                   bias=nmax[:, n % PR, 1:2], accum_out=psums[:, b % 2, 1, h:h + 1]).then_inc(p_ready, 1)
                if 3 <= n < STEPS + 3:
                    act.wait_ge(pT_ready, n - 2)
                    wait_past(act, pv_ready, n - 4)
                    act.activation(prT[:, (n - 3) % 2, :], ps[2 + (n - 3) % 2][:, 0:3 * P], ACT.Copy).then_inc(pT_out, 1)
                if n < STEPS and h == 8:
                    wait_past(act, adj_ready, b)
                    act.activation(tanh_sim[:], sim[:, ds(b * TB, TB), :], ACT.Tanh, scale=0.5).then_inc(tanh_ready, 1)
            shared_gate(0)
            oT_high(B - 1)
            high_part(2 * B - 2, B - 2)
            for i in range(1, FB):
                shared_gate(i)

            act.wait_ge(logits_ready, 1)
            act.activation(lgT[:, 0:HALF], ps[0][0:NEXP, :], ACT.Copy).then_inc(lgT_out, 1)
            high_part(2 * B - 1, B - 1)
            act.wait_ge(top_ready, 1)
            act.activation(score[:], toplg[:], ACT.Sigmoid).then_inc(score_ready, 1)
            act.wait_ge(score_ready, 1)
            for t in range(T):
                act.activation(xn[:, t, :], xn[:, t, :], ACT.Copy, scale=score[:, t:t + 1]).then_inc(xs_ready, 1)

            for i in range(FB, FB + BEFORE):
                shared_gate(i)

            def turned_rows(j):
                act.wait_ge(xg_turned, j + 1)
                wait_past(act, gu_done, j - 1)
                act.activation(xgT[:, j % 2].rearrange("p k r -> p (k r)"), ps[0][:, 0:E], ACT.Copy).then_inc(xgT_out, 1)

            def routed_gate(j):
                act.wait_ge(gu_done, j + 1)
                wait_past(act, rh_ready, j - 1)
                act.activation(rgate[:, j % 2], ps[1 + 4 * (j % 2)][:], ACT.Silu).then_inc(rgate_ready, 1)

            def turned_hidden(j):
                act.wait_ge(rh_turned, j + 1)
                wait_past(act, y_ready, j - 1)
                act.activation(flat(rhT[:, j % 2]), ps[3 + 4 * (j % 2)][:], ACT.Copy).then_inc(rhT_out, 1)

            turned_rows(0)
            for j in range(NSLOT + 1):
                if j < NSLOT:
                    routed_gate(j)
                if j + 1 < NSLOT:
                    turned_rows(j + 1)
                if j >= 1:
                    turned_hidden(j - 1)
            for i in range(FB + BEFORE, 2 * FB):
                shared_gate(i)
            act.wait_ge(slopes_negated, 1)
            act.wait_ge(distance_ready, 1)
            def powers(first, last):
                for h in range(first, last):
                    act.activation(decay[:, h, :], distance[:], ACT.Exp, scale=slopes[:, h:h + 1]).then_inc(powers_ready, 1)

            powers(0, 8)
            act.wait_ge(sdown_ready, B)
            act.wait_ge(head_in[0], 16)
            act.activation(wh[:, 0], head_raw[:, 0], ACT.Copy).then_inc(whi_ready, 1)
            act.wait_ge(v_in, 16)
            act.activation(vh[:], v_raw[:], ACT.Copy).then_inc(vhi_ready, 2)
            for b in range(B):
                high_part(2 * B + b, b)
                powers(8 + H1 // 2 * b // B, 8 + H1 // 2 * (b + 1) // B)

            def evacuate(h, i, what):
                pair_a, pair_b = banks[:, 0:2, :], banks[:, 2:4, :]
                if what == "q":
                    act.wait_ge(qd_ready, h + 1)
                    wait_past(act, scores_ready, 2 * h - 2)
                    act.activation(qd[:, i].rearrange("p (c n) -> p c n", c=2), pair_a, ACT.Silu).then_inc(qd_out, 1)
                elif what == "k":
                    act.wait_ge(kd_ready, h + 1)
                    wait_past(act, scores_ready, 2 * h - 2)
                    act.activation(kd[:, i].rearrange("p (c n) -> p c n", c=2), pair_b, ACT.Silu).then_inc(kd_out, 1)
                else:
                    act.wait_ge(gd_ready, h + 1)
                    wait_past(act, head_out, 2 * h - 2)
                    act.activation(gd[:, i].rearrange("p (c n) -> p c n", c=2), pair_b, ACT.Tanh, scale=0.5).then_inc(gd_out, 1)

            def evacuate_v(h, u):
                act.wait_ge(vd_ready, h + u + 1)
                wait_past(act, head_ready, 2 * h - 1 + u)
                act.activation(vd[:, 4 * u:4 * u + 4, :].rearrange("p (c t) d -> p c (t d)", c=2), banks[:, 0:2, :],
                               ACT.Silu).then_inc(vd_out, 1)

            def square(h, p):
                act.wait_ge(head_out, 2 * h + p + 1)
                wait_past(act, square_added, 2 * h + p - 1)
                act.activation(squares[:, p, :], ps[6 + p][:], ACT.Square).then_inc(squared, 1)

            def unit(h, i):
                evacuate(h + 1, 1 - i, "q")
                evacuate(h + 1, 1 - i, "k")
                square(h, 0)
                if i == 0:
                    evacuate(h + 1, 1 - i, "g")
                    square(h, 1)
                else:
                    evacuate_v(h + 1, 0)
                    square(h, 1)
                    evacuate_v(h + 1, 1)
                    evacuate(h + 1, 1 - i, "g")

            evacuate(0, 0, "q")
            evacuate(0, 0, "k")
            evacuate_v(0, 0)
            evacuate_v(0, 1)
            evacuate(0, 0, "g")
            unit(0, 0)
            unit(1, 1)
            with act.Fori(2, H1 - 2, 2) as h:
                unit(h, 0)
                unit(h + 1, 1)
            unit(H1 - 2, 0)
            square(H1 - 1, 0)
            square(H1 - 1, 1)
            act.wait_ge(wo_scaled, 1)
            act.wait_ge(head_ready, 2 * H1)
            act.activation(woh[:], wo[:], ACT.Copy).then_inc(late_high, 1)
            for i in range(2):
                act.wait_ge(fa_in[i], 16)
                act.activation(fah[:, i], fa[:, i], ACT.Copy).then_inc(late_high, 1)
            act.wait_ge(y1_ready, 1)
            act.activation(head_parts[:, :, 0:S], heads[:, :, 2 * S:3 * S], ACT.Copy).then_inc(late_high, 1)
            act.wait_ge(ex_ready, 2)
            for t in range(T):
                act.wait_ge(pair_ready, T + 2 + 2 * (t // (2 * TB)))
                act.activation(pair[:, t, :], ps[4 + t // (2 * TB)][:, (t // TB % 2) * S:(t // TB % 2 + 1) * S], ACT.Sigmoid,
                               bias=si[:, t:t + 1]).then_inc(pair_out, 1)
            act.wait_ge(fb_in, 32)
            act.activation(fbh[:], fb[:], ACT.Copy).then_inc(late_high, 1)
            act.wait_ge(y1_ready, 2)
            act.activation(head_parts[:, :, S:2 * S], heads[:, :, 3 * S:4 * S], ACT.Copy).then_inc(late_high, 1)
            act.wait_ge(facol_in, 32)

            def gelu_high(b):
                if b == 0:
                    act.wait_ge(y1_ready, B)
                wait_past(act, f_ready, 2 * b - 2)
                act.wait_ge(f0_out, b + 1)
                act.activation(fh[:, b % 2, 0], f0[:, b % 2], ACT.Copy).then_inc(fh_ready, 1)

            def relu_high(b):
                act.wait_ge(f1_out, b + 1)
                act.activation(fh[:, b % 2, 1], f1[:, b % 2], ACT.Copy).then_inc(fh_ready, 1)

            for n in range(B + 2):
                b = n - 1
                if n >= 2:
                    gelu_high(n - 2)
                if n < B:
                    high_part(3 * B + n, n)
                if n >= 2:
                    relu_high(n - 2)
                if 0 <= b < B:
                    act.wait_ge(up_ready, 2 * b + 1)
                    if b >= 2:
                        act.wait_ge(late_low, LOW_BEFORE + b - 1)
                    for m in range(FB):
                        last = act.activation(f0[:, b % 2, m, :], ps[m // 2][:, (m % 2) * S:(m % 2 + 1) * S], ACT.Gelu,
                                              bias=facol[:, m:m + 1])
                    last.then_inc(f0_out, 1)

        @block.tensor
        def _(pe):
            def product3(dst, lh, ll, rh, rl, first, last):
                pe.matmul(dst, lh, rh, start=first, stop=False)
                pe.matmul(dst, lh, rl, start=False, stop=False)
                return pe.matmul(dst, ll, rh, start=False, stop=last)

            def transpose_norm(n, b):
                pe.wait_ge(xn_ready, TB * (n + 1))
                wait_past(pe, xl_ready, n - (norm_bank(n) != norm_bank(n - 1)))
                for k in range(K):
                    for t in range(TB):
                        last = pe.transpose(ps[norm_bank(n)][:, (k * TB + t) * P:(k * TB + t + 1) * P],
                                            xn[:, TB * b + t, k * P:(k + 1) * P], ident[:])
                last.then_inc(xT_ready, 1)

            pe.wait_ge(consts, 1)
            pe.wait_ge(ctx_in, 32)
            for i in range(4):
                pe.matmul(ps[3 + i][0:C, :], xw[:, i // 2, :], ctxT[:, (i % 2) * 512:(i % 2) * 512 + 512],
                          start=True, stop=True).then_inc(ctx_qk, 1)

            def project(b):
                pe.wait_ge(xl_ready, b + 1)
                cols = slice(b * S, (b + 1) * S)
                for w, bank, s_ready_, s_free in ((0, 0, q_ready, q_out), (1, 1, k_ready, k_out)):
                    pe.wait_ge(aw_split, w + 1)
                    wait_past(pe, s_free, b)
                    for m in range(K):
                        mc = slice(m * P, (m + 1) * P)
                        for k in range(K):
                            last = product3(ps[bank][:, m * S:(m + 1) * S], awh[:, w, k, mc], awl[:, w, k, mc],
                                            xh[:, k, cols], xl[:, k, cols], k == 0, k == K - 1)
                    last.then_inc(s_ready_, 1)
                pe.wait_ge(aw_split, 3)
                wait_past(pe, v_out, b)
                for t in range(TB):
                    tc = slice(b * S + t * P, b * S + (t + 1) * P)
                    for k in range(K):
                        last = product3(ps[2][:, t * E:(t + 1) * E], xh[:, k, tc], xl[:, k, tc],
                                        awh[:, 2, k, :], awl[:, 2, k, :], k == 0, k == K - 1)
                last.then_inc(v_ready, 1)

            transpose_norm(0, 0)
            pe.wait_ge(ctx_qk_out, 4)
            for t in range(T):
                mm = pe.matmul(ps[3 + t // TB][:, (t % TB) * S:(t % TB + 1) * S], cQ[:, t * P:(t + 1) * P],
                               cK[:, (t // TB) * S:(t // TB + 1) * S], start=True, stop=True)
                if t % TB == TB - 1:
                    mm.then_inc(sim_ready, 1)
            for b in range(B):
                if b + 1 < B:
                    transpose_norm(b + 1, b + 1)
                project(b)

            def heads_transposed(b):
                pe.wait_ge(o_out, b + 1)
                pe.wait_ge(xl_ready, min(B + b, 2 * B - 2))
                for k in range(K):
                    for t in range(TB):
                        last = pe.transpose(ps[7][:, (k * TB + t) * P:(k * TB + t + 1) * P],
                                            on[:, t, k * P:(k + 1) * P], ident[:])
                last.then_inc(oT_ready, 1)

            def adjacency_transposed(b):
                pe.wait_ge(adj_ready, b + 1)
                for i in range(TB):
                    for j in range(TB):
                        last = pe.transpose(ps[4 + b % 2][:, (i * TB + j) * P:(i * TB + j + 1) * P],
                                            adj[:, j, i * P:(i + 1) * P], ident[:])
                last.then_inc(adjT_ready, 1)

            def heads_out(b):
                pe.wait_ge(ol_ready, b + 1)
                for t in range(TB):
                    for k in range(K):
                        tc = slice(t * P, (t + 1) * P)
                        last = product3(ps[7][:, t * E:(t + 1) * E], oh[:, k, tc], ol[:, k, tc],
                                        awh[:, 3, k, :], awl[:, 3, k, :], k == 0, k == K - 1)
                last.then_inc(wo_ready, 1)

            def scores(n):
                b, h = divmod(n, H0)
                pe.wait_ge(qm_ready, n + 1)
                wait_past(pe, max_ready, n - 2)
                bank = ps[SCORE_BANKS[n % 3]]
                pe.matmul(bank[:, 0:P], qm[:, n % QM, 0:P], kT[:, h // HB, ds(b * S, P)], start=True, stop=True)
                pe.matmul(bank[:, P:3 * P], qm[:, n % QM, P:2 * P], kT[:, h // HB, ds(b * S, S)],
                          start=True, stop=True).then_inc(s_ready, 1)

            def turn_probs(n):
                pe.wait_ge(p_ready, n + 1)
                wait_past(pe, pT_out, n - 1)
                for i in range(3):
                    last = pe.transpose(ps[2 + n % 2][:, i * P:(i + 1) * P], pr[:, n % PR, i * P:(i + 1) * P], ident[:])
                last.then_inc(pT_ready, 1)

            def values(n):
                b, h = divmod(n, H0)
                pe.wait_ge(pT_out, n + 1)
                if h == 0:
                    wait_past(pe, o_out, b - 1)
                c0, bank = h * D0, ps[4 + b % 2]
                pe.matmul(bank[:, c0:c0 + D0], prT[:, n % 2, 0:P], v[:, ds(b * TB, 1), c0:c0 + D0],
                          start=True, stop=True)
                pe.matmul(bank[:, E + c0:E + c0 + D0], prT[:, n % 2, P:2 * P], v[:, ds(b * TB, 1), c0:c0 + D0],
                          start=True, stop=False)
                pe.matmul(bank[:, E + c0:E + c0 + D0], prT[:, n % 2, 2 * P:3 * P], v[:, ds(b * TB + 1, 1), c0:c0 + D0],
                          start=False, stop=True).then_inc(pv_ready, 1)

            pe.wait_ge(q_out, B)
            pe.wait_ge(k_out, B)
            pe.wait_ge(v_out, B)
            pe.wait_ge(sim_out, B)

            def shared_down(half):
                pe.wait_ge(sd_in, 16)
                pe.wait_ge(sh_ready, FB * (half + 1))
                for b in range(2):
                    wait_past(pe, sdown_added, 2 * half)
                    for t in range(TB):
                        tc = slice((b * TB + t) * P, (b * TB + t + 1) * P)
                        for m in range(FB):
                            last = pe.matmul(ps[5 + b][:, t * E:(t + 1) * E], hT[:, m, tc], sd[:, m, :],
                                             start=(m == 0), stop=(m == FB - 1))
                    last.then_inc(sdown_ready, 1)

            def shared_up(i):
                half, m = divmod(i, FB)
                cols, mc = slice(half * HALF, (half + 1) * HALF), slice(m * P, (m + 1) * P)
                wait_past(pe, sh_ready, i - 1)
                for bank, hi, lo in ((shared_banks(i)[0], sgh, sgl), (shared_banks(i)[1], suh, sul)):
                    for k in range(K):
                        last = product3(ps[bank][:], hi[:, k, mc], lo[:, k, mc], xh[:, k, cols], xl[:, k, cols],
                                        k == 0, k == K - 1)
                last.then_inc(sgu_ready, 1)

            for n in range(STEPS + TAIL):
                if n < STEPS:
                    scores(n)
                if n == STEPS + 1:
                    pe.wait_ge(max_ready, STEPS - 1)
                    pe.wait_ge(shared_split, 2 * K)
                    pe.wait_ge(xl_ready, B + 2)
                    shared_up(0)
                if 3 <= n < STEPS + 3:
                    turn_probs(n - 3)
                if 5 <= n < STEPS + 5:
                    values(n - 5)
                if batch_at(n, 22) is not None:
                    pe.wait_ge(wo_ready, batch_at(n, 22) + 1)
                    transpose_norm(B + batch_at(n, 22), batch_at(n, 22))
                for offset, stage in ((8, heads_transposed), (9, adjacency_transposed), (10, heads_out)):
                    if batch_at(n, offset) is not None:
                        stage(batch_at(n, offset))
            heads_transposed(B - 1)
            adjacency_transposed(B - 1)
            pe.wait_ge(sh_ready, 1)
            transpose_norm(2 * B - 2, B - 2)
            heads_out(B - 1)
            shared_up(1)
            shared_up(2)
            shared_up(3)

            pe.wait_ge(rw_split, 1)

            def logits(half):
                cols = slice(half * HALF, (half + 1) * HALF)
                for k in range(K):
                    last = product3(ps[7 * half][0:NEXP, :], rwh[:, k, :], rwl[:, k, :], xh[:, k, cols], xl[:, k, cols],
                                    k == 0, k == K - 1)
                last.then_inc(logits_ready, 1)

            logits(0)
            pe.wait_ge(wo_ready, B)
            transpose_norm(2 * B - 1, B - 1)
            pe.wait_ge(xl_ready, 2 * B)
            logits(1)
            pe.wait_ge(lgT_out, 2)
            for t in range(T):
                last = pe.transpose(ps[0][:, t * NEXP:(t + 1) * NEXP], lgT[:, t * P:(t + 1) * P], ident[0:NEXP, 0:NEXP])
            last.then_inc(logits_ready, 1)
            pe.wait_ge(onehot_ready, 1)
            pe.matmul(ps[0][:, 64:64 + T * NEXP], before[:], flat(onehot[:]), start=True, stop=True)
            pe.matmul(ps[0][:, 128:128 + T * NEXP], ones[:], flat(onehot[:]), start=True, stop=True).then_inc(counts_ready, 1)
            shared_down(0)
            for i in range(FB, FB + BEFORE):
                shared_up(i)

            def turn_rows(j):
                pe.wait_ge(xg_in[j % 3], 16 * (j // 3 + 1))
                if j == 0:
                    pe.wait_ge(slot_ready, 1)
                wait_past(pe, xgT_out, j)
                for k in range(K):
                    last = pe.transpose(ps[0][:, k * P:(k + 1) * P], xg[:, j % 3, k * P:(k + 1) * P], ident[:])
                last.then_inc(xg_turned, 1)

            def gate_up(j):
                e = pe.value_load(tile_expert[0:1, j:j + 1], min_val=0, max_val=NEXP - 1)
                pe.wait_ge(xgT_out, j + 1)
                wait_past(pe, rh_ready, j - 1)
                if j == 1:
                    pe.wait_ge(sdown_added, 2)
                for bank in range(2):
                    for k in range(K):
                        last = pe.matmul(ps[1 + 4 * (j % 2) + bank][:], xgT[:, j % 2, k, :], gu[:, ds(e, 1), k, bank * FI:(bank + 1) * FI],
                                         start=(k == 0), stop=(k == K - 1))
                last.then_inc(gu_done, 1)
                return e

            def turn_hidden(j):
                pe.wait_ge(rh_ready, j + 1)
                wait_past(pe, rhT_out, j - 1)
                for m in range(FB):
                    last = pe.transpose(ps[3 + 4 * (j % 2)][:, m * P:(m + 1) * P], rh[:, j % 2, m * P:(m + 1) * P], ident[:])
                last.then_inc(rh_turned, 1)

            def down(j, e):
                pe.wait_ge(rhT_out, j + 1)
                wait_past(pe, y_out, j)
                for m in range(FB):
                    last = pe.matmul(ps[4][:, 0:E], rhT[:, j % 2, m, :], dn[:, ds(e, 1), m, :], start=(m == 0), stop=(m == FB - 1))
                last.then_inc(y_ready, 1)

            pe.wait_ge(sh_ready, FB + BEFORE)
            pe.wait_ge(tile_ready, 1)
            pe.wait_ge(gu_in, 16 * NEXP)
            pe.wait_ge(dn_in, 16 * NEXP)
            turn_rows(0)
            experts = {}
            for j in range(NSLOT + 2):
                if j < NSLOT:
                    experts[j] = gate_up(j)
                if j + 1 < NSLOT:
                    turn_rows(j + 1)
                if 1 <= j <= NSLOT:
                    turn_hidden(j - 1)
                if j >= 2:
                    down(j - 2, experts.pop(j - 2))
            for i in range(FB + BEFORE, 2 * FB):
                if i % 2:
                    pe.wait_ge(y_out, NSLOT)
                shared_up(i)
            shared_down(1)
            pe.wait_ge(y_out, NSLOT)
            for b in range(B - 1):
                transpose_norm(2 * B + b, b)

            def project_half(dst, i, c, half):
                hc = slice(half * HALF, (half + 1) * HALF)
                for k in range(K):
                    last = product3(ps[dst + half][:], wh[:, i, k, c:c + D1], wl[:, i, k, c:c + D1],
                                    xh[:, k, hc], xl[:, k, hc], k == 0, k == K - 1)
                return last

            def project_head(h, i, what):
                c = "qkg".index(what) * D1
                if what == "q":
                    pe.wait_ge(w_split, h + 1)
                    if i == 1:
                        pe.wait_ge(vd_out, h + 1)
                    else:
                        wait_past(pe, qd_out, h)
                    dst, s_ = 0, qd_ready
                elif what == "k":
                    wait_past(pe, gd_out, h)
                    dst, s_ = 2, kd_ready
                else:
                    pe.wait_ge(kd_out, h + 1)
                    dst, s_ = 2, gd_ready
                for half in range(2):
                    last = project_half(dst, i, c, half)
                last.then_inc(s_, 1)

            def project_v(h, u):
                if u == 0:
                    pe.wait_ge(v_split, h + 2)
                    pe.wait_ge(qd_out, h + 1)
                else:
                    pe.wait_ge(vd_out, h + 1)
                for t in range(4):
                    tc = slice((4 * u + t) * P, (4 * u + t + 1) * P)
                    for k in range(K):
                        last = product3(ps[t // 2][:, (t % 2) * 2 * D1:(t % 2 + 1) * 2 * D1], xh[:, k, tc], xl[:, k, tc],
                                        vh[:, k, :], vl[:, k, :], k == 0, k == K - 1)
                last.then_inc(vd_ready, 1)

            def score_pair(h, i, p):
                if p == 0:
                    pe.wait_ge(kd_out, h + 1)
                wait_past(pe, masked_ready, 2 * h + p)
                for j in range(2):
                    c0 = (2 * p + j) * S
                    pe.matmul(ps[4 + j][:, 0:S], kd[:, i, c0:c0 + P], qd[:, i, c0:c0 + S], start=True, stop=True)
                    last = pe.matmul(ps[4 + j][:, S:S + P], kd[:, i, c0 + P:c0 + S], qd[:, i, c0 + P:c0 + S],
                                     start=True, stop=True)
                last.then_inc(scores_ready, 1)

            def head_pair(h, i, p):
                pe.wait_ge(masked_ready, 2 * h + p + 1)
                pe.wait_ge(vd_out, h - i + p + 1)
                wait_past(pe, squared, 2 * h + p - 1)
                for j in range(2):
                    t = (2 * p + j) * TB
                    pe.matmul(ps[6 + p][:, j * S:(j + 1) * S], vd[:, t, i * D1:(i + 1) * D1], masked[:, p, j, 0:S], start=True, stop=False)
                    last = pe.matmul(ps[6 + p][:, j * S + P:(j + 1) * S], vd[:, t + 1, i * D1:(i + 1) * D1], masked[:, p, j, S:S + P],
                                     start=False, stop=True)
                last.then_inc(head_ready, 1)

            def unit(h, i):
                project_head(h + 1, 1 - i, "q")
                score_pair(h, i, 0)
                project_head(h + 1, 1 - i, "k")
                score_pair(h, i, 1)
                head_pair(h, i, 0)
                if i == 0:
                    project_head(h + 1, 1 - i, "g")
                    head_pair(h, i, 1)
                else:
                    project_v(h + 1, 0)
                    head_pair(h, i, 1)
                    project_v(h + 1, 1)
                    project_head(h + 1, 1 - i, "g")

            pe.wait_ge(w_split, 1)
            pe.wait_ge(xl_ready, 2 * B + 2)
            project_half(0, 0, 0, 0)
            project_half(2, 0, D1, 0)
            transpose_norm(3 * B - 1, B - 1)
            pe.wait_ge(xl_ready, 3 * B)
            project_half(0, 0, 0, 1).then_inc(qd_ready, 1)
            project_half(2, 0, D1, 1).then_inc(kd_ready, 1)
            project_v(0, 0)
            project_v(0, 1)
            project_head(0, 0, "g")
            unit(0, 0)
            unit(1, 1)
            with pe.Fori(2, H1 - 2, 2) as h:
                unit(h, 0)
                unit(h + 1, 1)
            unit(H1 - 2, 0)

            def project_heads(b, t, first, last_h, between=None):
                tc = slice((TB * b + t) * P, (TB * b + t + 1) * P)
                if b == 3:
                    pe.wait_ge(late_low, 8)
                for h in range(first, last_h):
                    if b == 2 and t == 0 and h % 4 == 0:
                        pe.wait_ge(late_low, 3 + h // 4)
                    if b >= 2:
                        high = slice((TB * (b - 2) + t) * P, (TB * (b - 2) + t + 1) * P)
                        last = product3(ps[out_bank(b, t)][:, t * E:(t + 1) * E], head_parts[:, h, high],
                                        head_parts[:, h, tc], woh[:, h, :], wol[:, h, :], h == 0, h == H1 - 1)
                        continue
                    if between is not None and h >= last_h - T:
                        between(h - last_h + T)
                    last = pe.matmul(ps[out_bank(b, t)][:, t * E:(t + 1) * E], heads[:, h, tc], wo[:, h, :],
                                     start=(h == 0), stop=(h == H1 - 1))
                    if b == 1 and t == 1 and h in (3, 7, 11):
                        last.then_inc(wo_used, 1)
                return last

            score_pair(H1 - 1, 1, 0)
            pe.wait_ge(wo_scaled, 1)
            pe.wait_ge(qd_out, H1)
            pe.wait_ge(head_out, 2 * (H1 // 4))
            project_heads(0, 0, 0, H1 // 4)
            score_pair(H1 - 1, 1, 1)
            pe.wait_ge(head_out, 2 * (H1 - 1))
            project_heads(0, 0, H1 // 4, H1 - 1)
            head_pair(H1 - 1, 1, 0)
            head_pair(H1 - 1, 1, 1)

            def row_weights(t):
                if t == 0:
                    pe.wait_ge(ex_ready, 1)
                pe.matmul(ps[3][:, t:t + 1], ctx2[:, t * P:(t + 1) * P], ex[:, 0:1], start=True, stop=True).then_inc(pair_ready, 1)

            def square_sums(t):
                if t == 0:
                    pe.wait_ge(square_added, 2 * H1)
                pe.matmul(ps[2][:, t:t + 1], flat(square_sum[:])[:, t * P:(t + 1) * P], ones[:, 0:1],
                          start=True, stop=True).then_inc(ms_ready, 1)

            project_heads(0, 1, 0, H1 - 1, row_weights)
            for b in range(B):
                pe.matmul(ps[4 + b // 2][:, (b % 2) * S:(b % 2 + 1) * S], wj[:], ctx2[:, b * S:(b + 1) * S],
                          start=True, stop=True).then_inc(pair_ready, 1)
            pe.wait_ge(head_out, 2 * H1)
            project_heads(0, 0, H1 - 1, H1)
            project_heads(0, 1, H1 - 1, H1).then_inc(y1_ready, 1)
            pe.wait_ge(squared, 2 * H1)
            project_heads(1, 0, 0, H1 // 2, square_sums)
            project_heads(1, 0, H1 // 2, H1)
            project_heads(1, 1, 0, H1).then_inc(y1_ready, 1)

            def up(b):
                cols = slice(b * S, (b + 1) * S)
                for i, s_free in enumerate((f0_out, f1_out)):
                    wait_past(pe, s_free, b)
                    for m in range(FB):
                        mc = slice(m * P, (m + 1) * P)
                        for k in range(K):
                            last = product3(ps[4 * i + m // 2][:, (m % 2) * S:(m % 2 + 1) * S], fah[:, i, k, mc],
                                            fal[:, i, k, mc], xh[:, k, cols], xl[:, k, cols], k == 0, k == K - 1)
                    last.then_inc(up_ready, 1)

            def down_experts(b):
                if b == 0:
                    pe.wait_ge(y1_added, B - 1)
                if b == 1:
                    pe.wait_ge(y1_added, B)
                    pe.wait_ge(xl_ready, 4 * B)
                wait_past(pe, x_final, TB * (b - 1))
                pe.wait_ge(fa_split, 4)
                pe.wait_ge(late_low, LOW_BEFORE + b + 1)
                for i in range(2):
                    if i == 1:
                        pe.wait_ge(fl1_ready, b + 1)
                    for t in range(TB):
                        tc = slice(t * P, (t + 1) * P)
                        for m in range(FB):
                            last = product3(ps[2 + 4 * (b % 2) + t][:, i * E:(i + 1) * E], fh[:, b % 2, i, m, tc],
                                            fl[:, b % 2, i, m, tc], fbh[:, i, m, :], fbl[i][:, m, :], m == 0, m == FB - 1)
                        if i == 1:
                            last.then_inc(f_ready, 1)

            def ready_for_up(b):
                pe.wait_ge(xl_ready, 3 * B + b + 1)
                if b == 0:
                    pe.wait_ge(pair_out, T)
                    pe.wait_ge(fa_split, 2)

            def project_batch(b):
                if b == 2:
                    pe.wait_ge(rms_step, 1)
                else:
                    pe.wait_ge(y1_added, b - 1)
                project_heads(b, 0, 0, H1)
                transpose_norm(3 * B + b - 2, b - 2)
                project_heads(b, 1, 0, H1).then_inc(y1_ready, 1)

            project_batch(2)
            ready_for_up(0)
            up(0)
            project_batch(3)
            for b in range(1, B):
                if b + 1 < B:
                    transpose_norm(3 * B + b + 1, b + 1)
                ready_for_up(b)
                up(b)
                down_experts(b - 1)
            down_experts(B - 1)


def kernel(**inputs):
    import numpy as np
    import concourse.bacc as bacc
    from concourse.bass_utils import run_bass_kernel_spmd

    g = {k: np.asarray(v) for k, v in inputs.items()}
    ca = np.ascontiguousarray

    def cols(v):
        return v.reshape(-1, P).T

    w = g["L1_attn_w_qkv"].reshape(H1, 3, D1, E)
    wg = g["L1_attn_w_gate"].reshape(H1, 1, D1, E)
    heads = np.concatenate([w[:, :2], wg], axis=1)
    arrays = {
        "x": g["x"],
        "ctxT": g["ctx_512"].reshape(B * S, C).T,
        "aw": np.stack([g[f"L0_attn_W{n}"].T for n in "qkvo"]),
        "abcol": np.concatenate([cols(g["L0_attn_bq"]), cols(g["L0_attn_bk"])], axis=1),
        "abrow": np.stack([g["L0_attn_bv"], g["L0_attn_bo"]]),
        "xw": np.stack([g["L0_xattn_Wq"].T, g["L0_xattn_Wk"].T], axis=1),
        "gamma": g["L0_xattn_gamma_raw"].reshape(1, 1),
        "rw": g["L0_ffn_router_w"].T.reshape(K, P, NEXP).transpose(1, 0, 2),
        "gu": g["L0_ffn_gate_up_proj"],
        "dn": g["L0_ffn_down_proj"],
        "sg": g["L0_ffn_shared_gate_w"],
        "su": g["L0_ffn_shared_up_w"],
        "sd": g["L0_ffn_shared_down_w"],
        "slopes": g["L1_attn_slope_rate"].reshape(1, H1),
        "heads": heads.reshape(H1, 3 * D1, K, P).transpose(0, 3, 2, 1),
        "vpairs": w[:, 2].reshape(H1 // 2, 2 * D1, K, P).transpose(0, 3, 2, 1),
        "nw": cols(g["L1_attn_norm_w"]),
        "wo": g["L1_attn_w_out"].T.reshape(H1, D1, E).transpose(1, 0, 2),
        "ex": g["L1_xattn_W"].reshape(2, C).T,
        "eb": g["L1_xattn_b"].reshape(1, 1),
        "fg": g["L1_ffn_Wg"],
        "fa": np.stack([g["L1_ffn_W0a"].T, g["L1_ffn_W1a"].T]),
        "fb": np.stack([g["L1_ffn_W0b"].T, g["L1_ffn_W1b"].T]),
        "facol": np.concatenate([cols(g["L1_ffn_b0a"]), cols(g["L1_ffn_b1a"])], axis=1),
        "fbrow": np.stack([g["L1_ffn_b0b"], g["L1_ffn_b1b"]]),
    }
    nc = bacc.Bacc("TRN2", target_bir_lowering=False, num_devices=1)
    arrays = {f"in_{k}": ca(v) for k, v in arrays.items()}
    aps = {k[3:]: nc.dram_tensor(k, v.shape, mybir.dt.from_np(v.dtype), kind="ExternalInput").ap()
           for k, v in arrays.items()}
    out = nc.dram_tensor("out", (B, S, E), F32, kind="ExternalOutput").ap()
    sorted_in = nc.dram_tensor("sorted_in", (NSLOT * P, E), F32).ap()
    sorted_out = nc.dram_tensor("sorted_out", (NSLOT * P, E), F32).ap()
    decoder(nc, aps, sorted_in, sorted_out, out)
    return run_bass_kernel_spmd(nc, [arrays], core_ids=[0]).results[0]["out"]
```
